# Optimizing a Trainium2 kernel written in Bass

```python
import numpy as np
import jax
import jax.numpy as jnp

def _softmax(x, axis=-1):
    return jax.nn.softmax(x, axis=axis)
def _gelu(x):
    return jax.nn.gelu(x, approximate=True)
def _silu(x):
    return jax.nn.silu(x)
def _sigmoid(x):
    return jax.nn.sigmoid(x)
def _layernorm(x, axis=-1, eps=1e-5):
    m = jnp.mean(x, axis=axis, keepdims=True)
    v = jnp.var(x, axis=axis, keepdims=True)
    return (x - m) / jnp.sqrt(v + eps)
def _scatter_add(tgt, idx, src, axis=0):
    return tgt.at[idx].add(src)
def _segment_sum(src, seg, n):
    return jax.ops.segment_sum(src, seg, n)

kernel_name = 'mk_adj_ffn_d1_adj_256_5d840a'

def setup_inputs(seed: int = 0):
    np.random.seed(seed)
    _w = jnp.asarray
    def _rec_inputs():
        import jax
        import jax.numpy as jnp
        _gk = jax.random.key(seed)
        x = -0.000929 + 1 * jax.random.normal(jax.random.fold_in(_gk, 1), (4096, 256), jnp.float32)
        _w = (1.0 + jnp.arange(4096, dtype=jnp.float32)) ** -0.5
        _w = _w / _w.mean()
        _pij = jnp.clip(0.00390625 * _w[:, None] * _w[None, :], 0.0, 1.0)
        _a = jax.random.uniform(jax.random.fold_in(_gk, 2), (4096, 4096)) < _pij
        adj = _a.astype(jnp.int32)
        return x, adj
    x, adj = _rec_inputs()
    def _L0_gnn_setup():
        import jax, jax.numpy as jnp
        import numpy as np
        N = 4096
        F_IN = 256
        F_OUT = 64
        H = 4
        ALPHA = 0.2
        NEG_BIG = -9000000000000000.0
        key = jax.random.key(seed)
        k1, k2, k3, k4 = jax.random.split(key, 4)
        x = jax.random.normal(k1, (N, F_IN), dtype=jnp.float32)
        adj = jax.random.randint(k2, (N, N), 0, 2, dtype=jnp.int32)
        limW = float(np.sqrt(6.0 / (F_IN + F_OUT)))
        W = jax.random.uniform(k3, (H, F_IN, F_OUT), jnp.float32, -limW, limW)
        lima = float(np.sqrt(6.0 / (2 * F_OUT + 1)))
        a = jax.random.uniform(k4, (H, 2 * F_OUT, 1), jnp.float32, -lima, lima)
        return {'x': x, 'adj': adj, 'W': W, 'a': a}
    _L0_gnn_all = _L0_gnn_setup()
    _L0_gnn_in = {k: v for k, v in _L0_gnn_all.items() if k in ('W', 'a', )}
    del _L0_gnn_all

    def _L0_ffn_setup():
        import jax, jax.numpy as jnp
        import numpy as np
        B, T, C = (64, 384, 256)
        NH, NKV = (4, 2)
        HD = C // NH
        NREP = NH // NKV
        NE, TOPK = (8, 2)
        HID = int(8 / 3 * C)
        EPS_RMS = 1e-06

        def _rope_tables(t_len):
            inv_freq = 1.0 / 10000.0 ** (np.arange(0, HD, 2, dtype=np.float32) / HD)
            t = np.arange(t_len, dtype=np.float32)
            freqs = np.outer(t, inv_freq)
            emb = np.concatenate([freqs, freqs], axis=-1)
            return (jnp.asarray(np.cos(emb)), jnp.asarray(np.sin(emb)))

        def _rotate_half(x):
            h = x.shape[-1] // 2
            return jnp.concatenate([-x[..., h:], x[..., :h]], axis=-1)

        def _rmsnorm(v, w):
            return v * jax.lax.rsqrt(jnp.mean(v * v, axis=-1, keepdims=True) + EPS_RMS) * w
        key = jax.random.key(seed)
        ks = jax.random.split(key, 10)
        s = lambda k, shape: jax.random.normal(k, shape, jnp.float32) * 0.02
        return {'x': jax.random.normal(ks[0], (B, T, C), jnp.float32), 'ln1_w': jnp.ones((C,), jnp.float32), 'ln2_w': jnp.ones((C,), jnp.float32), 'wq': s(ks[1], (NH * HD, C)), 'wk': s(ks[2], (NKV * HD, C)), 'wv': s(ks[3], (NKV * HD, C)), 'wo': s(ks[4], (C, C)), 'router_w': s(ks[5], (NE, C)), 'w1': s(ks[6], (NE, HID, C)), 'w2': s(ks[7], (NE, C, HID)), 'w3': s(ks[8], (NE, HID, C))}
    _L0_ffn_all = _L0_ffn_setup()
    _L0_ffn_in = {k: v for k, v in _L0_ffn_all.items() if k in ('ln1_w', 'ln2_w', 'wq', 'wk', 'wv', 'wo', 'router_w', 'w1', 'w2', 'w3', )}
    del _L0_ffn_all

    return {
        "x": x,
        "adj": adj,
        "L0_gnn_W": _L0_gnn_in["W"],
        "L0_gnn_a": _L0_gnn_in["a"],
        "L0_ffn_ln1_w": _L0_ffn_in["ln1_w"],
        "L0_ffn_ln2_w": _L0_ffn_in["ln2_w"],
        "L0_ffn_wq": _L0_ffn_in["wq"],
        "L0_ffn_wk": _L0_ffn_in["wk"],
        "L0_ffn_wv": _L0_ffn_in["wv"],
        "L0_ffn_wo": _L0_ffn_in["wo"],
        "L0_ffn_router_w": _L0_ffn_in["router_w"],
        "L0_ffn_w1": _L0_ffn_in["w1"],
        "L0_ffn_w2": _L0_ffn_in["w2"],
        "L0_ffn_w3": _L0_ffn_in["w3"],
    }

def reference(x, adj, L0_gnn_W, L0_gnn_a, L0_ffn_ln1_w, L0_ffn_ln2_w, L0_ffn_wq, L0_ffn_wk, L0_ffn_wv, L0_ffn_wo, L0_ffn_router_w, L0_ffn_w1, L0_ffn_w2, L0_ffn_w3):
    import jax
    import jax.numpy as jnp
    def _L0_gnn_ref(x, adj, W, a):
        import jax, jax.numpy as jnp
        import numpy as np
        N = 4096
        F_IN = 256
        F_OUT = 64
        H = 4
        ALPHA = 0.2
        NEG_BIG = -9000000000000000.0
        Wh = jnp.einsum('nf,hfo->hno', x, W)
        a1 = a[:, :F_OUT, 0]
        a2 = a[:, F_OUT:, 0]
        s1 = jnp.einsum('hno,ho->hn', Wh, a1)
        s2 = jnp.einsum('hno,ho->hn', Wh, a2)
        e = jax.nn.leaky_relu(s1[:, :, None] + s2[:, None, :], ALPHA)
        e = jnp.where(adj[None, :, :] > 0, e, NEG_BIG)
        att = jax.nn.softmax(e, axis=-1)
        h_prime = jnp.einsum('hij,hjo->hio', att, Wh)
        return jnp.transpose(h_prime, (1, 0, 2)).reshape(N, H * F_OUT)

    def _L0_ffn_ref(x, ln1_w, ln2_w, wq, wk, wv, wo, router_w, w1, w2, w3):
        import jax, jax.numpy as jnp
        import numpy as np
        B, T, C = (64, 384, 256)
        NH, NKV = (4, 2)
        HD = C // NH
        NREP = NH // NKV
        NE, TOPK = (8, 2)
        HID = int(8 / 3 * C)
        EPS_RMS = 1e-06

        def _rope_tables(t_len):
            inv_freq = 1.0 / 10000.0 ** (np.arange(0, HD, 2, dtype=np.float32) / HD)
            t = np.arange(t_len, dtype=np.float32)
            freqs = np.outer(t, inv_freq)
            emb = np.concatenate([freqs, freqs], axis=-1)
            return (jnp.asarray(np.cos(emb)), jnp.asarray(np.sin(emb)))

        def _rotate_half(x):
            h = x.shape[-1] // 2
            return jnp.concatenate([-x[..., h:], x[..., :h]], axis=-1)

        def _rmsnorm(v, w):
            return v * jax.lax.rsqrt(jnp.mean(v * v, axis=-1, keepdims=True) + EPS_RMS) * w
        Bx, Tx, Cx = x.shape
        h = _rmsnorm(x, ln1_w)
        q = (h @ wq.T).reshape(Bx, Tx, NH, HD).transpose(0, 2, 1, 3)
        k = (h @ wk.T).reshape(Bx, Tx, NKV, HD).transpose(0, 2, 1, 3)
        v = (h @ wv.T).reshape(Bx, Tx, NKV, HD).transpose(0, 2, 1, 3)
        cos, sin = _rope_tables(Tx)
        cos, sin = (cos[None, None], sin[None, None])
        q = q * cos + _rotate_half(q) * sin
        k = k * cos + _rotate_half(k) * sin
        k = jnp.repeat(k, NREP, axis=1)
        v = jnp.repeat(v, NREP, axis=1)
        scores = jnp.einsum('bhtd,bhsd->bhts', q, k) / jnp.sqrt(jnp.float32(HD))
        causal = jnp.tril(jnp.ones((Tx, Tx), dtype=bool))
        scores = jnp.where(causal[None, None], scores, jnp.float32(-1e+30))
        att = jax.nn.softmax(scores, axis=-1)
        y = jnp.einsum('bhts,bhsd->bhtd', att, v).transpose(0, 2, 1, 3).reshape(Bx, Tx, Cx)
        x = x + y @ wo.T
        flat = _rmsnorm(x, ln2_w).reshape(-1, Cx)
        probs = jax.nn.softmax(flat @ router_w.T, axis=-1)
        tp, ti = jax.lax.top_k(probs, TOPK)
        tp = tp / (jnp.sum(tp, axis=-1, keepdims=True) + 1e-09)
        weights = jnp.sum(tp[..., None] * jax.nn.one_hot(ti, NE, dtype=flat.dtype), axis=1)
        out = jnp.zeros_like(flat)
        for e in range(NE):
            hh = jax.nn.silu(flat @ w1[e].T) * (flat @ w3[e].T)
            out = out + weights[:, e:e + 1] * (hh @ w2[e].T)
        return x + out.reshape(Bx, Tx, Cx)

    x = x + _L0_gnn_ref(_layernorm(x, axis=-1), adj, L0_gnn_W, L0_gnn_a)
    x = x + _L0_ffn_ref((_layernorm(x, axis=-1))[None], L0_ffn_ln1_w, L0_ffn_ln2_w, L0_ffn_wq, L0_ffn_wk, L0_ffn_wv, L0_ffn_wo, L0_ffn_router_w, L0_ffn_w1, L0_ffn_w2, L0_ffn_w3)[0]
    return x


_drawn_inputs = setup_inputs


def setup_inputs(seed=0):
    import zlib

    import numpy as np

    out = dict(_drawn_inputs(seed))
    spreads = {'L0_ffn_ln1_w': (1.0, 0.6), 'L0_ffn_ln2_w': (1.0, 0.6)}
    factors = {'L0_ffn_wq': 8.0,
     'L0_ffn_wk': 8.0,
     'L0_ffn_wv': 8.0,
     'L0_ffn_wo': 7.408,
     'L0_ffn_router_w': 6.143,
     'L0_ffn_w1': 5.516,
     'L0_ffn_w2': 5.44,
     'L0_ffn_w3': 5.446}
    for name, (base, spread) in spreads.items():
        noise = np.random.default_rng([zlib.crc32(name.encode()), seed]).standard_normal(out[name].shape)
        drawn = base * np.exp(spread * noise) if base else spread * noise
        out[name] = jnp.asarray(drawn.astype(out[name].dtype))
    for name, factor in factors.items():
        out[name] = (out[name] * factor).astype(out[name].dtype)
    return out
```

```python
from contextlib import ExitStack

import numpy as np

import concourse.bass as bass
from concourse import mybir

P = 128
N = 4096
C = 256
KC = C // P
NT = N // P
CH = 512
NC = N // CH
TPC = CH // P
H = 4
D = C // H
DA = D + 1
PARTS = 3
GW = PARTS * DA
GREST = GW - P
KV = 2
VW = 2 * (D + 1)
QKW = 6 * P
E = 8
HID = 682
MF = HID // P
MR = HID - MF * P
UPW = MF * 2 * P + 64 + MR
MT = MF + 1
EW = (KC * UPW + MT * C + NC - 1) // NC * NC
SLOPE = 0.2

ALU = mybir.AluOpType
ACT = mybir.ActivationFunctionType
AX = mybir.AxisListType
F32 = mybir.dt.float32
BF16 = mybir.dt.bfloat16
F32R = mybir.dt.float32r


class Pool:

    def __init__(self, nc, ctx):
        self.nc, self.ctx = nc, ctx

    def sb(self, name, shape, dt=F32):
        return self.ctx.enter_context(self.nc.sbuf_tensor(name, shape, dt))

    def bank(self, name, dt=F32, banks=1):
        cols = banks * (512 if dt == F32 else 1024)
        return self.ctx.enter_context(self.nc.psum_tensor(name, [P, cols], dt))

    def sem(self, name):
        return self.ctx.enter_context(self.nc.semaphore(name))


class Chain:

    def __init__(self, eng, sem):
        self.eng, self.sem, self.base, self.n = eng, sem, 0, 0

    def at(self, base):
        self.base, self.n = base, 0

    def step(self, ins):
        self.n += 1
        ins.then_inc(self.sem, 1)
        self.eng.wait_ge(self.sem, self.base + self.n)


def spread(ap, axis, count):
    ap = ap.unsqueeze(axis)
    shape = list(ap.shape)
    shape[axis] = count
    return ap.to_broadcast(shape)


def inverse_root(chain, v, root, y, t, roots_out, n):
    chain.eng.wait_ge(roots_out, n)
    chain.step(chain.eng.reciprocal(y, root))
    chain.step(chain.eng.tensor_tensor(t, y, y, ALU.mult))
    chain.step(chain.eng.tensor_tensor(t, t, v, ALU.mult))
    chain.step(chain.eng.tensor_scalar(t, t, -0.5, 1.5, ALU.mult, ALU.add))
    chain.step(chain.eng.tensor_tensor(y, y, t, ALU.mult))


def graph_prepare(nc, io, keep):
    with ExitStack() as ctx:
        m = Pool(nc, ctx)
        x = m.sb("gp_x", [P, NT, C])
        w = m.sb("gp_w", [P, KC, C + 2 * H])
        w_t = m.sb("gp_wt", [D, H, C])
        a_t = m.sb("gp_a", [D, 2 * H])
        ident = m.sb("gp_ident", [P, P])
        mean_of = m.sb("gp_ones", [P, P])
        st = m.sb("gp_stats", [P, NT, 6])
        mu = m.sb("gp_mu", [P, NT])
        var = m.sb("gp_var", [P, NT])
        tmp = m.sb("gp_tmp", [P, NT])
        root = m.sb("gp_root", [P, NT])
        rstd = m.sb("gp_rstd", [P, NT])
        xn = m.sb("gp_xn", [P, 2, C])
        xt = m.sb("gp_xt", [P, 2, KC, P])
        wh = m.sb("gp_wh", [P, NT, H, DA])
        rows = m.sb("gp_rows", [H, N])
        cm = m.sb("gp_cmax", [P, H])
        ca = m.sb("gp_call", [P, H])
        s2, s1 = keep.s2, keep.s1
        e2 = m.sb("gp_e2", [P, NT, H])
        f2 = m.sb("gp_f2", [P, NT, H])
        d2 = m.sb("gp_d2", [P, NT, H])
        u = m.sb("gp_u", [P, NT, H])
        u2 = m.sb("gp_u2", [P, NT, H])
        um = m.sb("gp_um", [P, NT, H])
        val = m.sb("gp_val", [P, 2, TPC * H, DA])
        ps_t = [m.bank(f"gp_ps_t{b}") for b in range(2)]
        ps_w = [m.bank(f"gp_ps_w{b}") for b in range(2)]
        ps_r = [m.bank(f"gp_ps_r{b}") for b in range(2)]
        ps_m = m.bank("gp_ps_m")

        loaded = m.sem("gp_loaded")
        wa_done = m.sem("gp_wa_done")
        wa_kept = m.sem("gp_wa_kept")
        dve_steps = m.sem("gp_dve_steps")
        set_up = m.sem("gp_set_up")
        stats_done = m.sem("gp_stats_done")
        var_done = m.sem("gp_var_done")
        root_done = m.sem("gp_root_done")
        xn_done = m.sem("gp_xn_done")
        xn_turned = m.sem("gp_xn_turned")
        xt_kept = m.sem("gp_xt_kept")
        wh_done = m.sem("gp_wh_done")
        rows_done = m.sem("gp_rows_done")
        wh_kept = m.sem("gp_wh_kept")
        rows_kept = m.sem("gp_rows_kept")
        scores_kept = m.sem("gp_scores_kept")
        summed = m.sem("gp_summed")
        mean_kept = m.sem("gp_mean_kept")
        max_done = m.sem("gp_max_done")
        all_max = m.sem("gp_all_max")
        exps_in = m.sem("gp_exps_in")
        exps_done = m.sem("gp_exps_done")
        val_done = m.sem("gp_val_done")
        hi_done = m.sem("gp_hi_done")
        rest_done = m.sem("gp_rest_done")
        mid_done = m.sem("gp_mid_done")
        lo_done = m.sem("gp_lo_done")
        stored = m.sem("gp_stored")
        block = ctx.enter_context(nc.Block())
        LOADS = 9

        @block.sync
        def _(sp):
            for q in range(4):
                sp.dma_start(x[:, 8 * q:8 * q + 8, :], io["x"].rearrange("(t p) f -> p t f", p=P)[:, 8 * q:8 * q + 8, :]).then_inc(loaded, 16)
            sp.dma_start(w[:, :, 0:C], io["w_cat"].rearrange("(k p) o -> p k o", p=P)).then_inc(loaded, 16)
            sp.dma_start(w_t[:], io["w_t"].rearrange("h o f -> o h f")).then_inc(loaded, 16)
            sp.dma_start(a_t[:], io["a_t"]).then_inc(loaded, 16)
            sp.dma_start(ident[:], io["ident"]).then_inc(loaded, 16)
            sp.dma_start(mean_of[:], io["mean_of"]).then_inc(loaded, 16)
            sp.wait_ge(rows_kept, NT)
            sp.dma_start(io["s1_rows"], rows[:]).then_inc(stored, 16)
            sp.wait_ge(stored, 16)

        @block.tensor
        def _(pe):
            pe.wait_ge(loaded, 16 * LOADS)
            for k in range(KC):
                for h in range(H):
                    for s in range(2):
                        col = k * 2 * H + (1 - s) * H + h
                        last = pe.matmul(ps_m[:, col:col + 1], w_t[:, h, k * P:(k + 1) * P],
                                         a_t[:, 2 * h + s:2 * h + s + 1], start=True, stop=True)
            last.then_inc(wa_done, 1)
            pe.wait_ge(wa_kept, 1)
            with pe.Fori(0, NT // 2) as i:
                for b in range(2):
                    pe.wait_ge(xn_done, i * 2 + (b + 1))
                    pe.wait_ge(xt_kept, i * 2 + b)
                    for k in range(KC):
                        last = pe.transpose(ps_t[b][:, k * P:(k + 1) * P], xn[:, b, k * P:(k + 1) * P], ident[:])
                    last.then_inc(xn_turned, 1)
                for b in range(2):
                    pe.wait_ge(xt_kept, i * 2 + (b + 1))
                    pe.wait_ge(wh_kept, i * 2 + b)
                    pe.wait_ge(scores_kept, i * 2 + b)
                    for k in range(KC):
                        last = pe.matmul(ps_w[b][:, 0:C + H * 2], xt[:, b, k, :], w[:, k, :], start=k == 0, stop=k == KC - 1)
                    last.then_inc(wh_done, 1)
                    pe.wait_ge(rows_kept, i * 2 + b)
                    for k in range(KC):
                        last = pe.matmul(ps_r[b][0:H, 0:P], w[:, k, C + H:C + 2 * H], xt[:, b, k, :], start=k == 0, stop=k == KC - 1)
                    last.then_inc(rows_done, 1)
            pe.wait_ge(wh_kept, NT)
            for t in range(NT):
                last = pe.matmul(ps_m[:, 0:C], mean_of[:], wh[:, t, :, 0:D], start=t == 0, stop=t == NT - 1)
            last.then_inc(summed, 1)

        @block.scalar
        def _(act):
            act.wait_ge(var_done, 1)
            act.activation(root[:], var[:], ACT.Sqrt).then_inc(root_done, 1)
            with act.Fori(0, NT // 2) as i:
                for b in range(2):
                    act.wait_ge(xn_turned, i * 2 + (b + 1))
                    act.wait_ge(rows_done, i * 2 + b)
                    act.activation(xt[:, b, :, :], ps_t[b][:, 0:C].rearrange("p (k n) -> p k n", k=KC), ACT.Copy).then_inc(xt_kept, 1)
                for b in range(2):
                    act.wait_ge(wh_done, i * 2 + (b + 1))
                    act.wait_ge(wh_kept, i * 2 + (b + 1))
                    act.activation(s2[:, bass.ds(i * 2 + b, 1), :], ps_w[b][:, C:C + H].unsqueeze(1), ACT.Copy)
                    act.activation(s1[:, bass.ds(i * 2 + b, 1), :], ps_w[b][:, C + H:C + 2 * H].unsqueeze(1), ACT.Copy).then_inc(scores_kept, 1)
                    act.wait_ge(rows_done, i * 2 + (b + 1))
                    act.activation(rows[:, bass.ds((i * 2 + b) * P, P)], ps_r[b][0:H, 0:P], ACT.Copy).then_inc(rows_kept, 1)
            act.wait_ge(exps_in, 1)
            act.activation(e2[:], d2[:], ACT.Exp).then_inc(exps_done, 1)
            act.activation(f2[:], d2[:], ACT.Exp, scale=SLOPE).then_inc(exps_done, 1)
            act.wait_ge(exps_in, 3)
            act.activation(keep.e1[:], u[:], ACT.Exp).then_inc(exps_done, 1)
            act.activation(keep.f1[:], u2[:], ACT.Exp).then_inc(exps_done, 1)
            with act.Fori(0, NC) as i:
                for b, g in enumerate((keep.ge, keep.gf)):
                    gv = g[:, bass.ds(i * TPC * H, TPC * H), :]
                    act.wait_ge(val_done, i * 2 + (b + 1))
                    act.activation(gv[:, :, 0:DA], val[:, b], ACT.Copy).then_inc(hi_done, 1)
                    act.wait_ge(rest_done, i * 2 + (b + 1))
                    act.activation(gv[:, :, DA:2 * DA], val[:, b], ACT.Copy).then_inc(mid_done, 1)

        @block.gpsimd
        def _(pool):
            pool.memset(wh[:, :, :, D:DA], 1.0).then_inc(set_up, 1)
            pool.wait_ge(max_done, 1)
            pool.partition_all_reduce(ca[:], cm[:], P, bass.bass_isa.ReduceOp.max).then_inc(all_max, 1)

        @block.vector
        def _(dve):
            chain = Chain(dve, dve_steps)
            dve.wait_ge(loaded, 16 * LOADS)
            dve.wait_ge(wa_done, 1)
            dve.tensor_copy(w[:, :, C:C + 2 * H], ps_m[:, 0:KC * 2 * H].rearrange("p (k c) -> p k c", k=KC)).then_inc(wa_kept, 1)
            with dve.Fori(0, NT // 4) as i:
                for b in range(4):
                    dve.bn_stats(st[:, bass.ds(i * 4 + b, 1), :].rearrange("p t s -> p (t s)"),
                                 x[:, bass.ds(i * 4 + b, 1), :].rearrange("p t s -> p (t s)")).then_inc(stats_done, 1)
            dve.wait_ge(stats_done, NT)
            layer_norm_tail(chain, st, mu, var, tmp, var_done)
            inverse_root(chain, var[:], root[:], rstd[:], tmp[:], root_done, 1)
            with dve.Fori(0, NT // 2) as i:
                for b in range(2):
                    t = i * 2 + b
                    dve.wait_ge(xn_turned, t)
                    dve.tensor_scalar(xn[:, b:b + 1, :], x[:, bass.ds(t, 1), :], mu[:, bass.ds(t, 1)], rstd[:, bass.ds(t, 1)],
                                      ALU.subtract, ALU.mult).then_inc(xn_done, 1)
                for b in range(2):
                    t = i * 2 + b
                    dve.wait_ge(wh_done, t + 1)
                    dve.tensor_copy(wh[:, bass.ds(t, 1), :, 0:D].rearrange("p t h d -> p (t h) d"),
                                    ps_w[b][:, 0:C].rearrange("p (h d) -> p h d", h=H)).then_inc(wh_kept, 1)
            dve.wait_ge(summed, 1)
            dve.tensor_copy(keep.mean[:], ps_m[:, 0:C]).then_inc(mean_kept, 1)
            dve.wait_ge(scores_kept, NT)
            dve.tensor_reduce(cm[:], s2[:].rearrange("p t h -> p h t"), AX.X, ALU.max).then_inc(max_done, 1)
            dve.wait_ge(all_max, 1)
            dve.tensor_tensor(d2[:], s2[:], spread(ca[:], 1, NT), ALU.subtract).then_inc(exps_in, 1)
            chain.step(dve.tensor_tensor(u[:], s1[:], spread(ca[:], 1, NT), ALU.add))
            chain.step(dve.scalar_tensor_tensor(um[:], u[:], SLOPE, u[:], ALU.mult, ALU.max))
            chain.step(dve.scalar_tensor_tensor(u2[:], u[:], SLOPE, um[:], ALU.mult, ALU.subtract))
            dve.tensor_tensor(u[:], u[:], um[:], ALU.subtract).then_inc(exps_in, 2)
            dve.wait_ge(exps_done, 2)
            dve.wait_ge(set_up, 1)
            with dve.Fori(0, NC) as i:
                whv = wh[:, bass.ds(i * TPC, TPC), :, :].rearrange("p t h d -> p (t h) d")
                for b, s in enumerate((e2, f2)):
                    dve.wait_ge(lo_done, i * 2)
                    dve.tensor_tensor(val[:, b], whv,
                                      spread(s[:, bass.ds(i * TPC, TPC), :].rearrange("p t h -> p (t h)"), 2, DA),
                                      ALU.mult).then_inc(val_done, 1)
                for b, g in enumerate((keep.ge, keep.gf)):
                    gv = g[:, bass.ds(i * TPC * H, TPC * H), :]
                    dve.wait_ge(val_done, i * 2 + 2)
                    dve.wait_ge(hi_done, i * 2 + (b + 1))
                    dve.tensor_tensor(val[:, b], val[:, b], gv[:, :, 0:DA], ALU.subtract).then_inc(rest_done, 1)
                for b, g in enumerate((keep.ge, keep.gf)):
                    gv = g[:, bass.ds(i * TPC * H, TPC * H), :]
                    dve.wait_ge(rest_done, i * 2 + 2)
                    dve.wait_ge(mid_done, i * 2 + (b + 1))
                    dve.tensor_tensor(gv[:, :, 2 * DA:3 * DA], val[:, b], gv[:, :, DA:2 * DA], ALU.subtract).then_inc(lo_done, 1)


def layer_norm_tail(chain, st, mu, var, tmp, var_done):
    dve = chain.eng
    chain.step(dve.tensor_tensor(mu[:], st[:, :, 1], st[:, :, 4], ALU.add))
    chain.step(dve.tensor_scalar(mu[:], mu[:], 0.5, None, ALU.mult))
    chain.step(dve.tensor_tensor(tmp[:], st[:, :, 1], st[:, :, 4], ALU.subtract))
    chain.step(dve.tensor_tensor(tmp[:], tmp[:], tmp[:], ALU.mult))
    chain.step(dve.tensor_tensor(var[:], st[:, :, 2], st[:, :, 5], ALU.add))
    chain.step(dve.tensor_scalar(var[:], var[:], 1.0 / C, 1e-5, ALU.mult, ALU.add))
    dve.scalar_tensor_tensor(var[:], tmp[:], 0.25, var[:], ALU.mult, ALU.add).then_inc(var_done, 1)


def graph_attention(nc, io, keep):
    QJ = N // 4
    NP2 = NT // 2
    USES = H * NP2 // 2
    with ExitStack() as ctx:
        m = Pool(nc, ctx)
        nat = m.sb("ga_nat", [P, 4, TPC, QJ], BF16)
        no_edge = m.sb("ga_no_edge", [P, NT, CH], BF16)
        identb = m.sb("ga_identb", [P, P], BF16)
        sel1 = m.sb("ga_sel1", [P, DA])
        sel2 = m.sb("ga_sel2", [GREST, DA])
        s1b = m.sb("ga_s1b", [P, H, CH])
        sign = m.sb("ga_sign", [P, 2, 2, CH], BF16)
        pos = m.sb("ga_pos", [P, 2, 2, CH], BF16)
        neg = m.sb("ga_neg", [P, 2, 2, CH], BF16)
        ev = m.sb("ga_ev", [P, 4, CH])
        out = m.sb("ga_out", [P, TPC, C])
        xr = m.sb("ga_xr", [P, TPC, C])
        te = m.sb("ga_te", [P, TPC, DA])
        tf = m.sb("ga_tf", [P, TPC, DA])
        lone = m.sb("ga_lone", [P, TPC, 1])
        den = m.sb("ga_den", [P, TPC, 1])
        acc = [m.bank(f"ga_acc{b}") for b in range(4)]
        ps_t = [m.bank(f"ga_ps_t{b}", BF16) for b in range(2)]
        ps_n = m.bank("ga_ps_n", F32, 2)

        const_in = m.sem("ga_const_in")
        cast_in = m.sem("ga_cast_in")
        adj_in = [m.sem(f"ga_adj_in{q}") for q in range(4)]
        rows_in = m.sem("ga_rows_in")
        x_in = m.sem("ga_x_in")
        turned = m.sem("ga_turned")
        no_edge_kept = [m.sem(f"ga_no_edge_kept{b}") for b in range(2)]
        signs = [m.sem(f"ga_signs{b}") for b in range(2)]
        pos_done = [m.sem(f"ga_pos_done{b}") for b in range(2)]
        neg_done = [m.sem(f"ga_neg_done{b}") for b in range(2)]
        mask_used = [m.sem(f"ga_mask_used{b}") for b in range(2)]
        ev_act = m.sem("ga_ev_act")
        ev_dve = m.sem("ga_ev_dve")
        natural = m.sem("ga_natural")
        nat_read = m.sem("ga_nat_read")
        steps = m.sem("ga_steps")
        stored = m.sem("ga_stored")
        block = ctx.enter_context(nc.Block())
        TAIL = 9

        @block.gpsimd
        def _(pool):
            pool.dma_start(identb[:], io["ident"]).then_inc(cast_in, 16)
            for q in range(4):
                pool.dma_start(nat[:, q], io["adj"][0:CH, q * QJ:(q + 1) * QJ].rearrange("(t p) j -> p t j", p=P)).then_inc(adj_in[q], 16)
            with pool.Fori(1, NC) as c:
                for q in range(4):
                    pool.wait_ge(turned, c * NP2 + ((q + 1) * (NP2 // 4) - NP2))
                    src = io["adj"][bass.ds(c * CH, CH), q * QJ:(q + 1) * QJ].rearrange("(t p) j -> p t j", p=P)
                    pool.dma_start(nat[:, q], src).then_inc(adj_in[q], 16)

        @block.sync
        def _(sp):
            sp.dma_start(sel1[:], io["sel"][0:P, :]).then_inc(const_in, 16)
            sp.dma_start(sel2[:], io["sel"][P:GW, :]).then_inc(const_in, 16)
            with sp.Fori(0, NC) as c:
                for b in range(2):
                    sp.wait_ge(signs[b], c * USES)
                for h in range(H):
                    sp.dma_start(s1b[:, h, :], io["s1_rows"][h, bass.ds(c * CH, CH)].partition_broadcast(P)).then_inc(rows_in, 16)
                sp.wait_ge(steps, c * (H * TAIL))
                sp.dma_start(xr[:], io["x"][bass.ds(c * CH, CH), :].rearrange("(t p) f -> p t f", p=P)).then_inc(x_in, 16)
                sp.wait_ge(steps, c * (H * TAIL) + H * TAIL)
                sp.dma_start(io["x1"][bass.ds(c * CH, CH), :].rearrange("(t p) f -> p t f", p=P), out[:]).then_inc(stored, 16)
            sp.wait_ge(stored, 16 * NC)

        @block.tensor
        def _(pe):
            pe.wait_ge(const_in, 32)
            pe.wait_ge(cast_in, 16)
            with pe.Fori(0, NC) as c:
                for q in range(4):
                    pe.wait_ge(adj_in[q], c * 16 + 16)
                    for k in range(NP2 // 4):
                        n = q * (NP2 // 4) + k
                        b = n % 2
                        pe.wait_ge(no_edge_kept[b], c * (NP2 // 2) + n // 2)
                        for j in range(2):
                            for it in range(TPC):
                                last = pe.transpose(ps_t[b][:, j * CH + it * P:j * CH + (it + 1) * P],
                                                    nat[:, q, it, (2 * k + j) * P:(2 * k + j + 1) * P], identb[:])
                        last.then_inc(turned, 1)
                with pe.Fori(0, H) as h:
                    hc = c * H + h
                    for n in range(NP2):
                        b = n % 2
                        for mask, ready, g, a in ((pos, pos_done, keep.ge, 0), (neg, neg_done, keep.gf, 2)):
                            pe.wait_ge(ready[b], hc * (NP2 // 2) + (n // 2 + 1))
                            for j in range(2):
                                jt = 2 * n + j
                                at = g[:, bass.ds(h + jt * H, 1), :].rearrange("p a g -> p (a g)")
                                pe.matmul(acc[a][:, :], at[:, 0:P], mask[:, b, j, :], start=jt == 0, stop=jt == NT - 1)
                                last = pe.matmul(acc[a + 1][0:GREST, :], at[:, P:GW], mask[:, b, j, :], start=jt == 0, stop=jt == NT - 1)
                        last.then_inc(mask_used[b], 1)
                    pe.wait_ge(ev_act, hc * 2 + 2)
                    pe.wait_ge(ev_dve, hc * 2 + 2)
                    pe.wait_ge(nat_read, hc)
                    for it in range(TPC):
                        for r in range(2):
                            o = ps_n[:, (it // 2) * 512 + ((it % 2) * 2 + r) * DA:(it // 2) * 512 + ((it % 2) * 2 + r + 1) * DA]
                            pe.matmul(o, ev[:, 2 * r, it * P:(it + 1) * P], sel1[:], start=True, stop=False)
                            last = pe.matmul(o, ev[0:GREST, 2 * r + 1, it * P:(it + 1) * P], sel2[:], start=False, stop=True)
                    last.then_inc(natural, 1)

        @block.scalar
        def _(act):
            with act.Fori(0, NC) as c:
                for n in range(0, NP2, 2):
                    act.wait_ge(turned, c * NP2 + (n + 1))
                    if n == 0:
                        act.wait_ge(neg_done[1], c * USES)
                    act.activation(no_edge[:, 2 * n:2 * n + 2, :], ps_t[0][:].rearrange("p (j i) -> p j i", j=2), ACT.Relu,
                                   scale=-1.0, bias=1.0).then_inc(no_edge_kept[0], 1)
                act.wait_ge(rows_in, c * (16 * H) + 16 * H)
                with act.Fori(0, H) as h:
                    hc = c * H + h
                    for n in range(NP2):
                        act.wait_ge(pos_done[n % 2], hc * (NP2 // 2) + n // 2)
                        for j in range(2):
                            last = act.activation(sign[:, n % 2, j:j + 1, :], s1b[:, bass.ds(h, 1), :], ACT.Sign,
                                                  bias=keep.s2[:, 2 * n + j, bass.ds(h, 1)])
                        last.then_inc(signs[n % 2], 1)
                    act.wait_ge(mask_used[1], hc * (NP2 // 2) + NP2 // 2)
                    act.wait_ge(natural, hc)
                    for a in (0, 2):
                        act.activation(ev[:, a, :], acc[a][:], ACT.Copy).then_inc(ev_act, 1)

        @block.vector
        def _(dve):
            chain = Chain(dve, steps)
            with dve.Fori(0, NC) as c:
                for n in range(1, NP2, 2):
                    dve.wait_ge(turned, c * NP2 + (n + 1))
                    dve.tensor_scalar(no_edge[:, 2 * n:2 * n + 2, :], ps_t[1][:].rearrange("p (j i) -> p j i", j=2), 0.0, None,
                                      ALU.is_le).then_inc(no_edge_kept[1], 1)
                with dve.Fori(0, H) as h:
                    hc = c * H + h
                    chain.at(hc * TAIL)
                    for n in range(NP2):
                        b = n % 2
                        use = hc * (NP2 // 2) + n // 2
                        if n == 0:
                            for k in range(2):
                                dve.wait_ge(no_edge_kept[k], c * (NP2 // 2) + NP2 // 2)
                        dve.wait_ge(signs[b], use + 1)
                        dve.wait_ge(mask_used[b], use)
                        no = no_edge[:, 2 * n:2 * n + 2, :].rearrange("p j i -> p (j i)")
                        dve.tensor_tensor(pos[:, b].rearrange("p j i -> p (j i)"), sign[:, b].rearrange("p j i -> p (j i)"), no,
                                          ALU.is_gt).then_inc(pos_done[b], 1)
                        dve.wait_ge(pos_done[b], use + 1)
                        dve.tensor_tensor(neg[:, b].rearrange("p j i -> p (j i)"), pos[:, b].rearrange("p j i -> p (j i)"), no,
                                          ALU.is_equal).then_inc(neg_done[b], 1)
                    dve.wait_ge(mask_used[1], hc * (NP2 // 2) + NP2 // 2)
                    dve.wait_ge(natural, hc)
                    for a in (1, 3):
                        dve.tensor_copy(ev[0:GREST, a, :], acc[a][0:GREST, :]).then_inc(ev_dve, 1)
                    dve.wait_ge(natural, hc + 1)
                    pn = ps_n[:].rearrange("p (g c) -> p g c", g=2)[:, :, 0:4 * DA].rearrange("p g (i r d) -> p g i r d", i=2, r=2)
                    def by(f):
                        return spread(f[:, bass.ds(c * TPC, TPC), bass.ds(h, 1)].rearrange("p (g i) h -> p g (i h)", g=2), 3, DA)
                    te4 = te[:].rearrange("p (g i) d -> p g i d", g=2)
                    tf4 = tf[:].rearrange("p (g i) d -> p g i d", g=2)
                    chain.step(dve.tensor_tensor(te4, pn[:, :, :, 0, :], by(keep.e1), ALU.mult))
                    ins = dve.tensor_tensor(tf4, pn[:, :, :, 1, :], by(keep.f1), ALU.mult)
                    ins.then_inc(nat_read, 1)
                    dve.wait_ge(nat_read, hc + 1)
                    chain.step(dve.tensor_tensor(te[:], te[:], tf[:], ALU.add))
                    chain.step(dve.tensor_scalar(lone[:], te[:, :, D:DA], 0.0, None, ALU.is_equal))
                    chain.step(dve.tensor_tensor(den[:], te[:, :, D:DA], lone[:], ALU.add))
                    chain.step(dve.reciprocal(den[:], den[:]))
                    chain.step(dve.tensor_tensor(te[:, :, 0:D], te[:, :, 0:D], den[:].to_broadcast([P, TPC, D]), ALU.mult))
                    chain.step(dve.tensor_tensor(tf[:, :, 0:D], lone[:].to_broadcast([P, TPC, D]),
                                                 spread(keep.mean[:, bass.ds(h * D, D)], 1, TPC), ALU.mult))
                    chain.step(dve.tensor_tensor(te[:, :, 0:D], te[:, :, 0:D], tf[:, :, 0:D], ALU.add))
                    dve.wait_ge(x_in, c * 16 + 16)
                    dve.wait_ge(stored, c * 16)
                    chain.step(dve.tensor_tensor(out[:, :, bass.ds(h * D, D)], te[:, :, 0:D],
                                                 xr[:, :, bass.ds(h * D, D)], ALU.add))
                    assert chain.n == TAIL


def products(pe, out, lhs, rhs, start=True, stop=True):
    n = len(lhs)
    for k in range(n):
        (lh, ll), (rh, rl) = lhs[k], rhs[k]
        pe.matmul(out, lh, rh, start=start and k == 0, stop=False)
        pe.matmul(out, lh, rl, start=False, stop=False)
        last = pe.matmul(out, ll, rh, start=False, stop=stop and k == n - 1)
    return last


def project_qkv(nc, io, keep):
    with ExitStack() as ctx:
        m = Pool(nc, ctx)
        y = keep.y
        va = m.sb("pq_va", [P, NT, KV, VW], F32R)
        raw = m.sb("pq_raw", [P, KC, QKW + P])
        wh = m.sb("pq_wh", [P, KC, QKW + P], F32R)
        wl = m.sb("pq_wl", [P, KC, QKW + P], F32R)
        ln1 = m.sb("pq_ln1", [P, KC])
        ident = m.sb("pq_ident", [P, P])
        trig = m.sb("pq_trig", [P, 2, CH])
        st = m.sb("pq_stats", [P, NT, 6])
        mu = m.sb("pq_mu", [P, NT])
        var = m.sb("pq_var", [P, NT])
        tmp = m.sb("pq_tmp", [P, NT])
        root = m.sb("pq_root", [P, NT])
        rstd = m.sb("pq_rstd", [P, NT])
        sq = m.sb("pq_sq", [P, NT])
        junk = m.sb("pq_junk", [P, 4, C])
        hn = m.sb("pq_hn", [P, TPC, C])
        hh = m.sb("pq_hh", [P, KC, CH], F32R)
        hl = m.sb("pq_hl", [P, KC, CH], F32R)
        ta = m.sb("pq_ta", [P, 3, CH])
        tb = m.sb("pq_tb", [P, 3, CH])
        rh = m.sb("pq_rh", [P, 3, CH], F32R)
        rl = m.sb("pq_rl", [P, 3, CH], F32R)
        ps_t = [m.bank(f"pq_ps_t{k}") for k in range(KC)]
        ps_a = [m.bank(f"pq_ps_a{b}") for b in range(2)]
        ps_b = [m.bank(f"pq_ps_b{b}") for b in range(2)]
        ps_v = m.bank("pq_ps_v")
        loaded = m.sem("pq_loaded")
        trig_in = m.sem("pq_trig_in")
        wh_done = m.sem("pq_wh_done")
        wl_done = m.sem("pq_wl_done")
        dve_steps = m.sem("pq_dve_steps")
        stats_done = m.sem("pq_stats_done")
        var_done = m.sem("pq_var_done")
        root_done = m.sem("pq_root_done")
        y_done = m.sem("pq_y_done")
        sq_done = m.sem("pq_sq_done")
        ms_done = m.sem("pq_ms_done")
        root2_done = m.sem("pq_root2_done")
        hn_done = m.sem("pq_hn_done")
        turned = m.sem("pq_turned")
        hh_done = m.sem("pq_hh_done")
        hl_done = m.sem("pq_hl_done")
        pair_done = m.sem("pq_pair_done")
        v_done = m.sem("pq_v_done")
        ta_done = m.sem("pq_ta_done")
        tb_done = m.sem("pq_tb_done")
        rope_done = m.sem("pq_rope_done")
        rh_done = m.sem("pq_rh_done")
        rl_done = m.sem("pq_rl_done")
        vh_done = m.sem("pq_vh_done")
        vl_done = m.sem("pq_vl_done")
        ones_set = m.sem("pq_ones_set")
        moved = m.sem("pq_moved")
        stored = m.sem("pq_stored")
        block = ctx.enter_context(nc.Block())
        LOADS = 7
        MOVES = 6

        @block.sync
        def _(sp):
            for q in range(4):
                sp.dma_start(y[:, 8 * q:8 * q + 8, :], io["x1"].rearrange("(t p) f -> p t f", p=P)[:, 8 * q:8 * q + 8, :]).then_inc(loaded, 16)
            sp.dma_start(raw[:], io["w_qkv"].rearrange("(k p) o -> p k o", p=P)).then_inc(loaded, 16)
            sp.dma_start(ln1[:], io["ln1"]).then_inc(loaded, 16)
            sp.dma_start(ident[:], io["ident"]).then_inc(loaded, 16)
            with sp.Fori(0, NC) as c:
                sp.wait_ge(tb_done, c * 3)
                sp.wait_ge(ta_done, c * 3)
                at = bass.ds(c * CH, CH)
                sp.dma_start(trig[:], io["trig"][:, :, at]).then_inc(trig_in, 16)
                for j in range(2):
                    sp.wait_ge(rh_done, c * 3 + (j + 1))
                    sp.wait_ge(rl_done, c * 3 + (j + 1))
                    sp.dma_start(io["q_high"][j * P:(j + 1) * P, at], rh[:, j, :].bitcast(F32)).then_inc(moved, 16)
                    sp.dma_start(io["q_low"][j * P:(j + 1) * P, at], rl[:, j, :].bitcast(F32)).then_inc(moved, 16)
                sp.wait_ge(rh_done, c * 3 + 3)
                sp.wait_ge(rl_done, c * 3 + 3)
                sp.dma_start(io["k_high"][:, at], rh[:, 2, :].bitcast(F32)).then_inc(moved, 16)
                sp.dma_start(io["k_low"][:, at], rl[:, 2, :].bitcast(F32)).then_inc(moved, 16)
            sp.wait_ge(moved, 16 * MOVES * NC)
            sp.wait_ge(vh_done, NC)
            sp.wait_ge(vl_done, NC)
            sp.wait_ge(ones_set, 2)
            for g in range(KV):
                sp.dma_start(io["va"][g], va[:, :, g, :].bitcast(F32)).then_inc(stored, 16)
            sp.wait_ge(stored, 16 * KV)

        @block.gpsimd
        def _(pool):
            pool.memset(va[:, :, :, D:DA].bitcast(F32), 1.0).then_inc(ones_set, 1)
            pool.memset(va[:, :, :, DA + D:VW].bitcast(F32), 0.0).then_inc(ones_set, 1)
            pool.wait_ge(ones_set, 2)

        @block.scalar
        def _(act):
            act.wait_ge(loaded, 16 * LOADS)
            act.activation(wh[:], raw[:], ACT.Copy).then_inc(wh_done, 1)
            act.wait_ge(var_done, 1)
            act.activation(root[:], var[:], ACT.Sqrt).then_inc(root_done, 1)
            with act.Fori(0, NT // 4) as i:
                act.wait_ge(sq_done, i * 4)
                for b in range(4):
                    t = i * 4 + b
                    act.wait_ge(y_done, t + 1)
                    act.activation(junk[:, b:b + 1, :], y[:, bass.ds(t, 1), :], ACT.Square, accum_out=sq[:, bass.ds(t, 1)]).then_inc(sq_done, 1)
            act.wait_ge(ms_done, 1)
            act.activation(root[:], var[:], ACT.Sqrt).then_inc(root2_done, 1)
            with act.Fori(0, NC) as c:
                act.wait_ge(turned, c + 1)
                act.wait_ge(v_done, c)
                for k in range(KC):
                    act.activation(hh[:, k, :], ps_t[k][:], ACT.Copy, scale=ln1[:, k:k + 1]).then_inc(hh_done, 1)
                act.wait_ge(moved, c * (16 * MOVES))
                for j in range(3):
                    act.wait_ge(rope_done, c * 3 + (j + 1))
                    act.activation(rh[:, j, :], ta[:, j, :], ACT.Copy).then_inc(rh_done, 1)
                act.wait_ge(v_done, c + 1)
                act.activation(va[:, bass.ds(c * TPC, TPC), :, 0:D].rearrange("p t g d -> p (t g) d"),
                               ps_v[:].rearrange("p (t g d) -> p (t g) d", g=KV, d=D), ACT.Copy).then_inc(vh_done, 1)

        @block.tensor
        def _(pe):
            pe.wait_ge(loaded, 16 * LOADS)
            pe.wait_ge(wh_done, 1)
            pe.wait_ge(wl_done, 1)
            with pe.Fori(0, NC) as c:
                pe.wait_ge(hn_done, c * TPC + TPC)
                pe.wait_ge(hl_done, c * KC)
                for k in range(KC):
                    for it in range(TPC):
                        last = pe.transpose(ps_t[k][:, it * P:(it + 1) * P], hn[:, it, k * P:(k + 1) * P], ident[:])
                last.then_inc(turned, 1)
                pe.wait_ge(hh_done, c * KC + KC)
                pe.wait_ge(hl_done, c * KC + KC)
                act_k = [(hh[:, k, :], hl[:, k, :]) for k in range(KC)]
                for j in range(3):
                    if j < 2:
                        pe.wait_ge(tb_done, c * 3)
                        pe.wait_ge(ta_done, c * 3)
                    else:
                        pe.wait_ge(tb_done, c * 3 + 1)
                        pe.wait_ge(ta_done, c * 3 + 1)
                    for s, ps in ((0, ps_a), (1, ps_b)):
                        col = slice((2 * j + s) * P, (2 * j + s + 1) * P)
                        last = products(pe, ps[j % 2][:], [(wh[:, k, col], wl[:, k, col]) for k in range(KC)], act_k)
                    last.then_inc(pair_done, 1)
                pe.wait_ge(vh_done, c)
                pe.wait_ge(vl_done, c)
                for it in range(TPC):
                    tok = slice(it * P, (it + 1) * P)
                    last = products(pe, ps_v[:, tok], [(hh[:, k, tok], hl[:, k, tok]) for k in range(KC)],
                                    [(wh[:, k, QKW:], wl[:, k, QKW:]) for k in range(KC)])
                last.then_inc(v_done, 1)

        @block.vector
        def _(dve):
            chain = Chain(dve, dve_steps)
            dve.wait_ge(loaded, 16 * LOADS)
            dve.wait_ge(wh_done, 1)
            dve.tensor_tensor(wl[:], raw[:], wh[:].bitcast(F32), ALU.subtract).then_inc(wl_done, 1)
            with dve.Fori(0, NT // 4) as i:
                for b in range(4):
                    dve.bn_stats(st[:, bass.ds(i * 4 + b, 1), :].rearrange("p t s -> p (t s)"),
                                 y[:, bass.ds(i * 4 + b, 1), :].rearrange("p t s -> p (t s)")).then_inc(stats_done, 1)
            dve.wait_ge(stats_done, NT)
            layer_norm_tail(chain, st, mu, var, tmp, var_done)
            inverse_root(chain, var[:], root[:], rstd[:], tmp[:], root_done, 1)
            with dve.Fori(0, NT) as t:
                dve.tensor_scalar(y[:, bass.ds(t, 1), :], y[:, bass.ds(t, 1), :], mu[:, bass.ds(t, 1)], rstd[:, bass.ds(t, 1)],
                                  ALU.subtract, ALU.mult).then_inc(y_done, 1)
            dve.wait_ge(sq_done, NT)
            dve.tensor_scalar(var[:], sq[:], 1.0 / C, 1e-6, ALU.mult, ALU.add).then_inc(ms_done, 1)
            inverse_root(chain, var[:], root[:], rstd[:], tmp[:], root2_done, 1)
            with dve.Fori(0, NC) as c:
                dve.wait_ge(turned, c)
                for it in range(TPC):
                    t = c * TPC + it
                    dve.tensor_scalar(hn[:, it:it + 1, :], y[:, bass.ds(t, 1), :], rstd[:, bass.ds(t, 1)], None, ALU.mult).then_inc(hn_done, 1)
                for k in range(KC):
                    dve.wait_ge(hh_done, c * KC + KC)
                    dve.scalar_tensor_tensor(hl[:, k, :], ps_t[k][:], ln1[:, k:k + 1], hh[:, k, :].bitcast(F32), ALU.mult,
                                             ALU.subtract).then_inc(hl_done, 1)
                dve.wait_ge(trig_in, c * 16 + 16)
                dve.wait_ge(moved, c * (16 * MOVES))
                for j in range(3):
                    dve.wait_ge(pair_done, c * 3 + (j + 1))
                    dve.wait_ge(rh_done, c * 3)
                    dve.tensor_tensor(ta[:, j, :], ps_a[j % 2][:], trig[:, 0, :], ALU.mult).then_inc(ta_done, 1)
                    dve.tensor_tensor(tb[:, j, :], ps_b[j % 2][:], trig[:, 1, :], ALU.mult).then_inc(tb_done, 1)
                    dve.wait_ge(tb_done, c * 3 + (j + 1))
                    dve.wait_ge(ta_done, c * 3 + (j + 1))
                    dve.tensor_tensor(ta[:, j, :], ta[:, j, :], tb[:, j, :], ALU.add).then_inc(rope_done, 1)
                    dve.wait_ge(rope_done, c * 3 + (j + 1))
                    dve.wait_ge(rh_done, c * 3 + (j + 1))
                    dve.tensor_tensor(rl[:, j, :], ta[:, j, :], rh[:, j, :].bitcast(F32), ALU.subtract).then_inc(rl_done, 1)
                dve.wait_ge(vh_done, c + 1)
                vt = va[:, bass.ds(c * TPC, TPC), :, :].rearrange("p t g d -> p (t g) d")
                dve.tensor_tensor(vt[:, :, DA:DA + D], ps_v[:].rearrange("p (t g d) -> p (t g) d", g=KV, d=D),
                                  vt[:, :, 0:D].bitcast(F32), ALU.subtract).then_inc(vl_done, 1)


def sequence_attention(nc, io, keep):
    with ExitStack() as ctx:
        m = Pool(nc, ctx)
        identb = m.sb("sa_identb", [P, P], BF16)
        ident = m.sb("sa_ident", [P, P])
        late_k = m.sb("sa_late_k", [P, P], BF16)
        late_q = m.sb("sa_late_q", [P, P], BF16)
        onesf = m.sb("sa_onesf", [P, P])
        ones = m.sb("sa_ones", [P, DA], F32R)
        ks = m.sb("sa_ks", [P, N], F32R)
        kb = m.sb("sa_kb", [DA, N], F32R)
        va = m.sb("sa_va", [P, NT, VW], F32R)
        qa = [m.sb(f"sa_qa{b}", [P, CH], F32R) for b in range(2)]
        qb = [m.sb(f"sa_qb{b}", [DA, CH], F32R) for b in range(2)]
        mx = [m.sb(f"sa_mx{b}", [P, TPC, NC]) for b in range(2)]
        m4 = [m.sb(f"sa_m4{b}", [P, TPC]) for b in range(2)]
        dg = m.sb("sa_dg", [P, TPC, P], F32R)
        ph = [m.sb(f"sa_ph{b}", [P, CH], F32R) for b in range(3)]
        pl = [m.sb(f"sa_pl{b}", [P, CH], F32R) for b in range(3)]
        ysb = m.sb("sa_ysb", [DA, CH])
        rec = m.sb("sa_rec", [P, TPC])
        yo = [m.sb(f"sa_yo{b}", [P, TPC, D]) for b in range(2)]
        ps_n = [m.bank(f"sa_ps_n{b}") for b in range(2)]
        ps_s = [m.bank(f"sa_ps_s{b}") for b in range(3)]
        ps_y = m.bank("sa_ps_y")
        ps_m = m.bank("sa_ps_m")
        ps_x = m.bank("sa_ps_x")
        const_in = m.sem("sa_const_in")
        cast_in = m.sem("sa_cast_in")
        ones_set = m.sem("sa_ones_set")
        kv_first_in = m.sem("sa_kv_first_in")
        kv_rest_in = m.sem("sa_kv_rest_in")
        q_in = [m.sem(f"sa_q_in{b}") for b in range(2)]
        scored = [m.sem(f"sa_scored{b}") for b in range(2)]
        part_max = [m.sem(f"sa_part_max{b}") for b in range(2)]
        max_done = m.sem("sa_max_done")
        diag_done = m.sem("sa_diag_done")
        spread_done = m.sem("sa_spread_done")
        shift_done = m.sem("sa_shift_done")
        full_scored = m.sem("sa_full_scored")
        exp_done = m.sem("sa_exp_done")
        ph_done = m.sem("sa_ph_done")
        pl_done = m.sem("sa_pl_done")
        p_used = m.sem("sa_p_used")
        y_kept = m.sem("sa_y_kept")
        y_turned = m.sem("sa_y_turned")
        rec_done = m.sem("sa_rec_done")
        y_done = m.sem("sa_y_done")
        stored = [m.sem(f"sa_stored{b}") for b in range(2)]
        block = ctx.enter_context(nc.Block())

        ROUNDS = [(c, b) for c in range(NC) for b in range(2)]
        R = len(ROUNDS)
        first = [[(it, kc, CH if kc < c else (it + 1) * P) for it in range(TPC) for kc in range(c + 1)] for c, _ in ROUNDS]
        second = [[(kt, max(0, kt - c * TPC) * P) for kt in range((c + 1) * TPC)] for c, _ in ROUNDS]
        first_before = [sum(map(len, first[:n])) for n in range(R + 1)]
        second_before = [sum(map(len, second[:n])) for n in range(R + 1)]
        FIRST, SECOND = first_before[R], second_before[R]
        assert FIRST % 2 == 0

        def ahead(n, i):
            within, all_ = max(1, len(second[n]) - 4), len(first[n + 1])
            return range(min(all_, i * all_ // within), min(all_, (i + 1) * all_ // within))

        def spread_at(n):
            return len(second[n]) - 3

        @block.sync
        def _(sp):
            sp.dma_start(ident[:], io["ident"]).then_inc(const_in, 16)
            with sp.Fori(0, KV) as g:
                for n, (c, b) in enumerate(ROUNDS):
                    sp.wait_ge(y_done, g * R + (n + 1))
                    sp.dma_start(io["ya"][c * CH:(c + 1) * CH, bass.ds(g * (2 * D) + b * D, D)].rearrange("(t p) d -> p t d", p=P),
                                 yo[n % 2][:]).then_inc(stored[n % 2], 16)
            for b in range(2):
                sp.wait_ge(stored[b], 8 * KV * R)

        @block.gpsimd
        def _(pool):
            pool.memset(onesf[:], 1.0).then_inc(ones_set, 1)
            for tile, name in ((identb, "ident"), (late_k, "late_k"), (late_q, "late_q")):
                pool.dma_start(tile[:], io[name]).then_inc(cast_in, 16)
            with pool.Fori(0, KV) as g:
                rows = bass.ds(g * D, D)
                pool.wait_ge(p_used, g * SECOND)
                def load_kv(tiles, done):
                    at = slice(tiles.start * P, tiles.stop * P)
                    pool.dma_start(ks[0:D, at], io["k_high"][rows, at]).then_inc(done, 16)
                    pool.dma_start(ks[D:P, at], io["k_low"][rows, at]).then_inc(done, 16)
                    pool.dma_start(kb[0:D, at], io["k_high"][rows, at]).then_inc(done, 16)
                    pool.dma_start(va[:, tiles], io["va"][bass.ds(g, 1), :, tiles, :].rearrange("g p t d -> (g p) t d")).then_inc(done, 16)

                load_kv(slice(0, TPC), kv_first_in)
                for n, (c, b) in enumerate(ROUNDS):
                    if n >= 2:
                        pool.wait_ge(p_used, g * SECOND + second_before[n - 1])
                    head, at = bass.ds(g * (2 * D) + b * D, D), slice(c * CH, (c + 1) * CH)
                    pool.dma_start(qa[n % 2][0:D, :], io["q_high"][head, at]).then_inc(q_in[n % 2], 16)
                    pool.dma_start(qa[n % 2][D:P, :], io["q_high"][head, at]).then_inc(q_in[n % 2], 16)
                    pool.dma_start(qb[n % 2][0:D, :], io["q_low"][head, at]).then_inc(q_in[n % 2], 16)
                    if n == 1:
                        load_kv(slice(TPC, NT), kv_rest_in)

        @block.tensor
        def _(pe):
            pe.wait_ge(const_in, 16)
            pe.wait_ge(cast_in, 48)
            pe.wait_ge(ones_set, 3)
            with pe.Fori(0, KV) as g:
                def first_pass(n, some):
                    c, _ = ROUNDS[n]
                    if some.start == 0:
                        pe.wait_ge(q_in[n % 2], g * (24 * R) + 48 * (n // 2 + 1))
                    for i in some:
                        it, kc, cols = first[n][i]
                        step = first_before[n] + i
                        pe.wait_ge(part_max[step % 2], g * (FIRST // 2) + step // 2)
                        ps = ps_n[step % 2]
                        last = pe.matmul(ps[:, 0:cols], qa[n % 2][0:D, it * P:(it + 1) * P], ks[0:D, kc * CH:kc * CH + cols],
                                         start=True, stop=kc < c)
                        if kc == c:
                            last = pe.matmul(ps[:, cols - P:cols], identb[:], late_k[:], start=False, stop=True)
                        last.then_inc(scored[step % 2], 1)

                def spread_shift(n):
                    pe.wait_ge(diag_done, g * (R * TPC) + TPC * (n + 1))
                    pe.wait_ge(shift_done, g * R + n)
                    for it in range(TPC):
                        last = pe.matmul(ps_m[0:DA, it * P:(it + 1) * P], ones[:], dg[:, it, :], start=True, stop=True)
                    last.then_inc(spread_done, 1)

                def scores(n, i):
                    c, _ = ROUNDS[n]
                    kt, lo = second[n][i]
                    step = second_before[n] + i
                    pe.wait_ge(pl_done, g * SECOND + max(0, step - 2))
                    ps, keys = ps_s[step % 3], slice(kt * P, (kt + 1) * P)
                    pe.matmul(ps[:, lo:CH], ks[:, keys], qa[n % 2][:, lo:CH], start=True, stop=False)
                    last = pe.matmul(ps[:, lo:CH], kb[:, keys], qb[n % 2][:, lo:CH], start=False, stop=kt < c * TPC)
                    if kt >= c * TPC:
                        last = pe.matmul(ps[:, lo:lo + P], identb[:], late_q[:], start=False, stop=True)
                    last.then_inc(full_scored, 1)

                def weigh(n, i):
                    kt, lo = second[n][i]
                    step = second_before[n] + i
                    pe.wait_ge(ph_done, g * SECOND + (step + 1))
                    pe.wait_ge(pl_done, g * SECOND + (step + 1))
                    high, low = va[:, kt, 0:DA], va[:, kt, DA:2 * DA]
                    out, last_kt = ps_y[0:DA, lo:CH], i == len(second[n]) - 1
                    pe.matmul(out, high, ph[step % 3][:, lo:CH], start=i == 0, stop=False)
                    pe.matmul(out, low, ph[step % 3][:, lo:CH], start=False, stop=False)
                    pe.matmul(out, high, pl[step % 3][:, lo:CH], start=False, stop=last_kt).then_inc(p_used, 1)

                def turn_back(n):
                    pe.wait_ge(y_kept, g * R + (n + 1))
                    pe.wait_ge(y_done, g * R + n)
                    for it in range(TPC):
                        last = pe.transpose(ps_x[:, it * DA:(it + 1) * DA], ysb[:, it * P:(it + 1) * P], ident[0:DA, 0:DA])
                    last.then_inc(y_turned, 1)

                pe.wait_ge(kv_first_in, g * 64 + 64)
                first_pass(0, range(len(first[0])))
                spread_shift(0)
                pe.wait_ge(shift_done, g * R + 1)
                scores(0, 0)
                scores(0, 1)
                for n in range(R):
                    for i in range(len(second[n])):
                        if i == spread_at(n) and n + 1 < R:
                            spread_shift(n + 1)
                        if i + 2 < len(second[n]):
                            scores(n, i + 2)
                        elif n + 1 < R:
                            if i + 2 == len(second[n]):
                                pe.wait_ge(shift_done, g * R + (n + 2))
                            scores(n + 1, i + 2 - len(second[n]))
                        if n + 1 < R:
                            if n == 1 and i == 0:
                                pe.wait_ge(kv_rest_in, g * 64 + 64)
                            first_pass(n + 1, ahead(n, i))
                        if i == 0:
                            pe.wait_ge(y_kept, g * R + n)
                        weigh(n, i)
                        if i == 1 and n > 0:
                            turn_back(n - 1)
                turn_back(R - 1)

        @block.scalar
        def _(act):
            act.wait_ge(ones_set, 1)
            act.activation(ones[:], onesf[:, 0:DA], ACT.Copy).then_inc(ones_set, 1)
            for k in range(N // CH):
                last = act.activation(kb[D:DA, k * CH:(k + 1) * CH].rearrange("o (a b) -> o a b", b=P),
                                      spread(onesf[D:DA, :], 1, TPC), ACT.Copy)
            last.then_inc(ones_set, 1)
            with act.Fori(0, KV) as g:
                def keep_shift(n):
                    act.wait_ge(spread_done, g * R + (n + 1))
                    act.wait_ge(p_used, g * SECOND + (second_before[n - 1] if n >= 2 else 0))
                    act.activation(qb[n % 2][D:DA, :], ps_m[D:DA, :], ACT.Copy).then_inc(shift_done, 1)

                def keep_sums(n):
                    act.wait_ge(p_used, g * SECOND + second_before[n + 1])
                    act.wait_ge(y_turned, g * R + n)
                    act.activation(ysb[:], ps_y[0:DA, :], ACT.Copy).then_inc(y_kept, 1)

                def exps(n, i):
                    lo, step = second[n][i][1], second_before[n] + i
                    act.wait_ge(full_scored, g * SECOND + (step + 1))
                    act.activation(ps_s[step % 3][:, lo:CH], ps_s[step % 3][:, lo:CH], ACT.Exp, scale=D ** -0.5).then_inc(exp_done, 1)

                def high_part(n, i):
                    lo, step = second[n][i][1], second_before[n] + i
                    act.wait_ge(exp_done, g * SECOND + (step + 1))
                    act.wait_ge(p_used, g * SECOND + max(0, step - 2))
                    act.activation(ph[step % 3][:, lo:CH], ps_s[step % 3][:, lo:CH], ACT.Copy).then_inc(ph_done, 1)

                keep_shift(0)
                for n in range(R):
                    for i in range(len(second[n])):
                        exps(n, i)
                        if i == len(second[n]) - 2 and n + 1 < R:
                            keep_shift(n + 1)
                        high_part(n, i)
                        if i == 0 and n > 0:
                            keep_sums(n - 1)
                keep_sums(R - 1)

        @block.vector
        def _(dve):
            dve.wait_ge(const_in, 16)
            with dve.Fori(0, KV) as g:
                def maxima(n, some):
                    for i in some:
                        it, kc, cols = first[n][i]
                        step = first_before[n] + i
                        dve.wait_ge(scored[step % 2], g * (FIRST // 2) + (step // 2 + 1))
                        dve.tensor_reduce(mx[n % 2][:, it, kc:kc + 1], ps_n[step % 2][:, 0:cols], AX.X, ALU.max).then_inc(part_max[step % 2], 1)

                def shift(n):
                    c, _ = ROUNDS[n]
                    for w in range(2):
                        dve.wait_ge(part_max[w], g * (FIRST // 2) + (first_before[n + 1] + 1 - w) // 2)
                    dve.tensor_reduce(m4[n % 2][:], mx[n % 2][:, :, 0:c + 1], AX.X, ALU.max).then_inc(max_done, 1)
                    dve.wait_ge(max_done, g * R + (n + 1))
                    dve.wait_ge(spread_done, g * R + n)
                    for it in range(TPC):
                        dve.tensor_scalar(dg[:, it, :], ident[:], m4[n % 2][:, it:it + 1], -1.0, ALU.mult, ALU.mult).then_inc(diag_done, 1)

                def finish(n):
                    dve.wait_ge(y_turned, g * R + (n + 1))
                    px = ps_x[:, 0:TPC * DA].rearrange("p (t d) -> p t d", d=DA)
                    dve.reciprocal(rec[:].unsqueeze(2), px[:, :, D:DA]).then_inc(rec_done, 1)
                    dve.wait_ge(rec_done, g * R + (n + 1))
                    dve.wait_ge(stored[n % 2], g * (8 * R) + 16 * (n // 2))
                    dve.tensor_tensor(yo[n % 2][:], px[:, :, 0:D], spread(rec[:], 2, D), ALU.mult).then_inc(y_done, 1)

                maxima(0, range(len(first[0])))
                shift(0)
                for n in range(R):
                    for i, (kt, lo) in enumerate(second[n]):
                        step = second_before[n] + i
                        dve.wait_ge(ph_done, g * SECOND + (step + 1))
                        dve.tensor_tensor(pl[step % 3][:, lo:CH], ps_s[step % 3][:, lo:CH], ph[step % 3][:, lo:CH].bitcast(F32),
                                          ALU.subtract).then_inc(pl_done, 1)
                        if n + 1 < R:
                            maxima(n + 1, ahead(n, i))
                            if ahead(n, i) and ahead(n, i).stop == len(first[n + 1]):
                                shift(n + 1)
                        if i == 2 and n > 0:
                            finish(n - 1)
                finish(R - 1)


def join_and_route(nc, io, keep):
    with ExitStack() as ctx:
        m = Pool(nc, ctx)
        y, h2h, h2l, w8 = keep.y, keep.h2h, keep.h2l, keep.w8
        weh, wel = keep.wh[0], keep.wl[0]
        ident = m.sb("jr_ident", [P, P])
        wo = m.sb("jr_wo", [P, KC, C])
        woh = m.sb("jr_woh", [P, KC, C], F32R)
        wol = m.sb("jr_wol", [P, KC, C], F32R)
        wr = m.sb("jr_wr", [P, KC, E])
        wrh = m.sb("jr_wrh", [P, KC, E], F32R)
        wrl = m.sb("jr_wrl", [P, KC, E], F32R)
        ln2 = m.sb("jr_ln2", [P, KC])
        raw = m.sb("jr_raw", [P, EW])
        rank = m.sb("jr_rank", [P, E])
        ya = [m.sb(f"jr_ya{b}", [P, TPC, C]) for b in range(2)]
        ah = [m.sb(f"jr_ah{b}", [P, KC, CH], F32R) for b in range(2)]
        al = [m.sb(f"jr_al{b}", [P, KC, CH], F32R) for b in range(2)]
        hn = [m.sb(f"jr_hn{b}", [P, TPC, C]) for b in range(2)]
        junk = m.sb("jr_junk", [P, TPC, C])
        sq = m.sb("jr_sq", [P, NT])
        var = m.sb("jr_var", [P, NT])
        root = m.sb("jr_root", [P, NT])
        r2 = m.sb("jr_r2", [P, NT])
        tmp = m.sb("jr_tmp", [P, NT])
        lt = m.sb("jr_lt", [E, 2, CH])
        lg = m.sb("jr_lg", [P, NT, E])
        one = m.sb("jr_one", [P, NT])
        first = m.sb("jr_first", [P, NT, E])
        pick = m.sb("jr_pick", [P, NT, E])
        top = m.sb("jr_top", [P, NT])
        ps_t = [[m.bank(f"jr_ps_t{b}{k}") for k in range(KC)] for b in range(2)]
        ps_y = [m.bank(f"jr_ps_y{b}") for b in range(2)]
        ps_l = m.bank("jr_ps_l")
        ps_g = m.bank("jr_ps_g")
        loaded = m.sem("jr_loaded")
        expert_in = m.sem("jr_expert_in")
        expert_high = m.sem("jr_expert_high")
        expert_low = m.sem("jr_expert_low")
        ya_in = [m.sem(f"jr_ya_in{b}") for b in range(2)]
        high_done = m.sem("jr_high_done")
        low_done = m.sem("jr_low_done")
        ya_turned = m.sem("jr_ya_turned")
        ah_done = m.sem("jr_ah_done")
        al_done = m.sem("jr_al_done")
        joined = m.sem("jr_joined")
        y2_done = m.sem("jr_y2_done")
        sq_done = m.sem("jr_sq_done")
        ms_done = m.sem("jr_ms_done")
        root_done = m.sem("jr_root_done")
        steps = m.sem("jr_steps")
        hn_done = m.sem("jr_hn_done")
        hn_turned = m.sem("jr_hn_turned")
        h2h_done = m.sem("jr_h2h_done")
        h2l_done = m.sem("jr_h2l_done")
        scored = m.sem("jr_scored")
        lt_kept = m.sem("jr_lt_kept")
        lt_turned = m.sem("jr_lt_turned")
        lg_kept = m.sem("jr_lg_kept")
        shifted = m.sem("jr_shifted")
        exps_done = m.sem("jr_exps_done")
        x1_in = [m.sem(f"jr_x1_in{b}") for b in range(2)]
        x1_added = m.sem("jr_x1_added")
        block = ctx.enter_context(nc.Block())
        LOADS = 5

        @block.sync
        def _(sp):
            sp.dma_start(wo[:], io["w_o"].rearrange("(k p) o -> p k o", p=P)).then_inc(loaded, 16)
            sp.dma_start(ident[:], io["ident"]).then_inc(loaded, 16)
            sp.dma_start(wr[:], io["w_r"].rearrange("(k p) o -> p k o", p=P)).then_inc(loaded, 16)
            sp.dma_start(ln2[:], io["ln2"]).then_inc(loaded, 16)
            sp.dma_start(rank[:], io["rank"]).then_inc(loaded, 16)
            with sp.Fori(0, NC // 2) as i:
                for b in range(2):
                    sp.wait_ge(ya_turned, i * 2 + b)
                    sp.dma_start(ya[b][:], io["ya"][bass.ds((i * 2 + b) * CH, CH), :].rearrange("(t p) f -> p t f", p=P)).then_inc(ya_in[b], 16)
            sp.dma_start(raw[:].rearrange("p (c w) -> p c w", c=NC), io["w_experts"][0:NC].rearrange("c p w -> p c w")).then_inc(expert_in, 16)
            for c in range(NC):
                if c < 2:
                    sp.wait_ge(ya_turned, NC - 1 + c)
                else:
                    sp.wait_ge(x1_added, c - 1)
                sp.dma_start(ya[c % 2][:], io["x1"][c * CH:(c + 1) * CH, :].rearrange("(t p) f -> p t f", p=P)).then_inc(x1_in[c % 2], 16)

        @block.gpsimd
        def _(pool):
            for c in range(NC):
                tiles = slice(c * TPC, (c + 1) * TPC)
                pool.wait_ge(x1_in[c % 2], 16 * (c // 2 + 1))
                pool.wait_ge(hn_turned, c + 1)
                pool.tensor_tensor(y[:, tiles, :], y[:, tiles, :], ya[c % 2][:], ALU.add).then_inc(x1_added, 1)

        @block.tensor
        def _(pe):
            pe.wait_ge(loaded, 16 * LOADS)
            pe.wait_ge(high_done, 2)
            pe.wait_ge(low_done, 2)
            with pe.Fori(0, NC // 2) as i:
                for b in range(2):
                    pe.wait_ge(ya_in[b], i * 16 + 16)
                    pe.wait_ge(al_done, i * 2 + b)
                    for k in range(KC):
                        for it in range(TPC):
                            last = pe.transpose(ps_t[b][k][:, it * P:(it + 1) * P], ya[b][:, it, k * P:(k + 1) * P], ident[:])
                    last.then_inc(ya_turned, 1)
                for b in range(2):
                    pe.wait_ge(ah_done, i * 2 + (b + 1))
                    pe.wait_ge(al_done, i * 2 + (b + 1))
                    for half in range(2):
                        pe.wait_ge(y2_done, i * 4 + max(0, 2 * b + half - 1))
                        for j in range(2):
                            tok = slice((2 * half + j) * P, (2 * half + j + 1) * P)
                            last = products(pe, ps_y[half][:, j * C:(j + 1) * C], [(ah[b][:, k, tok], al[b][:, k, tok]) for k in range(KC)],
                                            [(woh[:, k, :], wol[:, k, :]) for k in range(KC)])
                        last.then_inc(joined, 1)
            def score(c):
                pe.wait_ge(h2h_done, c + 1)
                pe.wait_ge(h2l_done, c + 1)
                if c > 0:
                    pe.wait_ge(lt_kept, c)
                at = slice(c * CH, (c + 1) * CH)
                products(pe, ps_l[0:E, :], [(wrh[:, k, :], wrl[:, k, :]) for k in range(KC)],
                         [(h2h[:, k, at], h2l[:, k, at]) for k in range(KC)]).then_inc(scored, 1)
            def turn_scores(c):
                pe.wait_ge(lt_kept, c + 1)
                if c > 0:
                    pe.wait_ge(lg_kept, c)
                for it in range(TPC):
                    last = pe.transpose(ps_g[:, it * E:(it + 1) * E], lt[:, c % 2, it * P:(it + 1) * P], ident[0:E, 0:E])
                last.then_inc(lt_turned, 1)
            for c in range(NC + 2):
                if c < NC:
                    b = c % 2
                    pe.wait_ge(hn_done, c + 1)
                    if c >= 2:
                        pe.wait_ge(h2h_done, c - 1)
                        pe.wait_ge(h2l_done, c - 1)
                    for k in range(KC):
                        for it in range(TPC):
                            last = pe.transpose(ps_t[b][k][:, it * P:(it + 1) * P],
                                                hn[b][:, it, k * P:(k + 1) * P], ident[:])
                    last.then_inc(hn_turned, 1)
                if c >= 2:
                    turn_scores(c - 2)
                if 1 <= c <= NC:
                    score(c - 1)

        @block.scalar
        def _(act):
            act.wait_ge(loaded, 16 * LOADS)
            act.activation(woh[:], wo[:], ACT.Copy).then_inc(high_done, 1)
            act.activation(wrh[:], wr[:], ACT.Copy).then_inc(high_done, 1)
            with act.Fori(0, NC // 2) as i:
                for b in range(2):
                    act.wait_ge(ya_turned, i * 2 + (b + 1))
                    act.wait_ge(joined, i * 4)
                    for k in range(KC):
                        last = act.activation(ah[b][:, k, :], ps_t[b][k][:], ACT.Copy)
                    last.then_inc(ah_done, 1)
                for q in range(4):
                    act.wait_ge(y2_done, i * 4 + (q + 1))
                    act.wait_ge(sq_done, i * 4 + q)
                    for j in range(2):
                        t = i * 8 + (2 * q + j)
                        last = act.activation(junk[:, j:j + 1, :], y[:, bass.ds(t, 1), :], ACT.Square, accum_out=sq[:, bass.ds(t, 1)])
                    last.then_inc(sq_done, 1)
            act.wait_ge(ms_done, 1)
            act.activation(root[:], var[:], ACT.Sqrt).then_inc(root_done, 1)
            for c in range(NC):
                b = c % 2
                at = slice(c * CH, (c + 1) * CH)
                act.wait_ge(hn_turned, c + 1)
                for k in range(KC):
                    last = act.activation(h2h[:, k, at], ps_t[b][k][:], ACT.Copy, scale=ln2[:, k:k + 1])
                last.then_inc(h2h_done, 1)
                act.wait_ge(scored, c + 1)
                if c >= 2:
                    act.wait_ge(lt_turned, c - 1)
                act.activation(lt[:, b, :], ps_l[0:E, :], ACT.Copy).then_inc(lt_kept, 1)
            act.wait_ge(expert_in, 16)
            act.activation(weh[:], raw[:], ACT.Copy).then_inc(expert_high, 1)
            act.wait_ge(shifted, 1)
            act.activation(lg[:], lg[:], ACT.Exp).then_inc(exps_done, 1)

        @block.vector
        def _(dve):
            chain = Chain(dve, steps)
            dve.wait_ge(high_done, 2)
            dve.tensor_tensor(wol[:], wo[:], woh[:].bitcast(F32), ALU.subtract).then_inc(low_done, 1)
            dve.tensor_tensor(wrl[:], wr[:], wrh[:].bitcast(F32), ALU.subtract).then_inc(low_done, 1)
            with dve.Fori(0, NC // 2) as i:
                for b in range(2):
                    dve.wait_ge(ah_done, i * 2 + (b + 1))
                    for k in range(KC):
                        last = dve.tensor_tensor(al[b][:, k, :], ps_t[b][k][:], ah[b][:, k, :].bitcast(F32), ALU.subtract)
                    last.then_inc(al_done, 1)
                for q in range(4):
                    dve.wait_ge(joined, i * 4 + (q + 1))
                    yt = y[:, bass.ds(i * 8 + 2 * q, 2), :]
                    dve.tensor_tensor(yt, yt, ps_y[q % 2][:].rearrange("p (t f) -> p t f", t=2), ALU.add).then_inc(y2_done, 1)
            dve.wait_ge(sq_done, NT // 2)
            dve.tensor_scalar(var[:], sq[:], 1.0 / C, 1e-6, ALU.mult, ALU.add).then_inc(ms_done, 1)
            inverse_root(chain, var[:], root[:], r2[:], tmp[:], root_done, 1)
            def normalise(c):
                tiles = slice(c * TPC, (c + 1) * TPC)
                if c >= 2:
                    dve.wait_ge(hn_turned, c - 1)
                dve.tensor_tensor(hn[c % 2][:], y[:, tiles, :], spread(r2[:, tiles], 2, C), ALU.mult).then_inc(hn_done, 1)
            def keep_scores(c):
                dve.wait_ge(lt_turned, c + 1)
                dve.tensor_copy(lg[:, c * TPC:(c + 1) * TPC, :], ps_g[:, 0:TPC * E].rearrange("p (t e) -> p t e", e=E)).then_inc(lg_kept, 1)
            normalise(0)
            for c in range(NC):
                if c + 1 < NC:
                    normalise(c + 1)
                dve.wait_ge(h2h_done, c + 1)
                at = slice(c * CH, (c + 1) * CH)
                for k in range(KC):
                    last = dve.scalar_tensor_tensor(h2l[:, k, at], ps_t[c % 2][k][:], ln2[:, k:k + 1], h2h[:, k, at].bitcast(F32),
                                                    ALU.mult, ALU.subtract)
                last.then_inc(h2l_done, 1)
                if c >= 2:
                    keep_scores(c - 2)
            keep_scores(NC - 2)
            keep_scores(NC - 1)
            dve.wait_ge(expert_high, 1)
            dve.tensor_tensor(wel[:], raw[:], weh[:].bitcast(F32), ALU.subtract).then_inc(expert_low, 1)
            dve.wait_ge(lg_kept, NC)
            chain.step(dve.tensor_reduce(one[:], lg[:], AX.X, ALU.max))
            dve.tensor_tensor(lg[:], lg[:], spread(one[:], 2, E), ALU.subtract).then_inc(shifted, 1)
            dve.wait_ge(exps_done, 1)
            chain.step(dve.tensor_reduce(one[:], lg[:], AX.X, ALU.add))
            chain.step(dve.reciprocal(one[:], one[:]))
            chain.step(dve.tensor_tensor(lg[:], lg[:], spread(one[:], 2, E), ALU.mult))
            def choose(out):
                chain.step(dve.tensor_reduce(top[:], w8[:], AX.X, ALU.max))
                chain.step(dve.tensor_tensor(pick[:], w8[:], spread(top[:], 2, E), ALU.is_equal))
                chain.step(dve.tensor_tensor(pick[:], pick[:], spread(rank[:], 1, NT), ALU.mult))
                chain.step(dve.tensor_reduce(one[:], pick[:], AX.X, ALU.max))
                chain.step(dve.tensor_tensor(out[:], spread(one[:], 2, E), spread(rank[:], 1, NT), ALU.is_equal))
            chain.step(dve.tensor_copy(w8[:], lg[:]))
            choose(first)
            chain.step(dve.scalar_tensor_tensor(w8[:], first[:], -2.0, w8[:], ALU.mult, ALU.add))
            choose(pick)
            chain.step(dve.tensor_tensor(pick[:], pick[:], first[:], ALU.add))
            chain.step(dve.tensor_tensor(w8[:], lg[:], pick[:], ALU.mult))
            chain.step(dve.tensor_reduce(one[:], w8[:], AX.X, ALU.add))
            chain.step(dve.tensor_scalar(one[:], one[:], 1e-9, None, ALU.add))
            chain.step(dve.reciprocal(one[:], one[:]))
            chain.step(dve.tensor_tensor(w8[:], w8[:], spread(one[:], 2, E), ALU.mult))


def experts(nc, io, keep):
    PIECE = EW // NC
    with ExitStack() as ctx:
        m = Pool(nc, ctx)
        y, w8 = keep.y, keep.w8
        raw = m.sb("ex_raw", [P, PIECE])
        act_s = [m.sb(f"ex_silu{b}", [P, CH]) for b in range(2)]
        prod = [m.sb(f"ex_prod{b}", [P, CH]) for b in range(2)]
        ph = [m.sb(f"ex_ph{b}", [P, CH], F32R) for b in range(3)]
        pl = [m.sb(f"ex_pl{b}", [P, CH], F32R) for b in range(3)]
        ps_g = [m.bank(f"ex_ps_g{b}") for b in range(2)]
        ps_u = [m.bank(f"ex_ps_u{b}") for b in range(2)]
        ps_o = [m.bank(f"ex_ps_o{b}") for b in range(TPC)]
        expert_in = m.sem("ex_expert_in")
        high_split = m.sem("ex_high_split")
        low_split = m.sem("ex_low_split")
        up_done = m.sem("ex_up_done")
        silu_done = m.sem("ex_silu_done")
        prod_done = m.sem("ex_prod_done")
        ph_done = m.sem("ex_ph_done")
        pl_done = m.sem("ex_pl_done")
        used = m.sem("ex_used")
        added = m.sem("ex_added")
        stored = m.sem("ex_stored")
        block = ctx.enter_context(nc.Block())
        assert MT % 2 == 0 and MT % 3 == 0

        def rows_of(mt):
            return P if mt < MF else MR

        def run_chunks(eng, pair, last_pair, chunk):
            for b in range(2):
                e = pair * 2 + b
                with eng.Fori(0, NC - 1) as c:
                    chunk(e, b, c, False, last_pair and b == 1)
                chunk(e, b, NC - 1, True, last_pair and b == 1)

        def run(eng, chunk):
            with eng.Fori(0, E // 2 - 1) as pair:
                run_chunks(eng, pair, False, chunk)
            run_chunks(eng, E // 2 - 1, True, chunk)

        @block.sync
        def _(sp):
            with sp.Fori(0, (E - 1) * NC) as p:
                sp.wait_ge(low_split, p)
                sp.dma_start(raw[:], io["w_experts"][bass.ds(p + NC, 1)].rearrange("o p w -> p (o w)")).then_inc(expert_in, 16)
            with sp.Fori(0, NC) as c:
                sp.wait_ge(added, c * TPC + ((E - 1) * NC * TPC + TPC))
                sp.dma_start(io["out"][bass.ds(c * CH, CH), :].rearrange("(t p) f -> p t f", p=P), y[:, bass.ds(c * TPC, TPC), :]).then_inc(stored, 16)
            sp.wait_ge(stored, 16 * NC)

        @block.tensor
        def _(pe):
            def up(e, b, c, mt):
                step = (e * NC + c) * MT + mt
                rhs = [(keep.h2h[:, k, bass.ds(c * CH, CH)], keep.h2l[:, k, bass.ds(c * CH, CH)]) for k in range(KC)]
                if mt < MF:
                    parts = ((ps_g[mt % 2][:], mt * 2 * P, P), (ps_u[mt % 2][:], (mt * 2 + 1) * P, P))
                else:
                    parts = ((ps_g[mt % 2][0:64 + MR, :], mt * 2 * P, 64 + MR),)
                for out, at, cols in parts:
                    last = products(pe, out, [(keep.wh[b][:, k * UPW + at:k * UPW + at + cols],
                                               keep.wl[b][:, k * UPW + at:k * UPW + at + cols]) for k in range(KC)], rhs)
                last.then_inc(up_done, 1)

            def down(e, b, c, mt):
                rows = rows_of(mt)
                at = KC * UPW + mt * C
                for it in range(TPC):
                    tok = slice(it * P, (it + 1) * P)
                    last = products(pe, ps_o[it][:, 0:C], [(ph[mt % 3][0:rows, tok], pl[mt % 3][0:rows, tok])],
                                    [(keep.wh[b][0:rows, at:at + C], keep.wl[b][0:rows, at:at + C])], start=mt == 0, stop=mt == MT - 1)
                last.then_inc(used, 1)

            def chunk(e, b, c, last_chunk, last_expert):
                ec = e * NC + c
                for mt in range(MT):
                    if mt + 1 < MT or not (last_chunk and last_expert):
                        if last_chunk and mt + 1 == MT:
                            pe.wait_ge(low_split, e * NC + NC)
                        pe.wait_ge(prod_done, ec * MT + mt)
                        if mt + 1 < MT:
                            up(e, b, c, mt + 1)
                        elif last_chunk:
                            up(e + 1, 1 - b, 0, 0)
                        else:
                            up(e, b, c + 1, 0)
                    if mt == 0:
                        pe.wait_ge(added, ec * TPC)
                    pe.wait_ge(pl_done, ec * MT + (mt + 1))
                    down(e, b, c, mt)

            up(0, 0, 0, 0)
            run(pe, chunk)

        @block.scalar
        def _(act):
            def hidden(base, mt):
                act.wait_ge(up_done, base + (mt + 1))
                if mt < MF:
                    act.activation(act_s[mt % 2][:], ps_g[mt % 2][:], ACT.Silu).then_inc(silu_done, 1)
                else:
                    act.activation(act_s[mt % 2][64:64 + MR, :], ps_g[mt % 2][0:MR, :], ACT.Silu).then_inc(silu_done, 1)
                act.wait_ge(prod_done, base + (mt + 1))
                rows = rows_of(mt)
                act.activation(ph[mt % 3][0:rows, :], prod[mt % 2][0:rows, :], ACT.Copy).then_inc(ph_done, 1)

            def chunk(e, b, c, last_chunk, last_expert):
                base = (e * NC + c) * MT
                for mt in range(1, MT):
                    hidden(base, mt)
                    if mt == MT - 2 and not last_expert:
                        at = bass.ds(c * PIECE, PIECE)
                        act.wait_ge(used, e * (NC * MT))
                        act.wait_ge(expert_in, e * (16 * NC) + (c * 16 + 16))
                        act.activation(keep.wh[1 - b][:, at], raw[:], ACT.Copy).then_inc(high_split, 1)
                if not (last_chunk and last_expert):
                    hidden(base + MT, 0)

            hidden(0, 0)
            run(act, chunk)

        @block.vector
        def _(dve):
            def hidden(base, mt):
                dve.wait_ge(silu_done, base + (mt + 1))
                rows = rows_of(mt)
                if mt < MF:
                    dve.tensor_tensor(prod[mt % 2][:], act_s[mt % 2][:], ps_u[mt % 2][:], ALU.mult).then_inc(prod_done, 1)
                else:
                    dve.tensor_tensor(prod[mt % 2][0:MR, :], act_s[mt % 2][64:64 + MR, :], ps_g[mt % 2][64:64 + MR, :],
                                      ALU.mult).then_inc(prod_done, 1)
                dve.wait_ge(ph_done, base + (mt + 1))
                dve.tensor_tensor(pl[mt % 3][0:rows, :], prod[mt % 2][0:rows, :], ph[mt % 3][0:rows, :].bitcast(F32),
                                  ALU.subtract).then_inc(pl_done, 1)

            def add(e, c):
                dve.wait_ge(used, (e * NC + c) * MT + MT)
                for it in range(TPC):
                    yt = y[:, bass.ds(c * TPC + it, 1), :].rearrange("p t f -> p (t f)")
                    by = w8[:, bass.ds(c * TPC + it, 1), bass.ds(e, 1)].rearrange("p t e -> p (t e)")
                    dve.scalar_tensor_tensor(yt, ps_o[it][:, 0:C], by, yt, ALU.mult, ALU.add).then_inc(added, 1)

            def chunk(e, b, c, last_chunk, last_expert):
                base = (e * NC + c) * MT
                for mt in range(1, MT):
                    hidden(base, mt)
                    if mt == MT - 2 and not last_expert:
                        at = bass.ds(c * PIECE, PIECE)
                        dve.wait_ge(high_split, e * NC + (c + 1))
                        dve.tensor_tensor(keep.wl[1 - b][:, at], raw[:], keep.wh[1 - b][:, at].bitcast(F32),
                                          ALU.subtract).then_inc(low_split, 1)
                if not (last_chunk and last_expert):
                    hidden(base + MT, 0)
                add(e, c)

            hidden(0, 0)
            run(dve, chunk)


class Keep:
    pass


def scratch(nc, io):
    for name, shape in (("s1_rows", [H, N]), ("x1", [N, C]), ("q_high", [C, N]), ("q_low", [C, N]), ("k_high", [KV * D, N]),
                        ("k_low", [KV * D, N]), ("va", [KV, P, NT, VW]), ("ya", [N, C])):
        if name not in io:
            io[name] = nc.dram_tensor(name, shape, F32, kind="Internal").ap()


def build(nc, io):
    scratch(nc, io)
    keep = Keep()
    with ExitStack() as ctx:
        g = Pool(nc, ctx)
        keep.s1 = g.sb("s1", [P, NT, H])
        keep.s2 = g.sb("s2", [P, NT, H])
        keep.e1 = g.sb("e1", [P, NT, H])
        keep.f1 = g.sb("f1", [P, NT, H])
        keep.mean = g.sb("mean_wh", [P, C])
        keep.ge = g.sb("ge", [P, NT * H, GW], BF16)
        keep.gf = g.sb("gf", [P, NT * H, GW], BF16)
        graph_prepare(nc, io, keep)
        graph_attention(nc, io, keep)
    keep = Keep()
    with ExitStack() as ctx:
        g = Pool(nc, ctx)
        keep.y = g.sb("y", [P, NT, C])
        project_qkv(nc, io, keep)
        sequence_attention(nc, io, keep)
        keep.h2h = g.sb("h2_high", [P, KC, N], F32R)
        keep.h2l = g.sb("h2_low", [P, KC, N], F32R)
        keep.w8 = g.sb("expert_weights", [P, NT, E])
        keep.wh = [g.sb("experts_high0", [P, EW], F32R)]
        keep.wl = [g.sb("experts_low0", [P, EW], F32R)]
        join_and_route(nc, io, keep)
        keep.wh.append(g.sb("experts_high1", [P, EW], F32R))
        keep.wl.append(g.sb("experts_low1", [P, EW], F32R))
        experts(nc, io, keep)


def lay_out(inputs):
    def given(name):
        return np.asarray(inputs[name])

    def turned(w):
        return w.reshape(C, -1, 2, D // 2)[:, :, ::-1, :].reshape(C, -1)

    w, a = given("L0_gnn_W"), given("L0_gnn_a")
    wq, wk, wv = (given("L0_ffn_" + n).T for n in ("wq", "wk", "wv"))
    w1, w2, w3 = (given("L0_ffn_" + n) for n in ("w1", "w2", "w3"))
    pieces = []
    for j in range(2):
        pieces += [wq[:, j * P:(j + 1) * P], turned(wq[:, j * P:(j + 1) * P])]
    pieces += [wk, turned(wk), wv]
    up = np.zeros((E, C, UPW), w1.dtype)
    for t in range(MF):
        rows = slice(t * P, (t + 1) * P)
        up[:, :, 2 * t * P:(2 * t + 1) * P] = w1[:, rows].transpose(0, 2, 1)
        up[:, :, (2 * t + 1) * P:(2 * t + 2) * P] = w3[:, rows].transpose(0, 2, 1)
    up[:, :, 2 * MF * P:2 * MF * P + MR] = w1[:, MF * P:].transpose(0, 2, 1)
    up[:, :, 2 * MF * P + 64:] = w3[:, MF * P:].transpose(0, 2, 1)
    down = np.zeros((E, MT * P, C), w2.dtype)
    down[:, :HID] = w2.transpose(0, 2, 1)
    w_experts = np.zeros((E, P, EW), w1.dtype)
    for k in range(KC):
        w_experts[:, :, k * UPW:(k + 1) * UPW] = up[:, k * P:(k + 1) * P]
    w_experts[:, :, KC * UPW:KC * UPW + MT * C] = down.reshape(E, MT, P, C).transpose(0, 2, 1, 3).reshape(E, P, MT * C)
    inv_freq = 1.0 / 10000.0 ** (np.arange(0, D, 2, dtype=np.float32) / D)
    freqs = np.outer(np.arange(N, dtype=np.float32), inv_freq)
    emb = np.concatenate([freqs, freqs], axis=-1)
    cos, sin = np.cos(emb).T, np.sin(emb).T
    sin = np.concatenate([-sin[:D // 2], sin[D // 2:]])
    trig = np.stack([np.tile(cos, (P // D, 1)), np.tile(sin, (P // D, 1))], axis=1).astype(np.float32)
    row = np.arange(P)
    arrays = {
        "x": given("x"),
        "adj": given("adj"),
        "w_cat": w.transpose(1, 0, 2).reshape(C, C),
        "w_t": w.transpose(0, 2, 1),
        "a_t": a.reshape(H, 2, D).transpose(2, 0, 1).reshape(D, 2 * H),
        "w_qkv": np.concatenate(pieces, axis=1),
        "ln1": given("L0_ffn_ln1_w").reshape(KC, P).T,
        "ln2": given("L0_ffn_ln2_w").reshape(KC, P).T,
        "w_o": given("L0_ffn_wo").T,
        "w_r": given("L0_ffn_router_w").T,
        "w_experts": w_experts.reshape(E, P, NC, EW // NC).transpose(0, 2, 1, 3).reshape(E * NC, P, EW // NC),
        "ident": np.eye(P, dtype=np.float32),
        "mean_of": np.full((P, P), 1.0 / N, np.float32),
        "sel": np.eye(DA, dtype=np.float32)[np.arange(GW) % DA],
        "trig": trig,
        "late_k": np.where(row[None, :] > row[:, None], -1e30, 0.0).astype(np.float32),
        "late_q": np.where(row[None, :] < row[:, None], -1e30, 0.0).astype(np.float32),
        "rank": np.tile(E - np.arange(E, dtype=np.float32), (P, 1)),
    }
    return {name: np.ascontiguousarray(value) for name, value in arrays.items()}


def kernel(**inputs):
    import concourse.bacc as bacc
    from concourse.bass_utils import run_bass_kernel_spmd

    nc = bacc.Bacc("TRN2", target_bir_lowering=False, num_devices=1)
    arrays = lay_out(inputs)
    io = {name: nc.dram_tensor(name, a.shape, mybir.dt.from_np(a.dtype), kind="ExternalInput").ap() for name, a in arrays.items()}
    io["out"] = nc.dram_tensor("out", [N, C], F32, kind="ExternalOutput").ap()
    build(nc, io)
    return run_bass_kernel_spmd(nc, [arrays], core_ids=[0]).results[0]["out"]
```

```python
from contextlib import ExitStack

import numpy as np

import concourse.bass as bass
from concourse import mybir

P = 128
N = 4096
C = 256
KC = C // P
NT = N // P
CH = 512
NC = N // CH
TPC = CH // P
H = 4
D = C // H
DA = D + 1
PARTS = 3
GW = PARTS * DA
GREST = GW - P
KV = 2
VW = 2 * (D + 1)
QKW = 6 * P
E = 8
HID = 682
MF = HID // P
MR = HID - MF * P
UPW = MF * 2 * P + 64 + MR
MT = MF + 1
PIECES = MT - 1
EW = (KC * UPW + MT * C + PIECES - 1) // PIECES * PIECES
SLOTS = 2 * N // CH + E - 1
RANK = slice(0, E)
EDGES = slice(E, E + NC)
UPTO = slice(E + NC, E + NC + E * E)
SLOT = slice(E + NC + E * E, E + NC + E * E + SLOTS)
ROW = slice(E + NC + E * E + SLOTS, E + NC + E * E + SLOTS + 1)
PLAN_COLS = ROW.stop
SLOPE = 0.2

ALU = mybir.AluOpType
ACT = mybir.ActivationFunctionType
AX = mybir.AxisListType
F32 = mybir.dt.float32
BF16 = mybir.dt.bfloat16
U32 = mybir.dt.uint32
F32R = mybir.dt.float32r


class Pool:

    def __init__(self, nc, ctx):
        self.nc, self.ctx, self.sems = nc, ctx, []

    def sb(self, name, shape, dt=F32):
        return self.ctx.enter_context(self.nc.sbuf_tensor(name, shape, dt))

    def bank(self, name, dt=F32, banks=1):
        cols = banks * (512 if dt == F32 else 1024)
        return self.ctx.enter_context(self.nc.psum_tensor(name, [P, cols], dt))

    def sem(self, name):
        if not self.sems:
            self.ctx.callback(self.clear)
        self.sems.append(self.nc.alloc_semaphore(name=name))
        return self.sems[-1]

    def clear(self):
        self.nc.clear_and_free_semaphores(self.sems)
        self.nc.all_engine_barrier()


class Chain:

    def __init__(self, eng, sem):
        self.eng, self.sem, self.base, self.n = eng, sem, 0, 0

    def at(self, base):
        self.base, self.n = base, 0

    def step(self, ins):
        self.n += 1
        ins.then_inc(self.sem, 1)
        self.eng.wait_ge(self.sem, self.base + self.n)


def spread(ap, axis, count):
    ap = ap.unsqueeze(axis)
    shape = list(ap.shape)
    shape[axis] = count
    return ap.to_broadcast(shape)


def inverse_root(chain, v, root, y, t, roots_out, n):
    chain.eng.wait_ge(roots_out, n)
    chain.step(chain.eng.reciprocal(y, root))
    chain.step(chain.eng.tensor_tensor(t, y, y, ALU.mult))
    chain.step(chain.eng.tensor_tensor(t, t, v, ALU.mult))
    chain.step(chain.eng.tensor_scalar(t, t, -0.5, 1.5, ALU.mult, ALU.add))
    chain.step(chain.eng.tensor_tensor(y, y, t, ALU.mult))


def graph_prepare(nc, io, keep):
    with ExitStack() as ctx:
        m = Pool(nc, ctx)
        x = m.sb("gp_x", [P, NT, C])
        w = m.sb("gp_w", [P, KC, C + 2 * H])
        w_t = m.sb("gp_wt", [D, H, C])
        a_t = m.sb("gp_a", [D, 2 * H])
        ident = m.sb("gp_ident", [P, P])
        mean_of = m.sb("gp_ones", [P, P])
        st = m.sb("gp_stats", [P, NT, 6])
        mu = m.sb("gp_mu", [P, NT])
        var = m.sb("gp_var", [P, NT])
        tmp = m.sb("gp_tmp", [P, NT])
        root = m.sb("gp_root", [P, NT])
        rstd = m.sb("gp_rstd", [P, NT])
        xn = m.sb("gp_xn", [P, 2, C])
        xt = m.sb("gp_xt", [P, 2, KC, P])
        wh = m.sb("gp_wh", [P, NT, H, DA])
        rows = m.sb("gp_rows", [H, N])
        cm = m.sb("gp_cmax", [P, H])
        ca = m.sb("gp_call", [P, H])
        s2, s1 = keep.s2, keep.s1
        e2 = m.sb("gp_e2", [P, NT, H])
        f2 = m.sb("gp_f2", [P, NT, H])
        d2 = m.sb("gp_d2", [P, NT, H])
        u = m.sb("gp_u", [P, NT, H])
        u2 = m.sb("gp_u2", [P, NT, H])
        um = m.sb("gp_um", [P, NT, H])
        val = m.sb("gp_val", [P, 2, TPC * H, DA])
        ps_t = [m.bank(f"gp_ps_t{b}") for b in range(2)]
        ps_w = [m.bank(f"gp_ps_w{b}") for b in range(2)]
        ps_r = [m.bank(f"gp_ps_r{b}") for b in range(2)]
        ps_m = m.bank("gp_ps_m")

        loaded = m.sem("gp_loaded")
        wa_done = m.sem("gp_wa_done")
        wa_kept = m.sem("gp_wa_kept")
        dve_steps = m.sem("gp_dve_steps")
        set_up = m.sem("gp_set_up")
        stats_done = m.sem("gp_stats_done")
        var_done = m.sem("gp_var_done")
        root_done = m.sem("gp_root_done")
        xn_done = m.sem("gp_xn_done")
        xn_turned = m.sem("gp_xn_turned")
        xt_kept = m.sem("gp_xt_kept")
        wh_done = m.sem("gp_wh_done")
        rows_done = m.sem("gp_rows_done")
        wh_kept = m.sem("gp_wh_kept")
        rows_kept = m.sem("gp_rows_kept")
        scores_kept = m.sem("gp_scores_kept")
        summed = m.sem("gp_summed")
        mean_kept = m.sem("gp_mean_kept")
        max_done = m.sem("gp_max_done")
        all_max = m.sem("gp_all_max")
        exps_in = m.sem("gp_exps_in")
        exps_done = m.sem("gp_exps_done")
        val_done = m.sem("gp_val_done")
        hi_done = m.sem("gp_hi_done")
        rest_done = m.sem("gp_rest_done")
        mid_done = m.sem("gp_mid_done")
        lo_done = m.sem("gp_lo_done")
        stored = m.sem("gp_stored")
        block = ctx.enter_context(nc.Block())
        LOADS = 9

        @block.sync
        def _(sp):
            for q in range(4):
                sp.dma_start(x[:, 8 * q:8 * q + 8, :], io["x"].rearrange("(t p) f -> p t f", p=P)[:, 8 * q:8 * q + 8, :]).then_inc(loaded, 16)
            sp.dma_start(w[:, :, 0:C], io["w_cat"].rearrange("(k p) o -> p k o", p=P)).then_inc(loaded, 16)
            sp.dma_start(w_t[:], io["w_t"].rearrange("h o f -> o h f")).then_inc(loaded, 16)
            sp.dma_start(a_t[:], io["a_t"]).then_inc(loaded, 16)
            sp.dma_start(ident[:], io["ident"]).then_inc(loaded, 16)
            sp.dma_start(mean_of[:], io["mean_of"]).then_inc(loaded, 16)
            sp.wait_ge(rows_kept, NT)
            sp.dma_start(io["s1_rows"], rows[:]).then_inc(stored, 16)
            sp.wait_ge(stored, 16)

        @block.tensor
        def _(pe):
            pe.wait_ge(loaded, 16 * LOADS)
            for k in range(KC):
                for h in range(H):
                    for s in range(2):
                        col = k * 2 * H + (1 - s) * H + h
                        last = pe.matmul(ps_m[:, col:col + 1], w_t[:, h, k * P:(k + 1) * P],
                                         a_t[:, 2 * h + s:2 * h + s + 1], start=True, stop=True)
            last.then_inc(wa_done, 1)
            pe.wait_ge(wa_kept, 1)
            with pe.Fori(0, NT // 2) as i:
                for b in range(2):
                    pe.wait_ge(xn_done, i * 2 + (b + 1))
                    pe.wait_ge(xt_kept, i * 2 + b)
                    for k in range(KC):
                        last = pe.transpose(ps_t[b][:, k * P:(k + 1) * P], xn[:, b, k * P:(k + 1) * P], ident[:])
                    last.then_inc(xn_turned, 1)
                for b in range(2):
                    pe.wait_ge(xt_kept, i * 2 + (b + 1))
                    pe.wait_ge(wh_kept, i * 2 + b)
                    pe.wait_ge(scores_kept, i * 2 + b)
                    for k in range(KC):
                        last = pe.matmul(ps_w[b][:, 0:C + H * 2], xt[:, b, k, :], w[:, k, :], start=k == 0, stop=k == KC - 1)
                    last.then_inc(wh_done, 1)
                    pe.wait_ge(rows_kept, i * 2 + b)
                    for k in range(KC):
                        last = pe.matmul(ps_r[b][0:H, 0:P], w[:, k, C + H:C + 2 * H], xt[:, b, k, :], start=k == 0, stop=k == KC - 1)
                    last.then_inc(rows_done, 1)
            pe.wait_ge(wh_kept, NT)
            for t in range(NT):
                last = pe.matmul(ps_m[:, 0:C], mean_of[:], wh[:, t, :, 0:D], start=t == 0, stop=t == NT - 1)
            last.then_inc(summed, 1)

        @block.scalar
        def _(act):
            act.wait_ge(var_done, 1)
            act.activation(root[:], var[:], ACT.Sqrt).then_inc(root_done, 1)
            with act.Fori(0, NT // 2) as i:
                for b in range(2):
                    act.wait_ge(xn_turned, i * 2 + (b + 1))
                    act.wait_ge(rows_done, i * 2 + b)
                    act.activation(xt[:, b, :, :], ps_t[b][:, 0:C].rearrange("p (k n) -> p k n", k=KC), ACT.Copy).then_inc(xt_kept, 1)
                for b in range(2):
                    act.wait_ge(wh_done, i * 2 + (b + 1))
                    act.wait_ge(wh_kept, i * 2 + (b + 1))
                    act.activation(s2[:, bass.ds(i * 2 + b, 1), :], ps_w[b][:, C:C + H].unsqueeze(1), ACT.Copy)
                    act.activation(s1[:, bass.ds(i * 2 + b, 1), :], ps_w[b][:, C + H:C + 2 * H].unsqueeze(1), ACT.Copy).then_inc(scores_kept, 1)
                    act.wait_ge(rows_done, i * 2 + (b + 1))
                    act.activation(rows[:, bass.ds((i * 2 + b) * P, P)], ps_r[b][0:H, 0:P], ACT.Copy).then_inc(rows_kept, 1)
            act.wait_ge(exps_in, 1)
            act.activation(e2[:], d2[:], ACT.Exp).then_inc(exps_done, 1)
            act.activation(f2[:], d2[:], ACT.Exp, scale=SLOPE).then_inc(exps_done, 1)
            act.wait_ge(exps_in, 3)
            act.activation(keep.e1[:], u[:], ACT.Exp).then_inc(exps_done, 1)
            act.activation(keep.f1[:], u2[:], ACT.Exp).then_inc(exps_done, 1)
            with act.Fori(0, NC) as i:
                for b, g in enumerate((keep.ge, keep.gf)):
                    gv = g[:, bass.ds(i * TPC * H, TPC * H), :]
                    act.wait_ge(val_done, i * 2 + (b + 1))
                    act.activation(gv[:, :, 0:DA], val[:, b], ACT.Copy).then_inc(hi_done, 1)
                    act.wait_ge(rest_done, i * 2 + (b + 1))
                    act.activation(gv[:, :, DA:2 * DA], val[:, b], ACT.Copy).then_inc(mid_done, 1)

        @block.gpsimd
        def _(pool):
            pool.memset(wh[:, :, :, D:DA], 1.0).then_inc(set_up, 1)
            pool.wait_ge(max_done, 1)
            pool.partition_all_reduce(ca[:], cm[:], P, bass.bass_isa.ReduceOp.max).then_inc(all_max, 1)

        @block.vector
        def _(dve):
            chain = Chain(dve, dve_steps)
            dve.wait_ge(loaded, 16 * LOADS)
            dve.wait_ge(wa_done, 1)
            dve.tensor_copy(w[:, :, C:C + 2 * H], ps_m[:, 0:KC * 2 * H].rearrange("p (k c) -> p k c", k=KC)).then_inc(wa_kept, 1)
            with dve.Fori(0, NT // 4) as i:
                for b in range(4):
                    dve.bn_stats(st[:, bass.ds(i * 4 + b, 1), :].rearrange("p t s -> p (t s)"),
                                 x[:, bass.ds(i * 4 + b, 1), :].rearrange("p t s -> p (t s)")).then_inc(stats_done, 1)
            dve.wait_ge(stats_done, NT)
            layer_norm_tail(chain, st, mu, var, tmp, var_done)
            inverse_root(chain, var[:], root[:], rstd[:], tmp[:], root_done, 1)
            with dve.Fori(0, NT // 2) as i:
                for b in range(2):
                    t = i * 2 + b
                    dve.wait_ge(xn_turned, t)
                    dve.tensor_scalar(xn[:, b:b + 1, :], x[:, bass.ds(t, 1), :], mu[:, bass.ds(t, 1)], rstd[:, bass.ds(t, 1)],
                                      ALU.subtract, ALU.mult).then_inc(xn_done, 1)
                for b in range(2):
                    t = i * 2 + b
                    dve.wait_ge(wh_done, t + 1)
                    dve.tensor_copy(wh[:, bass.ds(t, 1), :, 0:D].rearrange("p t h d -> p (t h) d"),
                                    ps_w[b][:, 0:C].rearrange("p (h d) -> p h d", h=H)).then_inc(wh_kept, 1)
            dve.wait_ge(summed, 1)
            dve.tensor_copy(keep.mean[:], ps_m[:, 0:C]).then_inc(mean_kept, 1)
            dve.wait_ge(scores_kept, NT)
            dve.tensor_reduce(cm[:], s2[:].rearrange("p t h -> p h t"), AX.X, ALU.max).then_inc(max_done, 1)
            dve.wait_ge(all_max, 1)
            dve.tensor_tensor(d2[:], s2[:], spread(ca[:], 1, NT), ALU.subtract).then_inc(exps_in, 1)
            chain.step(dve.tensor_tensor(u[:], s1[:], spread(ca[:], 1, NT), ALU.add))
            chain.step(dve.scalar_tensor_tensor(um[:], u[:], SLOPE, u[:], ALU.mult, ALU.max))
            chain.step(dve.scalar_tensor_tensor(u2[:], u[:], SLOPE, um[:], ALU.mult, ALU.subtract))
            dve.tensor_tensor(u[:], u[:], um[:], ALU.subtract).then_inc(exps_in, 2)
            dve.wait_ge(exps_done, 2)
            dve.wait_ge(set_up, 1)
            with dve.Fori(0, NC) as i:
                whv = wh[:, bass.ds(i * TPC, TPC), :, :].rearrange("p t h d -> p (t h) d")
                for b, s in enumerate((e2, f2)):
                    dve.wait_ge(lo_done, i * 2)
                    dve.tensor_tensor(val[:, b], whv,
                                      spread(s[:, bass.ds(i * TPC, TPC), :].rearrange("p t h -> p (t h)"), 2, DA),
                                      ALU.mult).then_inc(val_done, 1)
                for b, g in enumerate((keep.ge, keep.gf)):
                    gv = g[:, bass.ds(i * TPC * H, TPC * H), :]
                    dve.wait_ge(val_done, i * 2 + 2)
                    dve.wait_ge(hi_done, i * 2 + (b + 1))
                    dve.tensor_tensor(val[:, b], val[:, b], gv[:, :, 0:DA], ALU.subtract).then_inc(rest_done, 1)
                for b, g in enumerate((keep.ge, keep.gf)):
                    gv = g[:, bass.ds(i * TPC * H, TPC * H), :]
                    dve.wait_ge(rest_done, i * 2 + 2)
                    dve.wait_ge(mid_done, i * 2 + (b + 1))
                    dve.tensor_tensor(gv[:, :, 2 * DA:3 * DA], val[:, b], gv[:, :, DA:2 * DA], ALU.subtract).then_inc(lo_done, 1)


def layer_norm_tail(chain, st, mu, var, tmp, var_done):
    dve = chain.eng
    chain.step(dve.tensor_tensor(mu[:], st[:, :, 1], st[:, :, 4], ALU.add))
    chain.step(dve.tensor_scalar(mu[:], mu[:], 0.5, None, ALU.mult))
    chain.step(dve.tensor_tensor(tmp[:], st[:, :, 1], st[:, :, 4], ALU.subtract))
    chain.step(dve.tensor_tensor(tmp[:], tmp[:], tmp[:], ALU.mult))
    chain.step(dve.tensor_tensor(var[:], st[:, :, 2], st[:, :, 5], ALU.add))
    chain.step(dve.tensor_scalar(var[:], var[:], 1.0 / C, 1e-5, ALU.mult, ALU.add))
    dve.scalar_tensor_tensor(var[:], tmp[:], 0.25, var[:], ALU.mult, ALU.add).then_inc(var_done, 1)


def graph_attention(nc, io, keep):
    QJ = N // 4
    NP2 = NT // 2
    USES = H * NP2 // 2
    with ExitStack() as ctx:
        m = Pool(nc, ctx)
        nat = m.sb("ga_nat", [P, 4, TPC, QJ], BF16)
        no_edge = m.sb("ga_no_edge", [P, NT, CH], BF16)
        identb = m.sb("ga_identb", [P, P], BF16)
        sel1 = m.sb("ga_sel1", [P, DA])
        sel2 = m.sb("ga_sel2", [GREST, DA])
        s1b = m.sb("ga_s1b", [P, H, CH])
        sign = m.sb("ga_sign", [P, 2, 2, CH], BF16)
        pos = m.sb("ga_pos", [P, 2, 2, CH], BF16)
        neg = m.sb("ga_neg", [P, 2, 2, CH], BF16)
        ev = m.sb("ga_ev", [P, 4, CH])
        out = m.sb("ga_out", [P, TPC, C])
        xr = m.sb("ga_xr", [P, TPC, C])
        te = m.sb("ga_te", [P, TPC, DA])
        tf = m.sb("ga_tf", [P, TPC, DA])
        lone = m.sb("ga_lone", [P, TPC, 1])
        den = m.sb("ga_den", [P, TPC, 1])
        acc = [m.bank(f"ga_acc{b}") for b in range(4)]
        ps_t = [m.bank(f"ga_ps_t{b}", BF16) for b in range(2)]
        ps_n = m.bank("ga_ps_n", F32, 2)

        const_in = m.sem("ga_const_in")
        cast_in = m.sem("ga_cast_in")
        adj_in = [m.sem(f"ga_adj_in{q}") for q in range(4)]
        rows_in = m.sem("ga_rows_in")
        x_in = m.sem("ga_x_in")
        turned = m.sem("ga_turned")
        no_edge_kept = [m.sem(f"ga_no_edge_kept{b}") for b in range(2)]
        signs = [m.sem(f"ga_signs{b}") for b in range(2)]
        pos_done = [m.sem(f"ga_pos_done{b}") for b in range(2)]
        neg_done = [m.sem(f"ga_neg_done{b}") for b in range(2)]
        mask_used = [m.sem(f"ga_mask_used{b}") for b in range(2)]
        ev_act = m.sem("ga_ev_act")
        ev_dve = m.sem("ga_ev_dve")
        natural = m.sem("ga_natural")
        nat_read = m.sem("ga_nat_read")
        steps = m.sem("ga_steps")
        stored = m.sem("ga_stored")
        block = ctx.enter_context(nc.Block())
        TAIL = 9

        @block.gpsimd
        def _(pool):
            pool.dma_start(identb[:], io["ident"]).then_inc(cast_in, 16)
            for q in range(4):
                pool.dma_start(nat[:, q], io["adj"][0:CH, q * QJ:(q + 1) * QJ].rearrange("(t p) j -> p t j", p=P)).then_inc(adj_in[q], 16)
            with pool.Fori(1, NC) as c:
                for q in range(4):
                    pool.wait_ge(turned, c * NP2 + ((q + 1) * (NP2 // 4) - NP2))
                    src = io["adj"][bass.ds(c * CH, CH), q * QJ:(q + 1) * QJ].rearrange("(t p) j -> p t j", p=P)
                    pool.dma_start(nat[:, q], src).then_inc(adj_in[q], 16)

        @block.sync
        def _(sp):
            sp.dma_start(sel1[:], io["sel"][0:P, :]).then_inc(const_in, 16)
            sp.dma_start(sel2[:], io["sel"][P:GW, :]).then_inc(const_in, 16)
            with sp.Fori(0, NC) as c:
                for b in range(2):
                    sp.wait_ge(signs[b], c * USES)
                for h in range(H):
                    sp.dma_start(s1b[:, h, :], io["s1_rows"][h, bass.ds(c * CH, CH)].partition_broadcast(P)).then_inc(rows_in, 16)
                sp.wait_ge(steps, c * (H * TAIL))
                sp.dma_start(xr[:], io["x"][bass.ds(c * CH, CH), :].rearrange("(t p) f -> p t f", p=P)).then_inc(x_in, 16)
                sp.wait_ge(steps, c * (H * TAIL) + H * TAIL)
                sp.dma_start(io["x1"][bass.ds(c * CH, CH), :].rearrange("(t p) f -> p t f", p=P), out[:]).then_inc(stored, 16)
            sp.wait_ge(stored, 16 * NC)

        @block.tensor
        def _(pe):
            pe.wait_ge(const_in, 32)
            pe.wait_ge(cast_in, 16)
            with pe.Fori(0, NC) as c:
                for q in range(4):
                    pe.wait_ge(adj_in[q], c * 16 + 16)
                    for k in range(NP2 // 4):
                        n = q * (NP2 // 4) + k
                        b = n % 2
                        pe.wait_ge(no_edge_kept[b], c * (NP2 // 2) + n // 2)
                        for j in range(2):
                            for it in range(TPC):
                                last = pe.transpose(ps_t[b][:, j * CH + it * P:j * CH + (it + 1) * P],
                                                    nat[:, q, it, (2 * k + j) * P:(2 * k + j + 1) * P], identb[:])
                        last.then_inc(turned, 1)
                with pe.Fori(0, H) as h:
                    hc = c * H + h
                    for n in range(NP2):
                        b = n % 2
                        for mask, ready, g, a in ((pos, pos_done, keep.ge, 0), (neg, neg_done, keep.gf, 2)):
                            pe.wait_ge(ready[b], hc * (NP2 // 2) + (n // 2 + 1))
                            for j in range(2):
                                jt = 2 * n + j
                                at = g[:, bass.ds(h + jt * H, 1), :].rearrange("p a g -> p (a g)")
                                pe.matmul(acc[a][:, :], at[:, 0:P], mask[:, b, j, :], start=jt == 0, stop=jt == NT - 1)
                                last = pe.matmul(acc[a + 1][0:GREST, :], at[:, P:GW], mask[:, b, j, :], start=jt == 0, stop=jt == NT - 1)
                        last.then_inc(mask_used[b], 1)
                    pe.wait_ge(ev_act, hc * 2 + 2)
                    pe.wait_ge(ev_dve, hc * 2 + 2)
                    pe.wait_ge(nat_read, hc)
                    for it in range(TPC):
                        for r in range(2):
                            o = ps_n[:, (it // 2) * 512 + ((it % 2) * 2 + r) * DA:(it // 2) * 512 + ((it % 2) * 2 + r + 1) * DA]
                            pe.matmul(o, ev[:, 2 * r, it * P:(it + 1) * P], sel1[:], start=True, stop=False)
                            last = pe.matmul(o, ev[0:GREST, 2 * r + 1, it * P:(it + 1) * P], sel2[:], start=False, stop=True)
                    last.then_inc(natural, 1)

        @block.scalar
        def _(act):
            with act.Fori(0, NC) as c:
                for n in range(0, NP2, 2):
                    act.wait_ge(turned, c * NP2 + (n + 1))
                    if n == 0:
                        act.wait_ge(neg_done[1], c * USES)
                    act.activation(no_edge[:, 2 * n:2 * n + 2, :], ps_t[0][:].rearrange("p (j i) -> p j i", j=2), ACT.Relu,
                                   scale=-1.0, bias=1.0).then_inc(no_edge_kept[0], 1)
                act.wait_ge(rows_in, c * (16 * H) + 16 * H)
                with act.Fori(0, H) as h:
                    hc = c * H + h
                    for n in range(NP2):
                        act.wait_ge(pos_done[n % 2], hc * (NP2 // 2) + n // 2)
                        for j in range(2):
                            last = act.activation(sign[:, n % 2, j:j + 1, :], s1b[:, bass.ds(h, 1), :], ACT.Sign,
                                                  bias=keep.s2[:, 2 * n + j, bass.ds(h, 1)])
                        last.then_inc(signs[n % 2], 1)
                    act.wait_ge(mask_used[1], hc * (NP2 // 2) + NP2 // 2)
                    act.wait_ge(natural, hc)
                    for a in (0, 2):
                        act.activation(ev[:, a, :], acc[a][:], ACT.Copy).then_inc(ev_act, 1)

        @block.vector
        def _(dve):
            chain = Chain(dve, steps)
            with dve.Fori(0, NC) as c:
                for n in range(1, NP2, 2):
                    dve.wait_ge(turned, c * NP2 + (n + 1))
                    dve.tensor_scalar(no_edge[:, 2 * n:2 * n + 2, :], ps_t[1][:].rearrange("p (j i) -> p j i", j=2), 0.0, None,
                                      ALU.is_le).then_inc(no_edge_kept[1], 1)
                with dve.Fori(0, H) as h:
                    hc = c * H + h
                    chain.at(hc * TAIL)
                    for n in range(NP2):
                        b = n % 2
                        use = hc * (NP2 // 2) + n // 2
                        if n == 0:
                            for k in range(2):
                                dve.wait_ge(no_edge_kept[k], c * (NP2 // 2) + NP2 // 2)
                        dve.wait_ge(signs[b], use + 1)
                        dve.wait_ge(mask_used[b], use)
                        no = no_edge[:, 2 * n:2 * n + 2, :].rearrange("p j i -> p (j i)")
                        dve.tensor_tensor(pos[:, b].rearrange("p j i -> p (j i)"), sign[:, b].rearrange("p j i -> p (j i)"), no,
                                          ALU.is_gt).then_inc(pos_done[b], 1)
                        dve.wait_ge(pos_done[b], use + 1)
                        dve.tensor_tensor(neg[:, b].rearrange("p j i -> p (j i)"), pos[:, b].rearrange("p j i -> p (j i)"), no,
                                          ALU.is_equal).then_inc(neg_done[b], 1)
                    dve.wait_ge(mask_used[1], hc * (NP2 // 2) + NP2 // 2)
                    dve.wait_ge(natural, hc)
                    for a in (1, 3):
                        dve.tensor_copy(ev[0:GREST, a, :], acc[a][0:GREST, :]).then_inc(ev_dve, 1)
                    dve.wait_ge(natural, hc + 1)
                    pn = ps_n[:].rearrange("p (g c) -> p g c", g=2)[:, :, 0:4 * DA].rearrange("p g (i r d) -> p g i r d", i=2, r=2)
                    def by(f):
                        return spread(f[:, bass.ds(c * TPC, TPC), bass.ds(h, 1)].rearrange("p (g i) h -> p g (i h)", g=2), 3, DA)
                    te4 = te[:].rearrange("p (g i) d -> p g i d", g=2)
                    tf4 = tf[:].rearrange("p (g i) d -> p g i d", g=2)
                    chain.step(dve.tensor_tensor(te4, pn[:, :, :, 0, :], by(keep.e1), ALU.mult))
                    ins = dve.tensor_tensor(tf4, pn[:, :, :, 1, :], by(keep.f1), ALU.mult)
                    ins.then_inc(nat_read, 1)
                    dve.wait_ge(nat_read, hc + 1)
                    chain.step(dve.tensor_tensor(te[:], te[:], tf[:], ALU.add))
                    chain.step(dve.tensor_scalar(lone[:], te[:, :, D:DA], 0.0, None, ALU.is_equal))
                    chain.step(dve.tensor_tensor(den[:], te[:, :, D:DA], lone[:], ALU.add))
                    chain.step(dve.reciprocal(den[:], den[:]))
                    chain.step(dve.tensor_tensor(te[:, :, 0:D], te[:, :, 0:D], den[:].to_broadcast([P, TPC, D]), ALU.mult))
                    chain.step(dve.tensor_tensor(tf[:, :, 0:D], lone[:].to_broadcast([P, TPC, D]),
                                                 spread(keep.mean[:, bass.ds(h * D, D)], 1, TPC), ALU.mult))
                    chain.step(dve.tensor_tensor(te[:, :, 0:D], te[:, :, 0:D], tf[:, :, 0:D], ALU.add))
                    dve.wait_ge(x_in, c * 16 + 16)
                    dve.wait_ge(stored, c * 16)
                    chain.step(dve.tensor_tensor(out[:, :, bass.ds(h * D, D)], te[:, :, 0:D],
                                                 xr[:, :, bass.ds(h * D, D)], ALU.add))
                    assert chain.n == TAIL


def products(pe, out, lhs, rhs, start=True, stop=True):
    n = len(lhs)
    for k in range(n):
        (lh, ll), (rh, rl) = lhs[k], rhs[k]
        pe.matmul(out, lh, rh, start=start and k == 0, stop=False)
        pe.matmul(out, lh, rl, start=False, stop=False)
        last = pe.matmul(out, ll, rh, start=False, stop=stop and k == n - 1)
    return last


def project_qkv(nc, io, keep):
    with ExitStack() as ctx:
        m = Pool(nc, ctx)
        y = keep.y
        va = m.sb("pq_va", [P, NT, KV, VW], F32R)
        raw = m.sb("pq_raw", [P, KC, QKW + P])
        wh = m.sb("pq_wh", [P, KC, QKW + P], F32R)
        wl = m.sb("pq_wl", [P, KC, QKW + P], F32R)
        ln1 = m.sb("pq_ln1", [P, KC])
        ident = m.sb("pq_ident", [P, P])
        trig = m.sb("pq_trig", [P, 2, CH])
        st = m.sb("pq_stats", [P, NT, 6])
        mu = m.sb("pq_mu", [P, NT])
        var = m.sb("pq_var", [P, NT])
        tmp = m.sb("pq_tmp", [P, NT])
        root = m.sb("pq_root", [P, NT])
        rstd = m.sb("pq_rstd", [P, NT])
        sq = m.sb("pq_sq", [P, NT])
        junk = m.sb("pq_junk", [P, 4, C])
        hn = m.sb("pq_hn", [P, TPC, C])
        hh = m.sb("pq_hh", [P, KC, CH], F32R)
        hl = m.sb("pq_hl", [P, KC, CH], F32R)
        ta = m.sb("pq_ta", [P, 3, CH])
        tb = m.sb("pq_tb", [P, 3, CH])
        rh = m.sb("pq_rh", [P, 3, CH], F32R)
        rl = m.sb("pq_rl", [P, 3, CH], F32R)
        ps_t = [m.bank(f"pq_ps_t{k}") for k in range(KC)]
        ps_a = [m.bank(f"pq_ps_a{b}") for b in range(2)]
        ps_b = [m.bank(f"pq_ps_b{b}") for b in range(2)]
        ps_v = m.bank("pq_ps_v")
        loaded = m.sem("pq_loaded")
        trig_in = m.sem("pq_trig_in")
        wh_done = m.sem("pq_wh_done")
        wl_done = m.sem("pq_wl_done")
        dve_steps = m.sem("pq_dve_steps")
        stats_done = m.sem("pq_stats_done")
        var_done = m.sem("pq_var_done")
        root_done = m.sem("pq_root_done")
        y_done = m.sem("pq_y_done")
        sq_done = m.sem("pq_sq_done")
        ms_done = m.sem("pq_ms_done")
        root2_done = m.sem("pq_root2_done")
        hn_done = m.sem("pq_hn_done")
        turned = m.sem("pq_turned")
        hh_done = m.sem("pq_hh_done")
        hl_done = m.sem("pq_hl_done")
        pair_done = m.sem("pq_pair_done")
        v_done = m.sem("pq_v_done")
        ta_done = m.sem("pq_ta_done")
        tb_done = m.sem("pq_tb_done")
        rope_done = m.sem("pq_rope_done")
        rh_done = m.sem("pq_rh_done")
        rl_done = m.sem("pq_rl_done")
        vh_done = m.sem("pq_vh_done")
        vl_done = m.sem("pq_vl_done")
        ones_set = m.sem("pq_ones_set")
        moved = m.sem("pq_moved")
        stored = m.sem("pq_stored")
        block = ctx.enter_context(nc.Block())
        LOADS = 7
        MOVES = 6

        @block.sync
        def _(sp):
            for q in range(4):
                sp.dma_start(y[:, 8 * q:8 * q + 8, :], io["x1"].rearrange("(t p) f -> p t f", p=P)[:, 8 * q:8 * q + 8, :]).then_inc(loaded, 16)
            sp.dma_start(raw[:], io["w_qkv"].rearrange("(k p) o -> p k o", p=P)).then_inc(loaded, 16)
            sp.dma_start(ln1[:], io["ln1"]).then_inc(loaded, 16)
            sp.dma_start(ident[:], io["ident"]).then_inc(loaded, 16)
            with sp.Fori(0, NC) as c:
                sp.wait_ge(tb_done, c * 3)
                sp.wait_ge(ta_done, c * 3)
                at = bass.ds(c * CH, CH)
                sp.dma_start(trig[:], io["trig"][:, :, at]).then_inc(trig_in, 16)
                for j in range(2):
                    sp.wait_ge(rh_done, c * 3 + (j + 1))
                    sp.wait_ge(rl_done, c * 3 + (j + 1))
                    sp.dma_start(io["q_high"][j * P:(j + 1) * P, at], rh[:, j, :].bitcast(F32)).then_inc(moved, 16)
                    sp.dma_start(io["q_low"][j * P:(j + 1) * P, at], rl[:, j, :].bitcast(F32)).then_inc(moved, 16)
                sp.wait_ge(rh_done, c * 3 + 3)
                sp.wait_ge(rl_done, c * 3 + 3)
                sp.dma_start(io["k_high"][:, at], rh[:, 2, :].bitcast(F32)).then_inc(moved, 16)
                sp.dma_start(io["k_low"][:, at], rl[:, 2, :].bitcast(F32)).then_inc(moved, 16)
            sp.wait_ge(moved, 16 * MOVES * NC)
            sp.wait_ge(vh_done, NC)
            sp.wait_ge(vl_done, NC)
            sp.wait_ge(ones_set, 2)
            for g in range(KV):
                sp.dma_start(io["va"][g], va[:, :, g, :].bitcast(F32)).then_inc(stored, 16)
            sp.wait_ge(stored, 16 * KV)

        @block.gpsimd
        def _(pool):
            pool.memset(va[:, :, :, D:DA].bitcast(F32), 1.0).then_inc(ones_set, 1)
            pool.memset(va[:, :, :, DA + D:VW].bitcast(F32), 0.0).then_inc(ones_set, 1)
            pool.wait_ge(ones_set, 2)

        @block.scalar
        def _(act):
            act.wait_ge(loaded, 16 * LOADS)
            act.activation(wh[:], raw[:], ACT.Copy).then_inc(wh_done, 1)
            act.wait_ge(var_done, 1)
            act.activation(root[:], var[:], ACT.Sqrt).then_inc(root_done, 1)
            with act.Fori(0, NT // 4) as i:
                act.wait_ge(sq_done, i * 4)
                for b in range(4):
                    t = i * 4 + b
                    act.wait_ge(y_done, t + 1)
                    act.activation(junk[:, b:b + 1, :], y[:, bass.ds(t, 1), :], ACT.Square, accum_out=sq[:, bass.ds(t, 1)]).then_inc(sq_done, 1)
            act.wait_ge(ms_done, 1)
            act.activation(root[:], var[:], ACT.Sqrt).then_inc(root2_done, 1)
            with act.Fori(0, NC) as c:
                act.wait_ge(turned, c + 1)
                act.wait_ge(v_done, c)
                for k in range(KC):
                    act.activation(hh[:, k, :], ps_t[k][:], ACT.Copy, scale=ln1[:, k:k + 1]).then_inc(hh_done, 1)
                act.wait_ge(moved, c * (16 * MOVES))
                for j in range(3):
                    act.wait_ge(rope_done, c * 3 + (j + 1))
                    act.activation(rh[:, j, :], ta[:, j, :], ACT.Copy).then_inc(rh_done, 1)
                act.wait_ge(v_done, c + 1)
                act.activation(va[:, bass.ds(c * TPC, TPC), :, 0:D].rearrange("p t g d -> p (t g) d"),
                               ps_v[:].rearrange("p (t g d) -> p (t g) d", g=KV, d=D), ACT.Copy).then_inc(vh_done, 1)

        @block.tensor
        def _(pe):
            pe.wait_ge(loaded, 16 * LOADS)
            pe.wait_ge(wh_done, 1)
            pe.wait_ge(wl_done, 1)
            with pe.Fori(0, NC) as c:
                pe.wait_ge(hn_done, c * TPC + TPC)
                pe.wait_ge(hl_done, c * KC)
                for k in range(KC):
                    for it in range(TPC):
                        last = pe.transpose(ps_t[k][:, it * P:(it + 1) * P], hn[:, it, k * P:(k + 1) * P], ident[:])
                last.then_inc(turned, 1)
                pe.wait_ge(hh_done, c * KC + KC)
                pe.wait_ge(hl_done, c * KC + KC)
                act_k = [(hh[:, k, :], hl[:, k, :]) for k in range(KC)]
                for j in range(3):
                    if j < 2:
                        pe.wait_ge(tb_done, c * 3)
                        pe.wait_ge(ta_done, c * 3)
                    else:
                        pe.wait_ge(tb_done, c * 3 + 1)
                        pe.wait_ge(ta_done, c * 3 + 1)
                    for s, ps in ((0, ps_a), (1, ps_b)):
                        col = slice((2 * j + s) * P, (2 * j + s + 1) * P)
                        last = products(pe, ps[j % 2][:], [(wh[:, k, col], wl[:, k, col]) for k in range(KC)], act_k)
                    last.then_inc(pair_done, 1)
                pe.wait_ge(vh_done, c)
                pe.wait_ge(vl_done, c)
                for it in range(TPC):
                    tok = slice(it * P, (it + 1) * P)
                    last = products(pe, ps_v[:, tok], [(hh[:, k, tok], hl[:, k, tok]) for k in range(KC)],
                                    [(wh[:, k, QKW:], wl[:, k, QKW:]) for k in range(KC)])
                last.then_inc(v_done, 1)

        @block.vector
        def _(dve):
            chain = Chain(dve, dve_steps)
            dve.wait_ge(loaded, 16 * LOADS)
            dve.wait_ge(wh_done, 1)
            dve.tensor_tensor(wl[:], raw[:], wh[:].bitcast(F32), ALU.subtract).then_inc(wl_done, 1)
            with dve.Fori(0, NT // 4) as i:
                for b in range(4):
                    dve.bn_stats(st[:, bass.ds(i * 4 + b, 1), :].rearrange("p t s -> p (t s)"),
                                 y[:, bass.ds(i * 4 + b, 1), :].rearrange("p t s -> p (t s)")).then_inc(stats_done, 1)
            dve.wait_ge(stats_done, NT)
            layer_norm_tail(chain, st, mu, var, tmp, var_done)
            inverse_root(chain, var[:], root[:], rstd[:], tmp[:], root_done, 1)
            with dve.Fori(0, NT) as t:
                dve.tensor_scalar(y[:, bass.ds(t, 1), :], y[:, bass.ds(t, 1), :], mu[:, bass.ds(t, 1)], rstd[:, bass.ds(t, 1)],
                                  ALU.subtract, ALU.mult).then_inc(y_done, 1)
            dve.wait_ge(sq_done, NT)
            dve.tensor_scalar(var[:], sq[:], 1.0 / C, 1e-6, ALU.mult, ALU.add).then_inc(ms_done, 1)
            inverse_root(chain, var[:], root[:], rstd[:], tmp[:], root2_done, 1)
            with dve.Fori(0, NC) as c:
                dve.wait_ge(turned, c)
                for it in range(TPC):
                    t = c * TPC + it
                    dve.tensor_scalar(hn[:, it:it + 1, :], y[:, bass.ds(t, 1), :], rstd[:, bass.ds(t, 1)], None, ALU.mult).then_inc(hn_done, 1)
                for k in range(KC):
                    dve.wait_ge(hh_done, c * KC + KC)
                    dve.scalar_tensor_tensor(hl[:, k, :], ps_t[k][:], ln1[:, k:k + 1], hh[:, k, :].bitcast(F32), ALU.mult,
                                             ALU.subtract).then_inc(hl_done, 1)
                dve.wait_ge(trig_in, c * 16 + 16)
                dve.wait_ge(moved, c * (16 * MOVES))
                for j in range(3):
                    dve.wait_ge(pair_done, c * 3 + (j + 1))
                    dve.wait_ge(rh_done, c * 3)
                    dve.tensor_tensor(ta[:, j, :], ps_a[j % 2][:], trig[:, 0, :], ALU.mult).then_inc(ta_done, 1)
                    dve.tensor_tensor(tb[:, j, :], ps_b[j % 2][:], trig[:, 1, :], ALU.mult).then_inc(tb_done, 1)
                    dve.wait_ge(tb_done, c * 3 + (j + 1))
                    dve.wait_ge(ta_done, c * 3 + (j + 1))
                    dve.tensor_tensor(ta[:, j, :], ta[:, j, :], tb[:, j, :], ALU.add).then_inc(rope_done, 1)
                    dve.wait_ge(rope_done, c * 3 + (j + 1))
                    dve.wait_ge(rh_done, c * 3 + (j + 1))
                    dve.tensor_tensor(rl[:, j, :], ta[:, j, :], rh[:, j, :].bitcast(F32), ALU.subtract).then_inc(rl_done, 1)
                dve.wait_ge(vh_done, c + 1)
                vt = va[:, bass.ds(c * TPC, TPC), :, :].rearrange("p t g d -> p (t g) d")
                dve.tensor_tensor(vt[:, :, DA:DA + D], ps_v[:].rearrange("p (t g d) -> p (t g) d", g=KV, d=D),
                                  vt[:, :, 0:D].bitcast(F32), ALU.subtract).then_inc(vl_done, 1)


def sequence_attention(nc, io, keep):
    with ExitStack() as ctx:
        m = Pool(nc, ctx)
        identb = m.sb("sa_identb", [P, P], BF16)
        ident = m.sb("sa_ident", [P, P])
        late_k = m.sb("sa_late_k", [P, P], BF16)
        late_q = m.sb("sa_late_q", [P, P], BF16)
        onesf = m.sb("sa_onesf", [P, P])
        ones = m.sb("sa_ones", [P, DA], F32R)
        zeros = m.sb("sa_zeros", [P, SLOTS * CH * C // (P * 4)])
        ks = m.sb("sa_ks", [P, N], F32R)
        kb = m.sb("sa_kb", [DA, N], F32R)
        va = m.sb("sa_va", [P, NT, VW], F32R)
        qa = [m.sb(f"sa_qa{b}", [P, CH], F32R) for b in range(2)]
        qb = [m.sb(f"sa_qb{b}", [DA, CH], F32R) for b in range(2)]
        mx = [m.sb(f"sa_mx{b}", [P, TPC, NC]) for b in range(2)]
        m4 = [m.sb(f"sa_m4{b}", [P, TPC]) for b in range(2)]
        dg = m.sb("sa_dg", [P, TPC, P], F32R)
        ph = [m.sb(f"sa_ph{b}", [P, CH], F32R) for b in range(3)]
        pl = [m.sb(f"sa_pl{b}", [P, CH], F32R) for b in range(3)]
        ysb = m.sb("sa_ysb", [DA, CH])
        rec = m.sb("sa_rec", [P, TPC])
        yo = [m.sb(f"sa_yo{b}", [P, TPC, D]) for b in range(2)]
        ps_n = [m.bank(f"sa_ps_n{b}") for b in range(2)]
        ps_s = [m.bank(f"sa_ps_s{b}") for b in range(3)]
        ps_y = m.bank("sa_ps_y")
        ps_m = m.bank("sa_ps_m")
        ps_x = m.bank("sa_ps_x")
        const_in = m.sem("sa_const_in")
        cast_in = m.sem("sa_cast_in")
        ones_set = m.sem("sa_ones_set")
        zeros_set = m.sem("sa_zeros_set")
        blanked = m.sem("sa_blanked")
        kv_first_in = m.sem("sa_kv_first_in")
        kv_rest_in = m.sem("sa_kv_rest_in")
        q_in = [m.sem(f"sa_q_in{b}") for b in range(2)]
        scored = [m.sem(f"sa_scored{b}") for b in range(2)]
        part_max = [m.sem(f"sa_part_max{b}") for b in range(2)]
        max_done = m.sem("sa_max_done")
        diag_done = m.sem("sa_diag_done")
        spread_done = m.sem("sa_spread_done")
        shift_done = m.sem("sa_shift_done")
        full_scored = m.sem("sa_full_scored")
        exp_done = m.sem("sa_exp_done")
        ph_done = m.sem("sa_ph_done")
        pl_done = m.sem("sa_pl_done")
        p_used = m.sem("sa_p_used")
        y_kept = m.sem("sa_y_kept")
        y_turned = m.sem("sa_y_turned")
        rec_done = m.sem("sa_rec_done")
        y_done = m.sem("sa_y_done")
        stored = [m.sem(f"sa_stored{b}") for b in range(2)]
        block = ctx.enter_context(nc.Block())

        ROUNDS = [(c, b) for c in range(NC) for b in range(2)]
        R = len(ROUNDS)
        first = [[(it, kc, CH if kc < c else (it + 1) * P) for it in range(TPC) for kc in range(c + 1)] for c, _ in ROUNDS]
        second = [[(kt, max(0, kt - c * TPC) * P) for kt in range((c + 1) * TPC)] for c, _ in ROUNDS]
        first_before = [sum(map(len, first[:n])) for n in range(R + 1)]
        second_before = [sum(map(len, second[:n])) for n in range(R + 1)]
        FIRST, SECOND = first_before[R], second_before[R]
        assert FIRST % 2 == 0

        def ahead(n, i):
            within, all_ = max(1, len(second[n]) - 4), len(first[n + 1])
            return range(min(all_, i * all_ // within), min(all_, (i + 1) * all_ // within))

        def spread_at(n):
            return len(second[n]) - 3

        BLANKED_AT = (7, 11)
        BLANK = SLOTS * CH // KV // len(BLANKED_AT)

        @block.sync
        def _(sp):
            sp.dma_start(ident[:], io["ident"]).then_inc(const_in, 16)
            sp.wait_ge(zeros_set, 1)
            with sp.Fori(0, KV) as g:
                for n, (c, b) in enumerate(ROUNDS):
                    sp.wait_ge(y_done, g * R + (n + 1))
                    sp.dma_start(io["ya"][c * CH:(c + 1) * CH, bass.ds(g * (2 * D) + b * D, D)].rearrange("(t p) d -> p t d", p=P),
                                 yo[n % 2][:]).then_inc(stored[n % 2], 16)
                    if n in BLANKED_AT:
                        at = g * (SLOTS * CH // KV) + BLANKED_AT.index(n) * BLANK
                        sp.dma_start(io["sorted_rows"][bass.ds(at, BLANK), :].rearrange("(p r) f -> p (r f)", p=P), zeros[:]).then_inc(blanked, 16)
            for b in range(2):
                sp.wait_ge(stored[b], 8 * KV * R)
            sp.wait_ge(blanked, 16 * KV * len(BLANKED_AT))

        @block.gpsimd
        def _(pool):
            pool.memset(onesf[:], 1.0).then_inc(ones_set, 1)
            pool.memset(zeros[:], 0.0).then_inc(zeros_set, 1)
            for tile, name in ((identb, "ident"), (late_k, "late_k"), (late_q, "late_q")):
                pool.dma_start(tile[:], io[name]).then_inc(cast_in, 16)
            with pool.Fori(0, KV) as g:
                rows = bass.ds(g * D, D)
                pool.wait_ge(p_used, g * SECOND)
                def load_kv(tiles, done):
                    at = slice(tiles.start * P, tiles.stop * P)
                    pool.dma_start(ks[0:D, at], io["k_high"][rows, at]).then_inc(done, 16)
                    pool.dma_start(ks[D:P, at], io["k_low"][rows, at]).then_inc(done, 16)
                    pool.dma_start(kb[0:D, at], io["k_high"][rows, at]).then_inc(done, 16)
                    pool.dma_start(va[:, tiles], io["va"][bass.ds(g, 1), :, tiles, :].rearrange("g p t d -> (g p) t d")).then_inc(done, 16)

                load_kv(slice(0, TPC), kv_first_in)
                for n, (c, b) in enumerate(ROUNDS):
                    if n >= 2:
                        pool.wait_ge(p_used, g * SECOND + second_before[n - 1])
                    head, at = bass.ds(g * (2 * D) + b * D, D), slice(c * CH, (c + 1) * CH)
                    pool.dma_start(qa[n % 2][0:D, :], io["q_high"][head, at]).then_inc(q_in[n % 2], 16)
                    pool.dma_start(qa[n % 2][D:P, :], io["q_high"][head, at]).then_inc(q_in[n % 2], 16)
                    pool.dma_start(qb[n % 2][0:D, :], io["q_low"][head, at]).then_inc(q_in[n % 2], 16)
                    if n == 1:
                        load_kv(slice(TPC, NT), kv_rest_in)

        @block.tensor
        def _(pe):
            pe.wait_ge(const_in, 16)
            pe.wait_ge(cast_in, 48)
            pe.wait_ge(ones_set, 3)
            with pe.Fori(0, KV) as g:
                def first_pass(n, some):
                    c, _ = ROUNDS[n]
                    if some.start == 0:
                        pe.wait_ge(q_in[n % 2], g * (24 * R) + 48 * (n // 2 + 1))
                    for i in some:
                        it, kc, cols = first[n][i]
                        step = first_before[n] + i
                        pe.wait_ge(part_max[step % 2], g * (FIRST // 2) + step // 2)
                        ps = ps_n[step % 2]
                        last = pe.matmul(ps[:, 0:cols], qa[n % 2][0:D, it * P:(it + 1) * P], ks[0:D, kc * CH:kc * CH + cols],
                                         start=True, stop=kc < c)
                        if kc == c:
                            last = pe.matmul(ps[:, cols - P:cols], identb[:], late_k[:], start=False, stop=True)
                        last.then_inc(scored[step % 2], 1)

                def spread_shift(n):
                    pe.wait_ge(diag_done, g * (R * TPC) + TPC * (n + 1))
                    pe.wait_ge(shift_done, g * R + n)
                    for it in range(TPC):
                        last = pe.matmul(ps_m[0:DA, it * P:(it + 1) * P], ones[:], dg[:, it, :], start=True, stop=True)
                    last.then_inc(spread_done, 1)

                def scores(n, i):
                    c, _ = ROUNDS[n]
                    kt, lo = second[n][i]
                    step = second_before[n] + i
                    pe.wait_ge(pl_done, g * SECOND + max(0, step - 2))
                    ps, keys = ps_s[step % 3], slice(kt * P, (kt + 1) * P)
                    pe.matmul(ps[:, lo:CH], ks[:, keys], qa[n % 2][:, lo:CH], start=True, stop=False)
                    last = pe.matmul(ps[:, lo:CH], kb[:, keys], qb[n % 2][:, lo:CH], start=False, stop=kt < c * TPC)
                    if kt >= c * TPC:
                        last = pe.matmul(ps[:, lo:lo + P], identb[:], late_q[:], start=False, stop=True)
                    last.then_inc(full_scored, 1)

                def weigh(n, i):
                    kt, lo = second[n][i]
                    step = second_before[n] + i
                    pe.wait_ge(ph_done, g * SECOND + (step + 1))
                    pe.wait_ge(pl_done, g * SECOND + (step + 1))
                    high, low = va[:, kt, 0:DA], va[:, kt, DA:2 * DA]
                    out, last_kt = ps_y[0:DA, lo:CH], i == len(second[n]) - 1
                    pe.matmul(out, high, ph[step % 3][:, lo:CH], start=i == 0, stop=False)
                    pe.matmul(out, low, ph[step % 3][:, lo:CH], start=False, stop=False)
                    pe.matmul(out, high, pl[step % 3][:, lo:CH], start=False, stop=last_kt).then_inc(p_used, 1)

                def turn_back(n):
                    pe.wait_ge(y_kept, g * R + (n + 1))
                    pe.wait_ge(y_done, g * R + n)
                    for it in range(TPC):
                        last = pe.transpose(ps_x[:, it * DA:(it + 1) * DA], ysb[:, it * P:(it + 1) * P], ident[0:DA, 0:DA])
                    last.then_inc(y_turned, 1)

                pe.wait_ge(kv_first_in, g * 64 + 64)
                first_pass(0, range(len(first[0])))
                spread_shift(0)
                pe.wait_ge(shift_done, g * R + 1)
                scores(0, 0)
                scores(0, 1)
                for n in range(R):
                    for i in range(len(second[n])):
                        if i == spread_at(n) and n + 1 < R:
                            spread_shift(n + 1)
                        if i + 2 < len(second[n]):
                            scores(n, i + 2)
                        elif n + 1 < R:
                            if i + 2 == len(second[n]):
                                pe.wait_ge(shift_done, g * R + (n + 2))
                            scores(n + 1, i + 2 - len(second[n]))
                        if n + 1 < R:
                            if n == 1 and i == 0:
                                pe.wait_ge(kv_rest_in, g * 64 + 64)
                            first_pass(n + 1, ahead(n, i))
                        if i == 0:
                            pe.wait_ge(y_kept, g * R + n)
                        weigh(n, i)
                        if i == 1 and n > 0:
                            turn_back(n - 1)
                turn_back(R - 1)

        @block.scalar
        def _(act):
            act.wait_ge(ones_set, 1)
            act.activation(ones[:], onesf[:, 0:DA], ACT.Copy).then_inc(ones_set, 1)
            for k in range(N // CH):
                last = act.activation(kb[D:DA, k * CH:(k + 1) * CH].rearrange("o (a b) -> o a b", b=P),
                                      spread(onesf[D:DA, :], 1, TPC), ACT.Copy)
            last.then_inc(ones_set, 1)
            with act.Fori(0, KV) as g:
                def keep_shift(n):
                    act.wait_ge(spread_done, g * R + (n + 1))
                    act.wait_ge(p_used, g * SECOND + (second_before[n - 1] if n >= 2 else 0))
                    act.activation(qb[n % 2][D:DA, :], ps_m[D:DA, :], ACT.Copy).then_inc(shift_done, 1)

                def keep_sums(n):
                    act.wait_ge(p_used, g * SECOND + second_before[n + 1])
                    act.wait_ge(y_turned, g * R + n)
                    act.activation(ysb[:], ps_y[0:DA, :], ACT.Copy).then_inc(y_kept, 1)

                def exps(n, i):
                    lo, step = second[n][i][1], second_before[n] + i
                    act.wait_ge(full_scored, g * SECOND + (step + 1))
                    act.activation(ps_s[step % 3][:, lo:CH], ps_s[step % 3][:, lo:CH], ACT.Exp, scale=D ** -0.5).then_inc(exp_done, 1)

                def high_part(n, i):
                    lo, step = second[n][i][1], second_before[n] + i
                    act.wait_ge(exp_done, g * SECOND + (step + 1))
                    act.wait_ge(p_used, g * SECOND + max(0, step - 2))
                    act.activation(ph[step % 3][:, lo:CH], ps_s[step % 3][:, lo:CH], ACT.Copy).then_inc(ph_done, 1)

                keep_shift(0)
                for n in range(R):
                    for i in range(len(second[n])):
                        exps(n, i)
                        if i == len(second[n]) - 2 and n + 1 < R:
                            keep_shift(n + 1)
                        high_part(n, i)
                        if i == 0 and n > 0:
                            keep_sums(n - 1)
                keep_sums(R - 1)

        @block.vector
        def _(dve):
            dve.wait_ge(const_in, 16)
            with dve.Fori(0, KV) as g:
                def maxima(n, some):
                    for i in some:
                        it, kc, cols = first[n][i]
                        step = first_before[n] + i
                        dve.wait_ge(scored[step % 2], g * (FIRST // 2) + (step // 2 + 1))
                        dve.tensor_reduce(mx[n % 2][:, it, kc:kc + 1], ps_n[step % 2][:, 0:cols], AX.X, ALU.max).then_inc(part_max[step % 2], 1)

                def shift(n):
                    c, _ = ROUNDS[n]
                    for w in range(2):
                        dve.wait_ge(part_max[w], g * (FIRST // 2) + (first_before[n + 1] + 1 - w) // 2)
                    dve.tensor_reduce(m4[n % 2][:], mx[n % 2][:, :, 0:c + 1], AX.X, ALU.max).then_inc(max_done, 1)
                    dve.wait_ge(max_done, g * R + (n + 1))
                    dve.wait_ge(spread_done, g * R + n)
                    for it in range(TPC):
                        dve.tensor_scalar(dg[:, it, :], ident[:], m4[n % 2][:, it:it + 1], -1.0, ALU.mult, ALU.mult).then_inc(diag_done, 1)

                def finish(n):
                    dve.wait_ge(y_turned, g * R + (n + 1))
                    px = ps_x[:, 0:TPC * DA].rearrange("p (t d) -> p t d", d=DA)
                    dve.reciprocal(rec[:].unsqueeze(2), px[:, :, D:DA]).then_inc(rec_done, 1)
                    dve.wait_ge(rec_done, g * R + (n + 1))
                    dve.wait_ge(stored[n % 2], g * (8 * R) + 16 * (n // 2))
                    dve.tensor_tensor(yo[n % 2][:], px[:, :, 0:D], spread(rec[:], 2, D), ALU.mult).then_inc(y_done, 1)

                maxima(0, range(len(first[0])))
                shift(0)
                for n in range(R):
                    for i, (kt, lo) in enumerate(second[n]):
                        step = second_before[n] + i
                        dve.wait_ge(ph_done, g * SECOND + (step + 1))
                        dve.tensor_tensor(pl[step % 3][:, lo:CH], ps_s[step % 3][:, lo:CH], ph[step % 3][:, lo:CH].bitcast(F32),
                                          ALU.subtract).then_inc(pl_done, 1)
                        if n + 1 < R:
                            maxima(n + 1, ahead(n, i))
                            if ahead(n, i) and ahead(n, i).stop == len(first[n + 1]):
                                shift(n + 1)
                        if i == 2 and n > 0:
                            finish(n - 1)
                finish(R - 1)


def join_and_route(nc, io, keep):
    with ExitStack() as ctx:
        m = Pool(nc, ctx)
        y = keep.y
        ident = m.sb("jr_ident", [P, P])
        wo = m.sb("jr_wo", [P, KC, C])
        woh = m.sb("jr_woh", [P, KC, C], F32R)
        wol = m.sb("jr_wol", [P, KC, C], F32R)
        wr = m.sb("jr_wr", [P, KC, E])
        wrh = m.sb("jr_wrh", [P, KC, E], F32R)
        wrl = m.sb("jr_wrl", [P, KC, E], F32R)
        ln2 = m.sb("jr_ln2", [P, KC])
        plan = m.sb("jr_plan", [P, PLAN_COLS])
        before = m.sb("jr_before", [P, P], BF16)
        ones = m.sb("jr_ones", [P, P], BF16)
        ya = [m.sb(f"jr_ya{b}", [P, TPC, C]) for b in range(2)]
        ah = [m.sb(f"jr_ah{b}", [P, KC, CH], F32R) for b in range(2)]
        al = [m.sb(f"jr_al{b}", [P, KC, CH], F32R) for b in range(2)]
        hn = m.sb("jr_hn", [P, NT, C])
        junk = m.sb("jr_junk", [P, TPC, C])
        sq = m.sb("jr_sq", [P, NT])
        var = m.sb("jr_var", [P, NT])
        root = m.sb("jr_root", [P, NT])
        r2 = m.sb("jr_r2", [P, NT])
        tmp = m.sb("jr_tmp", [P, NT])
        lt = m.sb("jr_lt", [E, 2, CH])
        lg = m.sb("jr_lg", [P, NT, E])
        w8 = m.sb("jr_w8", [P, NT, E])
        one = m.sb("jr_one", [P, NT])
        first = m.sb("jr_first", [P, NT, E])
        second = m.sb("jr_second", [P, NT, E])
        pick = m.sb("jr_pick", [P, NT, E])
        chosen = m.sb("jr_chosen", [P, NT, E], BF16)
        top = m.sb("jr_top", [P, NT])
        within = m.sb("jr_within", [P, NT, E])
        of_tile = m.sb("jr_of_tile", [P, NT, E])
        upto = [m.sb(f"jr_upto{b}", [P, NT, E]) for b in range(2)]
        place = m.sb("jr_place", [P, NT])
        over = m.sb("jr_over", [P, E, NC])
        slots = m.sb("jr_slots", [P, E])
        sums = m.sb("jr_sums", [P, E, E])
        end = m.sb("jr_end", [P, E])
        ended = m.sb("jr_ended", [P, SLOTS, E])
        owner = m.sb("jr_owner", [P, SLOTS])
        ps_t = [[m.bank(f"jr_ps_t{b}{k}") for k in range(KC)] for b in range(2)]
        ps_y = [m.bank(f"jr_ps_y{b}") for b in range(2)]
        ps_l = m.bank("jr_ps_l")
        ps_g = m.bank("jr_ps_g")
        loaded = m.sem("jr_loaded")
        cast_in = m.sem("jr_cast_in")
        ones_set = m.sem("jr_ones_set")
        chosen_done = m.sem("jr_chosen_done")
        counted = m.sem("jr_counted")
        owners_done = m.sem("jr_owners_done")
        places_done = m.sem("jr_places_done")
        scattered = m.sem("jr_scattered")
        expert_in = [m.sem(f"jr_expert_in{b}") for b in range(2)]
        expert_high = m.sem("jr_expert_high")
        expert_low = m.sem("jr_expert_low")
        ya_in = [m.sem(f"jr_ya_in{b}") for b in range(2)]
        high_done = m.sem("jr_high_done")
        low_done = m.sem("jr_low_done")
        ya_turned = m.sem("jr_ya_turned")
        ah_done = m.sem("jr_ah_done")
        al_done = m.sem("jr_al_done")
        joined = m.sem("jr_joined")
        y2_done = m.sem("jr_y2_done")
        sq_done = m.sem("jr_sq_done")
        ms_done = m.sem("jr_ms_done")
        root_done = m.sem("jr_root_done")
        steps = m.sem("jr_steps")
        hn_done = m.sem("jr_hn_done")
        hn_turned = m.sem("jr_hn_turned")
        h2h_done = m.sem("jr_h2h_done")
        h2l_done = m.sem("jr_h2l_done")
        scored = m.sem("jr_scored")
        lt_kept = m.sem("jr_lt_kept")
        lt_turned = m.sem("jr_lt_turned")
        lg_kept = m.sem("jr_lg_kept")
        shifted = m.sem("jr_shifted")
        exps_done = m.sem("jr_exps_done")
        x1_in = [m.sem(f"jr_x1_in{b}") for b in range(2)]
        x1_added = m.sem("jr_x1_added")
        block = ctx.enter_context(nc.Block())
        LOADS = 5

        @block.sync
        def _(sp):
            sp.dma_start(wo[:], io["w_o"].rearrange("(k p) o -> p k o", p=P)).then_inc(loaded, 16)
            sp.dma_start(ident[:], io["ident"]).then_inc(loaded, 16)
            sp.dma_start(wr[:], io["w_r"].rearrange("(k p) o -> p k o", p=P)).then_inc(loaded, 16)
            sp.dma_start(ln2[:], io["ln2"]).then_inc(loaded, 16)
            sp.dma_start(plan[:], io["plan"]).then_inc(loaded, 16)
            with sp.Fori(0, NC // 2) as i:
                for b in range(2):
                    sp.wait_ge(ya_turned, i * 2 + b)
                    sp.dma_start(ya[b][:], io["ya"][bass.ds((i * 2 + b) * CH, CH), :].rearrange("(t p) f -> p t f", p=P)).then_inc(ya_in[b], 16)
            for c in range(NC):
                if c < 2:
                    sp.wait_ge(ya_turned, NC - 1 + c)
                else:
                    sp.wait_ge(x1_added, c - 1)
                sp.dma_start(ya[c % 2][:], io["x1"][c * CH:(c + 1) * CH, :].rearrange("(t p) f -> p t f", p=P)).then_inc(x1_in[c % 2], 16)

        @block.gpsimd
        def _(pool):
            pool.dma_start(before[:], io["before"]).then_inc(cast_in, 16)
            pool.memset(ones[:], 1.0).then_inc(ones_set, 1)
            for c in range(NC):
                tiles = slice(c * TPC, (c + 1) * TPC)
                pool.wait_ge(x1_in[c % 2], 16 * (c // 2 + 1))
                pool.wait_ge(hn_turned, c + 1)
                pool.tensor_tensor(y[:, tiles, :], y[:, tiles, :], ya[c % 2][:], ALU.add).then_inc(x1_added, 1)
            pool.wait_ge(owners_done, 1)
            for b in range(2):
                gather_expert(pool, io, keep, b).then_inc(expert_in[b], 16)
            pool.wait_ge(places_done, 2)
            pool.wait_ge(hn_done, NC)
            for t in range(NT):
                for r in range(2):
                    pool.indirect_dma_start(io["sorted_rows"], bass.IndirectOffsetOnAxis(keep.place[:, r, t:t + 1], 0),
                                            hn[:, t, :], None).then_inc(scattered, 16)
            pool.wait_ge(scattered, 16 * 2 * NT)
            for b in range(2):
                pool.wait_ge(expert_in[b], 16)

        @block.tensor
        def _(pe):
            pe.wait_ge(loaded, 16 * LOADS)
            pe.wait_ge(high_done, 2)
            pe.wait_ge(low_done, 2)
            with pe.Fori(0, NC // 2) as i:
                for b in range(2):
                    pe.wait_ge(ya_in[b], i * 16 + 16)
                    pe.wait_ge(al_done, i * 2 + b)
                    for k in range(KC):
                        for it in range(TPC):
                            last = pe.transpose(ps_t[b][k][:, it * P:(it + 1) * P], ya[b][:, it, k * P:(k + 1) * P], ident[:])
                    last.then_inc(ya_turned, 1)
                for b in range(2):
                    pe.wait_ge(ah_done, i * 2 + (b + 1))
                    pe.wait_ge(al_done, i * 2 + (b + 1))
                    for half in range(2):
                        pe.wait_ge(y2_done, i * 4 + max(0, 2 * b + half - 1))
                        for j in range(2):
                            tok = slice((2 * half + j) * P, (2 * half + j + 1) * P)
                            last = products(pe, ps_y[half][:, j * C:(j + 1) * C], [(ah[b][:, k, tok], al[b][:, k, tok]) for k in range(KC)],
                                            [(woh[:, k, :], wol[:, k, :]) for k in range(KC)])
                        last.then_inc(joined, 1)
            def score(c):
                pe.wait_ge(h2h_done, c + 1)
                pe.wait_ge(h2l_done, c + 1)
                if c > 0:
                    pe.wait_ge(lt_kept, c)
                products(pe, ps_l[0:E, :], [(wrh[:, k, :], wrl[:, k, :]) for k in range(KC)],
                         [(ah[c % 2][:, k, :], al[c % 2][:, k, :]) for k in range(KC)]).then_inc(scored, 1)
            def turn_scores(c):
                pe.wait_ge(lt_kept, c + 1)
                if c > 0:
                    pe.wait_ge(lg_kept, c)
                for it in range(TPC):
                    last = pe.transpose(ps_g[:, it * E:(it + 1) * E], lt[:, c % 2, it * P:(it + 1) * P], ident[0:E, 0:E])
                last.then_inc(lt_turned, 1)
            for c in range(NC + 2):
                if c < NC:
                    b = c % 2
                    pe.wait_ge(hn_done, c + 1)
                    if c >= 2:
                        pe.wait_ge(h2h_done, c - 1)
                        pe.wait_ge(h2l_done, c - 1)
                    for k in range(KC):
                        for it in range(TPC):
                            last = pe.transpose(ps_t[b][k][:, it * P:(it + 1) * P],
                                                hn[:, c * TPC + it, k * P:(k + 1) * P], ident[:])
                    last.then_inc(hn_turned, 1)
                if c >= 2:
                    turn_scores(c - 2)
                if 1 <= c <= NC:
                    score(c - 1)
            pe.wait_ge(chosen_done, 1)
            pe.wait_ge(cast_in, 16)
            pe.wait_ge(ones_set, 1)
            pe.wait_ge(lg_kept, NC)
            picks = chosen[:].rearrange("p t e -> p (t e)")
            pe.matmul(ps_l[:, 0:NT * E], before[:], picks, start=True, stop=True)
            pe.matmul(ps_g[:, 0:NT * E], ones[:], picks, start=True, stop=True).then_inc(counted, 1)

        @block.scalar
        def _(act):
            act.wait_ge(loaded, 16 * LOADS)
            act.activation(woh[:], wo[:], ACT.Copy).then_inc(high_done, 1)
            act.activation(wrh[:], wr[:], ACT.Copy).then_inc(high_done, 1)
            with act.Fori(0, NC // 2) as i:
                for b in range(2):
                    act.wait_ge(ya_turned, i * 2 + (b + 1))
                    act.wait_ge(joined, i * 4)
                    for k in range(KC):
                        last = act.activation(ah[b][:, k, :], ps_t[b][k][:], ACT.Copy)
                    last.then_inc(ah_done, 1)
                for q in range(4):
                    act.wait_ge(y2_done, i * 4 + (q + 1))
                    act.wait_ge(sq_done, i * 4 + q)
                    for j in range(2):
                        t = i * 8 + (2 * q + j)
                        last = act.activation(junk[:, j:j + 1, :], y[:, bass.ds(t, 1), :], ACT.Square, accum_out=sq[:, bass.ds(t, 1)])
                    last.then_inc(sq_done, 1)
            act.wait_ge(ms_done, 1)
            act.activation(root[:], var[:], ACT.Sqrt).then_inc(root_done, 1)
            for c in range(NC):
                b = c % 2
                act.wait_ge(hn_turned, c + 1)
                if c >= 2:
                    act.wait_ge(scored, c - 1)
                for k in range(KC):
                    last = act.activation(ah[b][:, k, :], ps_t[b][k][:], ACT.Copy, scale=ln2[:, k:k + 1])
                last.then_inc(h2h_done, 1)
                act.wait_ge(scored, c + 1)
                if c >= 2:
                    act.wait_ge(lt_turned, c - 1)
                act.activation(lt[:, b, :], ps_l[0:E, :], ACT.Copy).then_inc(lt_kept, 1)
            act.wait_ge(shifted, 1)
            act.activation(lg[:], lg[:], ACT.Exp).then_inc(exps_done, 1)
            act.wait_ge(expert_in[0], 16)
            act.activation(keep.wh[0][:], keep.raw[0][:], ACT.Copy).then_inc(expert_high, 1)

        @block.vector
        def _(dve):
            chain = Chain(dve, steps)
            dve.wait_ge(high_done, 2)
            dve.tensor_tensor(wol[:], wo[:], woh[:].bitcast(F32), ALU.subtract).then_inc(low_done, 1)
            dve.tensor_tensor(wrl[:], wr[:], wrh[:].bitcast(F32), ALU.subtract).then_inc(low_done, 1)
            with dve.Fori(0, NC // 2) as i:
                for b in range(2):
                    dve.wait_ge(ah_done, i * 2 + (b + 1))
                    for k in range(KC):
                        last = dve.tensor_tensor(al[b][:, k, :], ps_t[b][k][:], ah[b][:, k, :].bitcast(F32), ALU.subtract)
                    last.then_inc(al_done, 1)
                for q in range(4):
                    dve.wait_ge(joined, i * 4 + (q + 1))
                    yt = y[:, bass.ds(i * 8 + 2 * q, 2), :]
                    dve.tensor_tensor(yt, yt, ps_y[q % 2][:].rearrange("p (t f) -> p t f", t=2), ALU.add).then_inc(y2_done, 1)
            dve.wait_ge(sq_done, NT // 2)
            dve.tensor_scalar(var[:], sq[:], 1.0 / C, 1e-6, ALU.mult, ALU.add).then_inc(ms_done, 1)
            inverse_root(chain, var[:], root[:], r2[:], tmp[:], root_done, 1)
            def normalise(c):
                tiles = slice(c * TPC, (c + 1) * TPC)
                dve.tensor_tensor(hn[:, tiles, :], y[:, tiles, :], spread(r2[:, tiles], 2, C), ALU.mult).then_inc(hn_done, 1)
            def keep_scores(c):
                dve.wait_ge(lt_turned, c + 1)
                dve.tensor_copy(lg[:, c * TPC:(c + 1) * TPC, :], ps_g[:, 0:TPC * E].rearrange("p (t e) -> p t e", e=E)).then_inc(lg_kept, 1)
            normalise(0)
            for c in range(NC):
                if c + 1 < NC:
                    normalise(c + 1)
                dve.wait_ge(h2h_done, c + 1)
                for k in range(KC):
                    last = dve.scalar_tensor_tensor(al[c % 2][:, k, :], ps_t[c % 2][k][:], ln2[:, k:k + 1], ah[c % 2][:, k, :].bitcast(F32),
                                                    ALU.mult, ALU.subtract)
                last.then_inc(h2l_done, 1)
                if c >= 2:
                    keep_scores(c - 2)
            keep_scores(NC - 2)
            keep_scores(NC - 1)
            dve.wait_ge(lg_kept, NC)
            chain.step(dve.tensor_reduce(one[:], lg[:], AX.X, ALU.max))
            dve.tensor_tensor(lg[:], lg[:], spread(one[:], 2, E), ALU.subtract).then_inc(shifted, 1)
            dve.wait_ge(exps_done, 1)
            chain.step(dve.tensor_reduce(one[:], lg[:], AX.X, ALU.add))
            chain.step(dve.reciprocal(one[:], one[:]))
            chain.step(dve.tensor_tensor(lg[:], lg[:], spread(one[:], 2, E), ALU.mult))
            def choose(out):
                chain.step(dve.tensor_reduce(top[:], w8[:], AX.X, ALU.max))
                chain.step(dve.tensor_tensor(pick[:], w8[:], spread(top[:], 2, E), ALU.is_equal))
                chain.step(dve.tensor_tensor(pick[:], pick[:], spread(plan[:, RANK], 1, NT), ALU.mult))
                chain.step(dve.tensor_reduce(one[:], pick[:], AX.X, ALU.max))
                chain.step(dve.tensor_tensor(out[:], spread(one[:], 2, E), spread(plan[:, RANK], 1, NT), ALU.is_equal))
            chain.step(dve.tensor_copy(w8[:], lg[:]))
            choose(first)
            chain.step(dve.scalar_tensor_tensor(w8[:], first[:], -2.0, w8[:], ALU.mult, ALU.add))
            choose(second)
            chain.step(dve.tensor_tensor(pick[:], second[:], first[:], ALU.add))
            dve.tensor_copy(chosen[:], pick[:]).then_inc(chosen_done, 1)
            chain.step(dve.tensor_tensor(w8[:], lg[:], pick[:], ALU.mult))
            dve.wait_ge(counted, 1)
            chain.step(dve.tensor_copy(of_tile[:].rearrange("p t e -> p (t e)"), ps_g[:, 0:NT * E]))
            old = of_tile
            for n in range(NT.bit_length() - 1):
                new, far = upto[n % 2], 1 << n
                chain.step(dve.tensor_copy(new[:, 0:far, :], old[:, 0:far, :]))
                chain.step(dve.tensor_tensor(new[:, far:, :], old[:, far:, :], old[:, 0:NT - far, :], ALU.add))
                old = new
            count = old[:, NT - 1, :]
            chain.step(dve.tensor_tensor(over[:], spread(count, 2, NC), spread(plan[:, EDGES], 1, E), ALU.is_gt))
            chain.step(dve.tensor_reduce(slots[:], over[:], AX.X, ALU.add))
            chain.step(dve.tensor_tensor(sums[:], spread(slots[:], 1, E), plan[:, UPTO].rearrange("p (a b) -> p a b", b=E), ALU.mult))
            chain.step(dve.tensor_reduce(end[:], sums[:], AX.X, ALU.add))
            chain.step(dve.tensor_tensor(ended[:], spread(end[:], 1, SLOTS), spread(plan[:, SLOT], 2, E), ALU.is_le))
            chain.step(dve.tensor_reduce(owner[:], ended[:], AX.X, ALU.add))
            chain.step(dve.tensor_scalar(owner[:], owner[:], E - 1.0, float(P), ALU.min, ALU.mult))
            dve.tensor_tensor(keep.owner_row[:], owner[:], plan[:, ROW].to_broadcast([P, SLOTS]), ALU.add).then_inc(owners_done, 1)
            chain.step(dve.tensor_tensor(end[:], end[:], slots[:], ALU.subtract))
            chain.step(dve.scalar_tensor_tensor(old[:], spread(end[:], 1, NT), float(CH), old[:], ALU.mult, ALU.add))
            chain.step(dve.tensor_tensor(old[:], old[:], of_tile[:], ALU.subtract))
            chain.step(dve.tensor_tensor(old[:].rearrange("p t e -> p (t e)"), old[:].rearrange("p t e -> p (t e)"), ps_l[:, 0:NT * E], ALU.add))
            for r, mine in enumerate((first, second)):
                chain.step(dve.tensor_tensor(pick[:], old[:], mine[:], ALU.mult))
                chain.step(dve.tensor_reduce(place[:], pick[:], AX.X, ALU.add))
                dve.tensor_copy(keep.place[:, r, :], place[:]).then_inc(places_done, 1)
                dve.wait_ge(places_done, r + 1)
            chain.step(dve.tensor_reduce(one[:], w8[:], AX.X, ALU.add))
            chain.step(dve.tensor_scalar(one[:], one[:], 1e-9, None, ALU.add))
            chain.step(dve.reciprocal(one[:], one[:]))
            for r, mine in enumerate((first, second)):
                chain.step(dve.tensor_tensor(pick[:], lg[:], mine[:], ALU.mult))
                chain.step(dve.tensor_reduce(top[:], pick[:], AX.X, ALU.add))
                chain.step(dve.tensor_tensor(keep.share[:, r, :], top[:], one[:], ALU.mult))
            dve.wait_ge(expert_high, 1)
            dve.tensor_tensor(keep.wl[0][:], keep.raw[0][:], keep.wh[0][:].bitcast(F32), ALU.subtract).then_inc(expert_low, 1)


def gather_expert(pool, io, keep, slot):
    return pool.indirect_dma_start(keep.raw[slot % 2][:], None, io["w_experts"],
                                   bass.IndirectOffsetOnAxis(keep.owner_row[:, slot:slot + 1], 0))


def experts(nc, io, keep):
    PIECE = EW // PIECES
    TURN_AT = MT - 3
    with ExitStack() as ctx:
        m = Pool(nc, ctx)
        ident = m.sb("ex_ident", [P, P])
        ln2 = m.sb("ex_ln2", [P, KC])
        rows = [m.sb(f"ex_rows{b}", [P, TPC, C]) for b in range(2)]
        xh = [m.sb(f"ex_xh{b}", [P, KC, CH], F32R) for b in range(2)]
        xl = [m.sb(f"ex_xl{b}", [P, KC, CH], F32R) for b in range(2)]
        silu = [m.sb(f"ex_silu{b}", [P, CH]) for b in range(2)]
        prod = [m.sb(f"ex_prod{b}", [P, CH]) for b in range(2)]
        ph = [m.sb(f"ex_ph{b}", [P, CH], F32R) for b in range(3)]
        pl = [m.sb(f"ex_pl{b}", [P, CH], F32R) for b in range(3)]
        out = [m.sb(f"ex_out{b}", [P, TPC, C]) for b in range(2)]
        ps_g = [m.bank(f"ex_ps_g{b}") for b in range(2)]
        ps_u = [m.bank(f"ex_ps_u{b}") for b in range(2)]
        ps_o = [m.bank(f"ex_ps_o{b}") for b in range(TPC)]
        loaded = m.sem("ex_loaded")
        rows_in = [m.sem(f"ex_rows_in{b}") for b in range(2)]
        turned = m.sem("ex_turned")
        xh_done = m.sem("ex_xh_done")
        xl_done = m.sem("ex_xl_done")
        expert_in = [m.sem(f"ex_expert_in{b}") for b in range(2)]
        high_split = m.sem("ex_high_split")
        low_split = m.sem("ex_low_split")
        up_done = m.sem("ex_up_done")
        silu_done = m.sem("ex_silu_done")
        prod_done = m.sem("ex_prod_done")
        ph_done = m.sem("ex_ph_done")
        pl_done = m.sem("ex_pl_done")
        used = m.sem("ex_used")
        out_act = m.sem("ex_out_act")
        out_dve = m.sem("ex_out_dve")
        stored = [m.sem(f"ex_stored{b}") for b in range(2)]
        block = ctx.enter_context(nc.Block())
        assert MT % 2 == 0 and MT % 3 == 0
        assert SLOTS % 2 == 1

        def tall(mt):
            return P if mt < MF else MR

        def run(eng, slot):
            with eng.Fori(0, SLOTS // 2) as pair:
                for b in range(2):
                    slot(pair * 2 + b, b, pair, False)
            slot(SLOTS - 1, 0, SLOTS // 2, True)

        @block.sync
        def _(sp):
            def load(s, b):
                sp.dma_start(rows[b][:], io["sorted_rows"][bass.ds(s * CH, CH), :].rearrange("(t p) f -> p t f", p=P)).then_inc(rows_in[b], 16)

            def slot(s, b, pair, last):
                if not last:
                    sp.wait_ge(turned, s * KC)
                    load(s + 1, 1 - b)
                sp.wait_ge(out_act, s * 2 + 2)
                sp.wait_ge(out_dve, s * 2 + 2)
                sp.dma_start(io["expert_rows"][bass.ds(s * CH, CH), :].rearrange("(t p) f -> p t f", p=P), out[b][:]).then_inc(stored[b], 16)

            sp.dma_start(ident[:], io["ident"]).then_inc(loaded, 16)
            sp.dma_start(ln2[:], io["ln2"]).then_inc(loaded, 16)
            load(0, 0)
            run(sp, slot)
            sp.wait_ge(stored[0], 16 * (SLOTS // 2 + 1))
            sp.wait_ge(stored[1], 16 * (SLOTS // 2))

        @block.gpsimd
        def _(pool):
            for s in range(2, SLOTS):
                pool.wait_ge(low_split, (s - 2) * PIECES)
                if s >= 4:
                    pool.wait_ge(expert_in[s % 2], 16 * (s // 2 - 1))
                gather_expert(pool, io, keep, s).then_inc(expert_in[s % 2], 16)

        @block.tensor
        def _(pe):
            def turn(s, b, pair, k):
                if k == 0:
                    pe.wait_ge(rows_in[b], pair * 16 + 16)
                else:
                    pe.wait_ge(xl_done, s * KC + k)
                for it in range(TPC):
                    last = pe.transpose(ps_u[1][:, it * P:(it + 1) * P], rows[b][:, it, k * P:(k + 1) * P], ident[:])
                last.then_inc(turned, 1)

            def up(b, mt):
                if mt < MF:
                    parts = ((ps_g[mt % 2][:], mt * 2 * P, P), (ps_u[mt % 2][:], (mt * 2 + 1) * P, P))
                else:
                    parts = ((ps_g[mt % 2][0:64 + MR, :], mt * 2 * P, 64 + MR),)
                for ps, at, cols in parts:
                    last = products(pe, ps, [(keep.wh[b][:, k * UPW + at:k * UPW + at + cols],
                                              keep.wl[b][:, k * UPW + at:k * UPW + at + cols]) for k in range(KC)],
                                    [(xh[b][:, k, :], xl[b][:, k, :]) for k in range(KC)])
                last.then_inc(up_done, 1)

            def down(b, mt):
                n, at = tall(mt), KC * UPW + mt * C
                for it in range(TPC):
                    tok = slice(it * P, (it + 1) * P)
                    last = products(pe, ps_o[it][:, 0:C], [(ph[mt % 3][0:n, tok], pl[mt % 3][0:n, tok])],
                                    [(keep.wh[b][0:n, at:at + C], keep.wl[b][0:n, at:at + C])], start=mt == 0, stop=mt == MT - 1)
                last.then_inc(used, 1)

            def slot(s, b, pair, last):
                for mt in range(MT):
                    if mt + 1 < MT:
                        pe.wait_ge(prod_done, s * MT + mt)
                        up(b, mt + 1)
                    elif not last:
                        pe.wait_ge(low_split, s * PIECES + PIECES)
                        pe.wait_ge(xl_done, s * KC + 2 * KC)
                        pe.wait_ge(prod_done, s * MT + mt)
                        up(1 - b, 0)
                    if mt == TURN_AT and not last:
                        pe.wait_ge(prod_done, s * MT + (mt + 1))
                        turn(s + 1, 1 - b, pair + b, 0)
                    if mt == 0:
                        pe.wait_ge(out_act, s * 2)
                        pe.wait_ge(out_dve, s * 2)
                    pe.wait_ge(pl_done, s * MT + (mt + 1))
                    down(b, mt)
                    if mt == TURN_AT and not last:
                        turn(s + 1, 1 - b, pair + b, 1)

            pe.wait_ge(loaded, 32)
            for k in range(KC):
                turn(0, 0, 0, k)
            pe.wait_ge(xl_done, KC)
            up(0, 0)
            run(pe, slot)

        @block.scalar
        def _(act):
            def hidden(base, mt):
                act.wait_ge(up_done, base + (mt + 1))
                if mt < MF:
                    act.activation(silu[mt % 2][:], ps_g[mt % 2][:], ACT.Silu).then_inc(silu_done, 1)
                else:
                    act.activation(silu[mt % 2][64:64 + MR, :], ps_g[mt % 2][0:MR, :], ACT.Silu).then_inc(silu_done, 1)
                act.wait_ge(prod_done, base + (mt + 1))
                act.activation(ph[mt % 3][0:tall(mt), :], prod[mt % 2][0:tall(mt), :], ACT.Copy).then_inc(ph_done, 1)

            def split_rows(s, b, k):
                act.wait_ge(turned, s * KC + (k + 1))
                act.activation(xh[b][:, k, :], ps_u[1][:], ACT.Copy, scale=ln2[:, k:k + 1]).then_inc(xh_done, 1)

            def slot(s, b, pair, last):
                for mt in range(MT):
                    if mt > 0:
                        hidden(s * MT, mt)
                    if mt < PIECES and not last:
                        if mt == 0:
                            act.wait_ge(used, s * MT)
                            act.wait_ge(expert_in[1 - b], pair * 16 + 16 * b)
                        at = slice(mt * PIECE, (mt + 1) * PIECE)
                        act.activation(keep.wh[1 - b][:, at], keep.raw[1 - b][:, at], ACT.Copy).then_inc(high_split, 1)
                    if mt == TURN_AT + 1 and not last:
                        for k in range(KC):
                            split_rows(s + 1, 1 - b, k)
                if not last:
                    hidden(s * MT + MT, 0)
                act.wait_ge(used, s * MT + MT)
                act.wait_ge(stored[b], pair * 16)
                for it in range(2):
                    act.activation(out[b][:, it, :], ps_o[it][:, 0:C], ACT.Copy).then_inc(out_act, 1)

            act.wait_ge(loaded, 32)
            for k in range(KC):
                split_rows(0, 0, k)
            hidden(0, 0)
            run(act, slot)

        @block.vector
        def _(dve):
            def hidden(base, mt):
                n = tall(mt)
                dve.wait_ge(silu_done, base + (mt + 1))
                if mt < MF:
                    dve.tensor_tensor(prod[mt % 2][:], silu[mt % 2][:], ps_u[mt % 2][:], ALU.mult).then_inc(prod_done, 1)
                else:
                    dve.tensor_tensor(prod[mt % 2][0:MR, :], silu[mt % 2][64:64 + MR, :], ps_g[mt % 2][64:64 + MR, :],
                                      ALU.mult).then_inc(prod_done, 1)
                dve.wait_ge(ph_done, base + (mt + 1))
                dve.tensor_tensor(pl[mt % 3][0:n, :], prod[mt % 2][0:n, :], ph[mt % 3][0:n, :].bitcast(F32),
                                  ALU.subtract).then_inc(pl_done, 1)

            def split_rows(s, b, k):
                dve.wait_ge(xh_done, s * KC + (k + 1))
                dve.scalar_tensor_tensor(xl[b][:, k, :], ps_u[1][:], ln2[:, k:k + 1], xh[b][:, k, :].bitcast(F32),
                                         ALU.mult, ALU.subtract).then_inc(xl_done, 1)

            def slot(s, b, pair, last):
                for mt in range(MT):
                    if mt > 0:
                        hidden(s * MT, mt)
                    if mt < PIECES and not last:
                        at = slice(mt * PIECE, (mt + 1) * PIECE)
                        dve.wait_ge(high_split, s * PIECES + (mt + 1))
                        dve.tensor_tensor(keep.wl[1 - b][:, at], keep.raw[1 - b][:, at], keep.wh[1 - b][:, at].bitcast(F32),
                                          ALU.subtract).then_inc(low_split, 1)
                    if mt == TURN_AT + 1 and not last:
                        for k in range(KC):
                            split_rows(s + 1, 1 - b, k)
                if not last:
                    hidden(s * MT + MT, 0)
                dve.wait_ge(used, s * MT + MT)
                dve.wait_ge(stored[b], pair * 16)
                for it in range(2, TPC):
                    dve.tensor_copy(out[b][:, it, :], ps_o[it][:, 0:C]).then_inc(out_dve, 1)

            for k in range(KC):
                split_rows(0, 0, k)
            hidden(0, 0)
            run(dve, slot)


def combine(nc, io, keep):
    RING = 4
    with ExitStack() as ctx:
        m = Pool(nc, ctx)
        y = keep.y
        got = [[m.sb(f"cb_got{b}{r}", [P, C]) for r in range(2)] for b in range(RING)]
        row_in = [[m.sem(f"cb_row_in{b}{r}") for r in range(2)] for b in range(RING)]
        half = m.sem("cb_half")
        added = m.sem("cb_added")
        stored = m.sem("cb_stored")
        block = ctx.enter_context(nc.Block())

        @block.gpsimd
        def _(pool):
            for t in range(NT):
                if t >= RING:
                    pool.wait_ge(added, t - RING + 1)
                for r in range(2):
                    pool.indirect_dma_start(got[t % RING][r][:], None, io["expert_rows"],
                                            bass.IndirectOffsetOnAxis(keep.place[:, r, t:t + 1], 0)).then_inc(row_in[t % RING][r], 16)

        @block.vector
        def _(dve):
            for t in range(NT):
                for r, done in enumerate((half, added)):
                    dve.wait_ge(row_in[t % RING][r], 16 * (t // RING + 1))
                    if r == 1:
                        dve.wait_ge(half, t + 1)
                    dve.scalar_tensor_tensor(y[:, t, :], got[t % RING][r][:], keep.share[:, r, t:t + 1], y[:, t, :],
                                             ALU.mult, ALU.add).then_inc(done, 1)

        @block.sync
        def _(sp):
            for c in range(NC):
                sp.wait_ge(added, (c + 1) * TPC)
                sp.dma_start(io["out"][c * CH:(c + 1) * CH, :].rearrange("(t p) f -> p t f", p=P), y[:, c * TPC:(c + 1) * TPC, :]).then_inc(stored, 16)
            sp.wait_ge(stored, 16 * NC)


class Keep:
    pass


def scratch(nc, io):
    for name, shape in (("s1_rows", [H, N]), ("x1", [N, C]), ("q_high", [C, N]), ("q_low", [C, N]), ("k_high", [KV * D, N]),
                        ("k_low", [KV * D, N]), ("va", [KV, P, NT, VW]), ("ya", [N, C]),
                        ("sorted_rows", [SLOTS * CH, C]), ("expert_rows", [SLOTS * CH, C])):
        if name not in io:
            io[name] = nc.dram_tensor(name, shape, F32, kind="Internal").ap()


def build(nc, io):
    scratch(nc, io)
    keep = Keep()
    with ExitStack() as ctx:
        g = Pool(nc, ctx)
        keep.s1 = g.sb("s1", [P, NT, H])
        keep.s2 = g.sb("s2", [P, NT, H])
        keep.e1 = g.sb("e1", [P, NT, H])
        keep.f1 = g.sb("f1", [P, NT, H])
        keep.mean = g.sb("mean_wh", [P, C])
        keep.ge = g.sb("ge", [P, NT * H, GW], BF16)
        keep.gf = g.sb("gf", [P, NT * H, GW], BF16)
        graph_prepare(nc, io, keep)
        graph_attention(nc, io, keep)
    keep = Keep()
    with ExitStack() as ctx:
        g = Pool(nc, ctx)
        keep.y = g.sb("y", [P, NT, C])
        project_qkv(nc, io, keep)
        sequence_attention(nc, io, keep)
        keep.place = g.sb("place", [P, 2, NT], U32)
        keep.share = g.sb("share", [P, 2, NT])
        keep.owner_row = g.sb("owner_row", [P, SLOTS], U32)
        keep.raw = [g.sb(f"expert_raw{b}", [P, EW]) for b in range(2)]
        keep.wh = [g.sb("expert_high0", [P, EW], F32R)]
        keep.wl = [g.sb("expert_low0", [P, EW], F32R)]
        join_and_route(nc, io, keep)
        keep.wh.append(g.sb("expert_high1", [P, EW], F32R))
        keep.wl.append(g.sb("expert_low1", [P, EW], F32R))
        experts(nc, io, keep)
        combine(nc, io, keep)


def lay_out(inputs):
    def given(name):
        return np.asarray(inputs[name])

    def turned(w):
        return w.reshape(C, -1, 2, D // 2)[:, :, ::-1, :].reshape(C, -1)

    w, a = given("L0_gnn_W"), given("L0_gnn_a")
    wq, wk, wv = (given("L0_ffn_" + n).T for n in ("wq", "wk", "wv"))
    w1, w2, w3 = (given("L0_ffn_" + n) for n in ("w1", "w2", "w3"))
    pieces = []
    for j in range(2):
        pieces += [wq[:, j * P:(j + 1) * P], turned(wq[:, j * P:(j + 1) * P])]
    pieces += [wk, turned(wk), wv]
    up = np.zeros((E, C, UPW), w1.dtype)
    for t in range(MF):
        rows = slice(t * P, (t + 1) * P)
        up[:, :, 2 * t * P:(2 * t + 1) * P] = w1[:, rows].transpose(0, 2, 1)
        up[:, :, (2 * t + 1) * P:(2 * t + 2) * P] = w3[:, rows].transpose(0, 2, 1)
    up[:, :, 2 * MF * P:2 * MF * P + MR] = w1[:, MF * P:].transpose(0, 2, 1)
    up[:, :, 2 * MF * P + 64:] = w3[:, MF * P:].transpose(0, 2, 1)
    down = np.zeros((E, MT * P, C), w2.dtype)
    down[:, :HID] = w2.transpose(0, 2, 1)
    w_experts = np.zeros((E, P, EW), w1.dtype)
    for k in range(KC):
        w_experts[:, :, k * UPW:(k + 1) * UPW] = up[:, k * P:(k + 1) * P]
    w_experts[:, :, KC * UPW:KC * UPW + MT * C] = down.reshape(E, MT, P, C).transpose(0, 2, 1, 3).reshape(E, P, MT * C)
    inv_freq = 1.0 / 10000.0 ** (np.arange(0, D, 2, dtype=np.float32) / D)
    freqs = np.outer(np.arange(N, dtype=np.float32), inv_freq)
    emb = np.concatenate([freqs, freqs], axis=-1)
    cos, sin = np.cos(emb).T, np.sin(emb).T
    sin = np.concatenate([-sin[:D // 2], sin[D // 2:]])
    trig = np.stack([np.tile(cos, (P // D, 1)), np.tile(sin, (P // D, 1))], axis=1).astype(np.float32)
    row = np.arange(P)
    plan = np.zeros((P, PLAN_COLS), np.float32)
    plan[:, RANK] = E - np.arange(E)
    plan[:, EDGES] = CH * np.arange(NC)
    plan[:, UPTO] = np.tril(np.ones((E, E))).reshape(1, E * E)
    plan[:, SLOT] = np.arange(SLOTS)
    plan[:, ROW] = row[:, None]
    arrays = {
        "x": given("x"),
        "adj": given("adj"),
        "w_cat": w.transpose(1, 0, 2).reshape(C, C),
        "w_t": w.transpose(0, 2, 1),
        "a_t": a.reshape(H, 2, D).transpose(2, 0, 1).reshape(D, 2 * H),
        "w_qkv": np.concatenate(pieces, axis=1),
        "ln1": given("L0_ffn_ln1_w").reshape(KC, P).T,
        "ln2": given("L0_ffn_ln2_w").reshape(KC, P).T,
        "w_o": given("L0_ffn_wo").T,
        "w_r": given("L0_ffn_router_w").T,
        "w_experts": w_experts.reshape(E * P, EW),
        "ident": np.eye(P, dtype=np.float32),
        "mean_of": np.full((P, P), 1.0 / N, np.float32),
        "sel": np.eye(DA, dtype=np.float32)[np.arange(GW) % DA],
        "trig": trig,
        "late_k": np.where(row[None, :] > row[:, None], -1e30, 0.0).astype(np.float32),
        "late_q": np.where(row[None, :] < row[:, None], -1e30, 0.0).astype(np.float32),
        "plan": plan,
        "before": np.triu(np.ones((P, P), np.float32), 1),
    }
    return {name: np.ascontiguousarray(value) for name, value in arrays.items()}


def kernel(**inputs):
    import concourse.bacc as bacc
    from concourse.bass_utils import run_bass_kernel_spmd

    nc = bacc.Bacc("TRN2", target_bir_lowering=False, num_devices=1)
    arrays = lay_out(inputs)
    io = {name: nc.dram_tensor(name, a.shape, mybir.dt.from_np(a.dtype), kind="ExternalInput").ap() for name, a in arrays.items()}
    io["out"] = nc.dram_tensor("out", [N, C], F32, kind="ExternalOutput").ap()
    build(nc, io)
    return run_bass_kernel_spmd(nc, [arrays], core_ids=[0]).results[0]["out"]
```

```python
from contextlib import ExitStack

import numpy as np

import concourse.bass as bass
from concourse import mybir

P = 128
N = 4096
C = 256
KC = C // P
NT = N // P
CH = 512
NC = N // CH
TPC = CH // P
H = 4
D = C // H
DA = D + 1
PARTS = 3
GW = PARTS * DA
KV = 2
VW = 2 * (D + 1)
QKW = 6 * P
E = 8
HID = 682
MF = HID // P
MR = HID - MF * P
UPW = MF * 2 * P + 64 + MR
MT = MF + 1
PIECES = MT - 1
EW = (KC * UPW + MT * C + PIECES - 1) // PIECES * PIECES
SLOTS = 2 * N // CH + E - 1
RANK = slice(0, E)
EDGES = slice(E, E + NC)
UPTO = slice(E + NC, E + NC + E * E)
SLOT = slice(E + NC + E * E, E + NC + E * E + SLOTS)
ROW = slice(E + NC + E * E + SLOTS, E + NC + E * E + SLOTS + 1)
PLAN_COLS = ROW.stop
SLOPE = 0.2

ALU = mybir.AluOpType
ACT = mybir.ActivationFunctionType
AX = mybir.AxisListType
F32 = mybir.dt.float32
BF16 = mybir.dt.bfloat16
U32 = mybir.dt.uint32
F32R = mybir.dt.float32r


class Pool:

    def __init__(self, nc, ctx):
        self.nc, self.ctx, self.sems = nc, ctx, []

    def sb(self, name, shape, dt=F32):
        return self.ctx.enter_context(self.nc.sbuf_tensor(name, shape, dt))

    def bank(self, name, dt=F32, banks=1):
        cols = banks * (512 if dt == F32 else 1024)
        return self.ctx.enter_context(self.nc.psum_tensor(name, [P, cols], dt))

    def sem(self, name):
        if not self.sems:
            self.ctx.callback(self.clear)
        self.sems.append(self.nc.alloc_semaphore(name=name))
        return self.sems[-1]

    def clear(self):
        self.nc.clear_and_free_semaphores(self.sems)
        self.nc.all_engine_barrier()


class Chain:

    def __init__(self, eng, sem):
        self.eng, self.sem, self.n = eng, sem, 0

    def step(self, ins):
        self.n += 1
        ins.then_inc(self.sem, 1)
        self.eng.wait_ge(self.sem, self.n)


def spread(ap, axis, count):
    ap = ap.unsqueeze(axis)
    shape = list(ap.shape)
    shape[axis] = count
    return ap.to_broadcast(shape)


def inverse_root(chain, v, root, y, t, roots_out, n):
    chain.eng.wait_ge(roots_out, n)
    chain.step(chain.eng.reciprocal(y, root))
    chain.step(chain.eng.tensor_tensor(t, y, y, ALU.mult))
    chain.step(chain.eng.tensor_tensor(t, t, v, ALU.mult))
    chain.step(chain.eng.tensor_scalar(t, t, -0.5, 1.5, ALU.mult, ALU.add))
    chain.step(chain.eng.tensor_tensor(y, y, t, ALU.mult))


def graph_prepare(nc, io, keep):
    with ExitStack() as ctx:
        m = Pool(nc, ctx)
        x = m.sb("gp_x", [P, NT, C])
        w = m.sb("gp_w", [P, KC, C + 2 * H])
        w_t = m.sb("gp_wt", [D, H, C])
        a_t = m.sb("gp_a", [D, 2 * H])
        ident = m.sb("gp_ident", [P, P])
        mean_of = m.sb("gp_ones", [P, P])
        st = m.sb("gp_stats", [P, NT, 6])
        mu = m.sb("gp_mu", [P, NT])
        var = m.sb("gp_var", [P, NT])
        tmp = m.sb("gp_tmp", [P, NT])
        root = m.sb("gp_root", [P, NT])
        rstd = m.sb("gp_rstd", [P, NT])
        xn = m.sb("gp_xn", [P, 2, C])
        xt = m.sb("gp_xt", [P, 2, KC, P])
        wh = m.sb("gp_wh", [P, NT, H, DA])
        rows = m.sb("gp_rows", [H, N])
        cm = m.sb("gp_cmax", [P, H])
        ca = m.sb("gp_call", [P, H])
        s2, s1 = keep.s2, keep.s1
        e2 = m.sb("gp_e2", [P, NT, H])
        f2 = m.sb("gp_f2", [P, NT, H])
        d2 = m.sb("gp_d2", [P, NT, H])
        u = m.sb("gp_u", [P, NT, H])
        u2 = m.sb("gp_u2", [P, NT, H])
        um = m.sb("gp_um", [P, NT, H])
        val = x[:].rearrange("p t f -> p (t f)")[:, 0:4 * TPC * H * DA].rearrange("p (n e a d) -> p n e a d", n=2, e=2, d=DA)
        ps_t = [m.bank(f"gp_ps_t{b}") for b in range(2)]
        ps_w = [m.bank(f"gp_ps_w{b}") for b in range(2)]
        ps_r = [m.bank(f"gp_ps_r{b}") for b in range(2)]
        ps_m = m.bank("gp_ps_m")

        loaded = m.sem("gp_loaded")
        x_in = [m.sem(f"gp_x_in{q}") for q in range(4)]
        wa_done = m.sem("gp_wa_done")
        wa_kept = m.sem("gp_wa_kept")
        dve_steps = m.sem("gp_dve_steps")
        set_up = m.sem("gp_set_up")
        stats_done = m.sem("gp_stats_done")
        var_done = m.sem("gp_var_done")
        root_done = m.sem("gp_root_done")
        xn_done = m.sem("gp_xn_done")
        xn_turned = m.sem("gp_xn_turned")
        xt_kept = m.sem("gp_xt_kept")
        wh_done = m.sem("gp_wh_done")
        rows_done = m.sem("gp_rows_done")
        wh_kept = m.sem("gp_wh_kept")
        rows_kept = m.sem("gp_rows_kept")
        scores_kept = m.sem("gp_scores_kept")
        summed = m.sem("gp_summed")
        mean_kept = m.sem("gp_mean_kept")
        max_done = m.sem("gp_max_done")
        all_max = m.sem("gp_all_max")
        exps_in = m.sem("gp_exps_in")
        exps_done = m.sem("gp_exps_done")
        val_done = m.sem("gp_val_done")
        hi_done = m.sem("gp_hi_done")
        rest_done = m.sem("gp_rest_done")
        mid_done = m.sem("gp_mid_done")
        lo_done = m.sem("gp_lo_done")
        stored = m.sem("gp_stored")
        block = ctx.enter_context(nc.Block())
        LOADS = 5

        def run(eng, pair):
            with eng.Fori(0, NT // 2 - 1) as i:
                pair(i, False)
            pair(NT // 2 - 1, True)

        @block.sync
        def _(sp):
            for q in range(4):
                sp.dma_start(x[:, 8 * q:8 * q + 8, :], io["x"].rearrange("(t p) f -> p t f", p=P)[:, 8 * q:8 * q + 8, :]).then_inc(x_in[q], 16)
            sp.dma_start(w[:, :, 0:C], io["w_cat"].rearrange("(k p) o -> p k o", p=P)).then_inc(loaded, 16)
            sp.dma_start(w_t[:], io["w_t"].rearrange("h o f -> o h f")).then_inc(loaded, 16)
            sp.dma_start(a_t[:], io["a_t"]).then_inc(loaded, 16)
            sp.dma_start(ident[:], io["ident"]).then_inc(loaded, 16)
            sp.dma_start(mean_of[:], io["mean_of"]).then_inc(loaded, 16)
            sp.wait_ge(rows_kept, NT)
            sp.dma_start(io["s1_rows"], rows[:]).then_inc(stored, 16)
            sp.wait_ge(stored, 16)

        @block.tensor
        def _(pe):
            pe.wait_ge(loaded, 16 * LOADS)
            for k in range(KC):
                for h in range(H):
                    for s in range(2):
                        col = k * 2 * H + (1 - s) * H + h
                        last = pe.matmul(ps_m[:, col:col + 1], w_t[:, h, k * P:(k + 1) * P],
                                         a_t[:, 2 * h + s:2 * h + s + 1], start=True, stop=True)
            last.then_inc(wa_done, 1)
            pe.wait_ge(wa_kept, 1)

            def turn(b, done, kept):
                pe.wait_ge(xn_done, done)
                if kept is not None:
                    pe.wait_ge(xt_kept, kept)
                for k in range(KC):
                    last = pe.transpose(ps_t[b][:, k * P:(k + 1) * P], xn[:, b, k * P:(k + 1) * P], ident[:])
                last.then_inc(xn_turned, 1)

            def pair(i, last_pair):
                if not last_pair:
                    for b in range(2):
                        turn(b, i * 2 + (b + 3), i * 2 + (b + 1))
                for b in range(2):
                    pe.wait_ge(xt_kept, i * 2 + (b + 1))
                    pe.wait_ge(wh_kept, i * 2)
                    pe.wait_ge(scores_kept, i * 2)
                    for k in range(KC):
                        last = pe.matmul(ps_w[b][:, 0:C + H * 2], xt[:, b, k, :], w[:, k, :], start=k == 0, stop=k == KC - 1)
                    last.then_inc(wh_done, 1)
                    pe.wait_ge(rows_kept, i * 2)
                    for k in range(KC):
                        last = pe.matmul(ps_r[b][0:H, 0:P], w[:, k, C + H:C + 2 * H], xt[:, b, k, :], start=k == 0, stop=k == KC - 1)
                    last.then_inc(rows_done, 1)

            for b in range(2):
                turn(b, b + 1, None)
            run(pe, pair)
            pe.wait_ge(wh_kept, NT)
            for t in range(NT):
                last = pe.matmul(ps_m[:, 0:C], mean_of[:], wh[:, t, :, 0:D], start=t == 0, stop=t == NT - 1)
            last.then_inc(summed, 1)

        @block.scalar
        def _(act):
            act.wait_ge(var_done, 1)
            act.activation(root[:], var[:], ACT.Sqrt).then_inc(root_done, 1)

            def keep_turned(b):
                act.activation(xt[:, b, :, :], ps_t[b][:, 0:C].rearrange("p (k n) -> p k n", k=KC), ACT.Copy).then_inc(xt_kept, 1)

            def pair(i, last):
                if not last:
                    for b in range(2):
                        act.wait_ge(xn_turned, i * 2 + (b + 3))
                        act.wait_ge(rows_done, i * 2 + (b + 1))
                        keep_turned(b)
                for b in range(2):
                    act.wait_ge(wh_done, i * 2 + (b + 1))
                    act.wait_ge(wh_kept, i * 2 + (b + 1))
                    act.activation(s2[:, bass.ds(i * 2 + b, 1), :], ps_w[b][:, C:C + H].unsqueeze(1), ACT.Copy)
                    act.activation(s1[:, bass.ds(i * 2 + b, 1), :], ps_w[b][:, C + H:C + 2 * H].unsqueeze(1), ACT.Copy).then_inc(scores_kept, 1)
                    act.wait_ge(rows_done, i * 2 + (b + 1))
                    act.activation(rows[:, bass.ds((i * 2 + b) * P, P)], ps_r[b][0:H, 0:P], ACT.Copy).then_inc(rows_kept, 1)

            for b in range(2):
                act.wait_ge(xn_turned, b + 1)
                keep_turned(b)
            run(act, pair)
            act.wait_ge(exps_in, 1)
            act.activation(e2[:], d2[:], ACT.Exp).then_inc(exps_done, 1)
            act.activation(f2[:], d2[:], ACT.Exp, scale=SLOPE).then_inc(exps_done, 1)
            act.wait_ge(exps_in, 3)
            act.activation(keep.e1[:], u[:], ACT.Exp).then_inc(exps_done, 1)
            act.activation(keep.f1[:], u2[:], ACT.Exp).then_inc(exps_done, 1)
            for n in range(NC):
                for e, g in enumerate((keep.ge, keep.gf)):
                    gv = g[:, n * TPC * H:(n + 1) * TPC * H, :]
                    act.wait_ge(val_done, n * 2 + (e + 1))
                    act.activation(gv[:, :, 0:DA], val[:, n % 2, e], ACT.Copy).then_inc(hi_done, 1)
                for e, g in enumerate((keep.ge, keep.gf)):
                    gv = g[:, n * TPC * H:(n + 1) * TPC * H, :]
                    act.wait_ge(rest_done, n * 2 + (e + 1))
                    act.activation(gv[:, :, DA:2 * DA], val[:, n % 2, e], ACT.Copy).then_inc(mid_done, 1)

        @block.gpsimd
        def _(pool):
            pool.memset(wh[:, :, :, D:DA], 1.0).then_inc(set_up, 1)
            pool.wait_ge(max_done, 1)
            pool.partition_all_reduce(ca[:], cm[:], P, bass.bass_isa.ReduceOp.max).then_inc(all_max, 1)
            pool.wait_ge(set_up, 1)
            pool.wait_ge(wh_kept, NT)
            pool.wait_ge(exps_done, 2)
            for n in range(NC):
                tiles = slice(n * TPC, (n + 1) * TPC)
                for e, f in enumerate((e2, f2)):
                    if n >= 2:
                        pool.wait_ge(lo_done, 2 * (n - 2) + (e + 1))
                    pool.tensor_tensor(val[:, n % 2, e], wh[:, tiles, :, :].rearrange("p t h d -> p (t h) d"),
                                       spread(f[:, tiles, :].rearrange("p t h -> p (t h)"), 2, DA), ALU.mult).then_inc(val_done, 1)

        @block.vector
        def _(dve):
            chain = Chain(dve, dve_steps)
            for n in range(NT):
                if n % 8 == 0:
                    dve.wait_ge(x_in[n // 8], 16)
                dve.bn_stats(st[:, n, :], x[:, n, :]).then_inc(stats_done, 1)
            dve.wait_ge(loaded, 16 * LOADS)
            dve.wait_ge(wa_done, 1)
            dve.tensor_copy(w[:, :, C:C + 2 * H], ps_m[:, 0:KC * 2 * H].rearrange("p (k c) -> p k c", k=KC)).then_inc(wa_kept, 1)
            dve.wait_ge(stats_done, NT)
            layer_norm_tail(chain, st, mu, var, tmp, var_done)
            inverse_root(chain, var[:], root[:], rstd[:], tmp[:], root_done, 1)

            def normalise(tile, b):
                dve.tensor_scalar(xn[:, b:b + 1, :], x[:, bass.ds(tile, 1), :], mu[:, bass.ds(tile, 1)], rstd[:, bass.ds(tile, 1)],
                                  ALU.subtract, ALU.mult).then_inc(xn_done, 1)

            def pair(i, last):
                if not last:
                    for b in range(2):
                        dve.wait_ge(xn_turned, i * 2 + (b + 1))
                        normalise(i * 2 + (b + 2), b)
                for b in range(2):
                    tile = i * 2 + b
                    dve.wait_ge(wh_done, tile + 1)
                    dve.tensor_copy(wh[:, bass.ds(tile, 1), :, 0:D].rearrange("p t h d -> p (t h) d"),
                                    ps_w[b][:, 0:C].rearrange("p (h d) -> p h d", h=H)).then_inc(wh_kept, 1)

            for b in range(2):
                normalise(b, b)
            run(dve, pair)
            dve.wait_ge(summed, 1)
            dve.tensor_copy(keep.mean[:], ps_m[:, 0:C]).then_inc(mean_kept, 1)
            dve.wait_ge(scores_kept, NT)
            dve.tensor_reduce(cm[:], s2[:].rearrange("p t h -> p h t"), AX.X, ALU.max).then_inc(max_done, 1)
            dve.wait_ge(all_max, 1)
            dve.tensor_tensor(d2[:], s2[:], spread(ca[:], 1, NT), ALU.subtract).then_inc(exps_in, 1)
            chain.step(dve.tensor_tensor(u[:], s1[:], spread(ca[:], 1, NT), ALU.add))
            chain.step(dve.scalar_tensor_tensor(um[:], u[:], SLOPE, u[:], ALU.mult, ALU.max))
            chain.step(dve.scalar_tensor_tensor(u2[:], u[:], SLOPE, um[:], ALU.mult, ALU.subtract))
            dve.tensor_tensor(u[:], u[:], um[:], ALU.subtract).then_inc(exps_in, 2)
            for n in range(NC):
                for e, g in enumerate((keep.ge, keep.gf)):
                    gv = g[:, n * TPC * H:(n + 1) * TPC * H, :]
                    dve.wait_ge(hi_done, n * 2 + (e + 1))
                    dve.tensor_tensor(val[:, n % 2, e], val[:, n % 2, e], gv[:, :, 0:DA], ALU.subtract).then_inc(rest_done, 1)
                for e, g in enumerate((keep.ge, keep.gf)):
                    gv = g[:, n * TPC * H:(n + 1) * TPC * H, :]
                    dve.wait_ge(mid_done, n * 2 + (e + 1))
                    dve.tensor_tensor(gv[:, :, 2 * DA:3 * DA], val[:, n % 2, e], gv[:, :, DA:2 * DA], ALU.subtract).then_inc(lo_done, 1)


def layer_norm_tail(chain, st, mu, var, tmp, var_done, raw_var=None):
    dve = chain.eng
    chain.step(dve.tensor_tensor(mu[:], st[:, :, 1], st[:, :, 4], ALU.add))
    chain.step(dve.tensor_scalar(mu[:], mu[:], 0.5, None, ALU.mult))
    chain.step(dve.tensor_tensor(tmp[:], st[:, :, 1], st[:, :, 4], ALU.subtract))
    chain.step(dve.tensor_tensor(tmp[:], tmp[:], tmp[:], ALU.mult))
    chain.step(dve.tensor_tensor(var[:], st[:, :, 2], st[:, :, 5], ALU.add))
    chain.step(dve.tensor_scalar(var[:], var[:], 1.0 / C, None, ALU.mult))
    chain.step(dve.scalar_tensor_tensor(var[:], tmp[:], 0.25, var[:], ALU.mult, ALU.add))
    if raw_var is not None:
        chain.step(dve.tensor_copy(raw_var[:], var[:]))
    dve.tensor_scalar(var[:], var[:], 1e-5, None, ALU.add).then_inc(var_done, 1)


def graph_attention(nc, io, keep):
    QJ = N // 4
    NP2 = NT // 2
    STEPS = H * NP2
    MASKS = 4
    AHEAD = TPC
    with ExitStack() as ctx:
        m = Pool(nc, ctx)
        nat = m.sb("ga_nat", [P, 4, TPC, QJ], BF16)
        no_edge = m.sb("ga_no_edge", [P, NT, CH], BF16)
        identb = m.sb("ga_identb", [P, P], BF16)
        s1b = m.sb("ga_s1b", [P, H, CH])
        sign = m.sb("ga_sign", [P, 2, 2, CH], BF16)
        pos = m.sb("ga_pos", [P, MASKS, 2, CH], BF16)
        neg = m.sb("ga_neg", [P, MASKS, 2, CH], BF16)
        out = m.sb("ga_out", [P, TPC, C])
        xr = m.sb("ga_xr", [P, TPC, C])
        te = m.sb("ga_te", [P, TPC, DA])
        tf = m.sb("ga_tf", [P, TPC, DA])
        lone = m.sb("ga_lone", [P, TPC, 1])
        den = m.sb("ga_den", [P, TPC, 1])
        acc = [m.bank(f"ga_acc{b}", F32, TPC) for b in range(2)]
        ps_t = [acc[1][:, b * 512:(b + 1) * 512].bitcast(BF16) for b in range(AHEAD)]

        cast_in = m.sem("ga_cast_in")
        adj_in = [m.sem(f"ga_adj_in{q}") for q in range(4)]
        rows_in = [m.sem(f"ga_rows_in{h}") for h in range(H)]
        x_in = m.sem("ga_x_in")
        turned = m.sem("ga_turned")
        no_edge_kept = [m.sem(f"ga_no_edge_kept{b}") for b in range(2)]
        signs = m.sem("ga_signs")
        pos_done = m.sem("ga_pos_done")
        neg_done = m.sem("ga_neg_done")
        mask_used = m.sem("ga_mask_used")
        sums_read = m.sem("ga_sums_read")
        steps = m.sem("ga_steps")
        stored = m.sem("ga_stored")
        block = ctx.enter_context(nc.Block())
        TAIL = 12
        COUNTED = TAIL - 1
        TAIL_AT = NP2 - TAIL

        @block.gpsimd
        def _(pool):
            pool.dma_start(identb[:], io["ident"]).then_inc(cast_in, 16)
            for q in range(4):
                pool.dma_start(nat[:, q], io["adj"][0:CH, q * QJ:(q + 1) * QJ].rearrange("(t p) j -> p t j", p=P)).then_inc(adj_in[q], 16)
            with pool.Fori(1, NC) as c:
                for q in range(4):
                    pool.wait_ge(turned, c * NP2 + ((q + 1) * (NP2 // 4) - NP2))
                    src = io["adj"][bass.ds(c * CH, CH), q * QJ:(q + 1) * QJ].rearrange("(t p) j -> p t j", p=P)
                    pool.dma_start(nat[:, q], src).then_inc(adj_in[q], 16)

        @block.sync
        def _(sp):
            def load_rows(c, h):
                sp.dma_start(s1b[:, h, :], io["s1_rows"][h, bass.ds(c * CH, CH)].partition_broadcast(P)).then_inc(rows_in[h], 16)

            def load_x(c):
                sp.dma_start(xr[:], io["x"][bass.ds(c * CH, CH), :].rearrange("(t p) f -> p t f", p=P)).then_inc(x_in, 16)

            def store(c):
                sp.wait_ge(steps, c * (H * COUNTED) + H * COUNTED)
                sp.dma_start(io["x1"][bass.ds(c * CH, CH), :].rearrange("(t p) f -> p t f", p=P), out[:]).then_inc(stored, 16)

            for h in range(H):
                load_rows(0, h)
            load_x(0)
            with sp.Fori(0, NC - 1) as c:
                for h in range(H):
                    sp.wait_ge(signs, c * STEPS + (h + 1) * NP2)
                    load_rows(c + 1, h)
                store(c)
                load_x(c + 1)
            store(NC - 1)
            sp.wait_ge(stored, 16 * NC)

        @block.tensor
        def _(pe):
            pe.wait_ge(cast_in, 16)
            with pe.Fori(0, NC) as c:
                def turn(n):
                    q, k, b = n // (NP2 // 4), n % (NP2 // 4), n % AHEAD
                    if k == 0:
                        pe.wait_ge(adj_in[q], c * 16 + 16)
                    if n >= AHEAD:
                        pe.wait_ge(no_edge_kept[n % 2], c * (NP2 // 2) + (n - AHEAD) // 2 + 1)
                    for j in range(2):
                        for it in range(TPC):
                            last = pe.transpose(ps_t[b][:, j * CH + it * P:j * CH + (it + 1) * P],
                                                nat[:, q, it, (2 * k + j) * P:(2 * k + j + 1) * P], identb[:])
                    last.then_inc(turned, 1)

                pe.wait_ge(sums_read, c * H)
                for n in range(AHEAD):
                    turn(n)
                for h in range(H):
                    if h == 1:
                        for b in range(2):
                            pe.wait_ge(no_edge_kept[b], c * (NP2 // 2) + NP2 // 2)
                    if h > 1:
                        pe.wait_ge(sums_read, c * H + (h - 1))
                    for n in range(NP2):
                        if h == 0 and n + AHEAD < NP2:
                            turn(n + AHEAD)
                        step = h * NP2 + n
                        for r, (mask, ready, g) in enumerate(((pos, pos_done, keep.ge), (neg, neg_done, keep.gf))):
                            pe.wait_ge(ready, c * STEPS + (step + 1))
                            for j in range(2):
                                jt = 2 * n + j
                                for it in range(TPC):
                                    last = pe.matmul(acc[h % 2][:, it * 512 + r * GW:it * 512 + (r + 1) * GW],
                                                     mask[:, step % MASKS, j, it * P:(it + 1) * P], g[:, jt * H + h, :],
                                                     start=jt == 0 and r == 0, stop=jt == NT - 1, skip_group_check=True)
                        last.then_inc(mask_used, 1)

        @block.scalar
        def _(act):
            with act.Fori(0, NC) as c:
                def keep_edges(n):
                    act.wait_ge(turned, c * NP2 + (n + 1))
                    if n == 0:
                        act.wait_ge(neg_done, c * STEPS)
                    act.activation(no_edge[:, 2 * n:2 * n + 2, :], ps_t[n % AHEAD].rearrange("p (j i) -> p j i", j=2), ACT.Relu,
                                   scale=-1.0, bias=1.0).then_inc(no_edge_kept[0], 1)

                keep_edges(0)
                for h in range(H):
                    act.wait_ge(rows_in[h], c * 16 + 16)
                    for n in range(NP2):
                        step = h * NP2 + n
                        act.wait_ge(pos_done, c * STEPS + max(0, step - 1))
                        for j in range(2):
                            last = act.activation(sign[:, n % 2, j, :], s1b[:, h, :], ACT.Sign, bias=keep.s2[:, 2 * n + j, h:h + 1])
                        last.then_inc(signs, 1)
                        if h == 0 and n % 2 == 0 and n + 2 < NP2:
                            keep_edges(n + 2)

        @block.vector
        def _(dve):
            with dve.Fori(0, NC) as c:
                def keep_edges(n):
                    dve.wait_ge(turned, c * NP2 + (n + 1))
                    dve.tensor_scalar(no_edge[:, 2 * n:2 * n + 2, :], ps_t[n % AHEAD].rearrange("p (j i) -> p j i", j=2), 0.0, None,
                                      ALU.is_le).then_inc(no_edge_kept[1], 1)

                def tail(h, k):
                    parts = acc[h % 2][:].rearrange("p (i c) -> p i c", i=TPC)
                    def sum_of(r):
                        return parts[:, :, r * GW:(r + 1) * GW].rearrange("p i (r d) -> p i d r", r=PARTS)
                    def by(f):
                        return spread(f[:, bass.ds(c * TPC, TPC), h], 2, DA)
                    cols = slice(h * D, (h + 1) * D)
                    done = h * COUNTED + (k if k < 2 else k - 1)
                    if done > 0:
                        dve.wait_ge(steps, c * (H * COUNTED) + done)
                    if k == 2:
                        dve.wait_ge(sums_read, c * H + (h + 1))
                    if k == 0:
                        dve.wait_ge(mask_used, c * STEPS + (h + 1) * NP2)
                        ins = dve.tensor_reduce(te[:], sum_of(0), AX.X, ALU.add)
                    elif k == 1:
                        ins = dve.tensor_reduce(tf[:], sum_of(1), AX.X, ALU.add)
                    elif k == 2:
                        ins = dve.tensor_tensor(te[:], te[:], by(keep.e1), ALU.mult)
                    elif k == 3:
                        ins = dve.tensor_tensor(tf[:], tf[:], by(keep.f1), ALU.mult)
                    elif k == 4:
                        ins = dve.tensor_tensor(te[:], te[:], tf[:], ALU.add)
                    elif k == 5:
                        ins = dve.tensor_scalar(lone[:], te[:, :, D:DA], 0.0, None, ALU.is_equal)
                    elif k == 6:
                        ins = dve.tensor_tensor(den[:], te[:, :, D:DA], lone[:], ALU.add)
                    elif k == 7:
                        ins = dve.reciprocal(den[:], den[:])
                    elif k == 8:
                        ins = dve.tensor_tensor(te[:, :, 0:D], te[:, :, 0:D], den[:].to_broadcast([P, TPC, D]), ALU.mult)
                    elif k == 9:
                        ins = dve.tensor_tensor(tf[:, :, 0:D], lone[:].to_broadcast([P, TPC, D]), spread(keep.mean[:, cols], 1, TPC), ALU.mult)
                    elif k == 10:
                        ins = dve.tensor_tensor(te[:, :, 0:D], te[:, :, 0:D], tf[:, :, 0:D], ALU.add)
                    elif k == 11:
                        if h == 0:
                            dve.wait_ge(x_in, c * 16 + 16)
                            dve.wait_ge(stored, c * 16)
                        ins = dve.tensor_tensor(out[:, :, cols], te[:, :, 0:D], xr[:, :, cols], ALU.add)
                    ins.then_inc(sums_read if k == 1 else steps, 1)

                def flat(tile):
                    return tile.rearrange("p j i -> p (j i)")

                def make_pos(step):
                    n = step % NP2
                    dve.wait_ge(signs, c * STEPS + (step + 1))
                    if step < NP2:
                        dve.wait_ge(no_edge_kept[n % 2], c * (NP2 // 2) + (n // 2 + 1))
                    dve.wait_ge(mask_used, c * STEPS + max(0, step + 1 - MASKS))
                    dve.tensor_tensor(flat(pos[:, step % MASKS]), flat(sign[:, n % 2]), flat(no_edge[:, 2 * n:2 * n + 2, :]),
                                      ALU.is_gt).then_inc(pos_done, 1)

                def make_neg(step):
                    n = step % NP2
                    dve.wait_ge(pos_done, c * STEPS + (step + 1))
                    dve.tensor_tensor(flat(neg[:, step % MASKS]), flat(pos[:, step % MASKS]), flat(no_edge[:, 2 * n:2 * n + 2, :]),
                                      ALU.is_equal).then_inc(neg_done, 1)

                keep_edges(1)
                make_pos(0)
                for h in range(H):
                    for n in range(NP2):
                        if h * NP2 + n + 1 < STEPS:
                            make_pos(h * NP2 + n + 1)
                        make_neg(h * NP2 + n)
                        if h == 0 and n % 2 == 1 and n + 2 < NP2:
                            keep_edges(n + 2)
                        if h > 0 and n >= TAIL_AT:
                            tail(h - 1, n - TAIL_AT)
                for k in range(TAIL):
                    tail(H - 1, k)


def products(pe, out, lhs, rhs, start=True, stop=True, shared=False):
    n = len(lhs)
    for k in range(n):
        (lh, ll), (rh, rl) = lhs[k], rhs[k]
        pe.matmul(out, lh, rh, start=start and k == 0, stop=False, skip_group_check=shared)
        pe.matmul(out, lh, rl, start=False, stop=False, skip_group_check=shared)
        last = pe.matmul(out, ll, rh, start=False, stop=stop and k == n - 1, skip_group_check=shared)
    return last


def project_qkv(nc, io, keep):
    with ExitStack() as ctx:
        m = Pool(nc, ctx)
        y = keep.y
        va = m.sb("pq_va", [P, NT, KV, VW], F32R)
        raw = m.sb("pq_raw", [P, KC, QKW + P])
        wh = m.sb("pq_wh", [P, KC, QKW + P], F32R)
        wl = m.sb("pq_wl", [P, KC, QKW + P], F32R)
        ln1 = m.sb("pq_ln1", [P, KC])
        ident = m.sb("pq_ident", [P, P])
        trig = [m.sb(f"pq_trig{b}", [P, 2, CH]) for b in range(2)]
        st = m.sb("pq_stats", [P, NT, 6])
        mu = m.sb("pq_mu", [P, NT])
        var = m.sb("pq_var", [P, NT])
        tmp = m.sb("pq_tmp", [P, NT])
        root = m.sb("pq_root", [P, NT])
        rstd = m.sb("pq_rstd", [P, NT])
        mean_square = m.sb("pq_mean_square", [P, NT])
        hn = m.sb("pq_hn", [P, TPC, C])
        hh = [m.sb(f"pq_hh{b}", [P, KC, CH], F32R) for b in range(2)]
        hl = [m.sb(f"pq_hl{b}", [P, KC, CH], F32R) for b in range(2)]
        ta = m.sb("pq_ta", [P, 3, CH])
        tb = m.sb("pq_tb", [P, 3, CH])
        rh = [m.sb(f"pq_rh{b}", [P, 3, CH], F32R) for b in range(2)]
        rl = [m.sb(f"pq_rl{b}", [P, 3, CH], F32R) for b in range(2)]
        ps_t = [m.bank(f"pq_ps_t{k}") for k in range(KC)]
        ps_a = [m.bank(f"pq_ps_a{b}") for b in range(2)]
        ps_b = [m.bank(f"pq_ps_b{b}") for b in range(2)]
        ps_v = m.bank("pq_ps_v")
        loaded = m.sem("pq_loaded")
        x1_in = [m.sem(f"pq_x1_in{q}") for q in range(4)]
        trig_in = [m.sem(f"pq_trig_in{b}") for b in range(2)]
        wh_done = m.sem("pq_wh_done")
        wl_done = m.sem("pq_wl_done")
        dve_steps = m.sem("pq_dve_steps")
        stats_done = m.sem("pq_stats_done")
        var_done = m.sem("pq_var_done")
        root_done = m.sem("pq_root_done")
        y_done = m.sem("pq_y_done")
        ms_done = m.sem("pq_ms_done")
        root2_done = m.sem("pq_root2_done")
        hn_done = m.sem("pq_hn_done")
        turned = m.sem("pq_turned")
        hh_done = m.sem("pq_hh_done")
        hl_done = m.sem("pq_hl_done")
        pair_done = m.sem("pq_pair_done")
        v_done = m.sem("pq_v_done")
        ta_done = m.sem("pq_ta_done")
        tb_done = m.sem("pq_tb_done")
        rope_done = m.sem("pq_rope_done")
        rh_done = m.sem("pq_rh_done")
        rl_done = m.sem("pq_rl_done")
        vh_done = m.sem("pq_vh_done")
        vl_done = m.sem("pq_vl_done")
        ones_set = m.sem("pq_ones_set")
        moved = [m.sem(f"pq_moved{b}") for b in range(2)]
        stored = m.sem("pq_stored")
        block = ctx.enter_context(nc.Block())
        LOADS = 3
        MOVES = 6

        def run(eng, chunk):
            with eng.Fori(0, NC // 2 - 1) as pair:
                for b in range(2):
                    chunk(pair * 2 + b, b, pair, False)
            for b in range(2):
                chunk(NC - 2 + b, b, NC // 2 - 1, b == 1)

        @block.sync
        def _(sp):
            def load_trig(c, b):
                sp.dma_start(trig[b][:], io["trig"][:, :, bass.ds(c * CH, CH)]).then_inc(trig_in[b], 16)

            def chunk(c, b, pair, last):
                if not last:
                    sp.wait_ge(tb_done, c * 3)
                    sp.wait_ge(ta_done, c * 3)
                    load_trig(c + 1, 1 - b)
                at = bass.ds(c * CH, CH)
                for j in range(3):
                    sp.wait_ge(rh_done, c * 3 + (j + 1))
                    sp.wait_ge(rl_done, c * 3 + (j + 1))
                    to, row = ("q", j * P) if j < 2 else ("k", 0)
                    sp.dma_start(io[to + "_high"][row:row + P, at], rh[b][:, j, :].bitcast(F32)).then_inc(moved[b], 16)
                    sp.dma_start(io[to + "_low"][row:row + P, at], rl[b][:, j, :].bitcast(F32)).then_inc(moved[b], 16)
                sp.wait_ge(vh_done, c + 1)
                sp.wait_ge(vl_done, c + 1)
                tiles = bass.ds(c * TPC, TPC)
                for g in range(KV):
                    sp.dma_start(io["va"][g, :, tiles, :], va[:, tiles, g, :].bitcast(F32)).then_inc(stored, 16)

            for q in range(4):
                sp.dma_start(y[:, 8 * q:8 * q + 8, :], io["x1"].rearrange("(t p) f -> p t f", p=P)[:, 8 * q:8 * q + 8, :]).then_inc(x1_in[q], 16)
                if q == 0:
                    sp.dma_start(raw[:], io["w_qkv"].rearrange("(k p) o -> p k o", p=P)).then_inc(loaded, 16)
                    sp.dma_start(ln1[:], io["ln1"]).then_inc(loaded, 16)
                    sp.dma_start(ident[:], io["ident"]).then_inc(loaded, 16)
            load_trig(0, 0)
            sp.wait_ge(ones_set, 2)
            run(sp, chunk)
            for b in range(2):
                sp.wait_ge(moved[b], 16 * MOVES * (NC // 2))
            sp.wait_ge(stored, 16 * KV * NC)

        @block.gpsimd
        def _(pool):
            pool.memset(va[:, :, :, D:DA].bitcast(F32), 1.0).then_inc(ones_set, 1)
            pool.memset(va[:, :, :, DA + D:VW].bitcast(F32), 0.0).then_inc(ones_set, 1)
            pool.wait_ge(ones_set, 2)

        @block.scalar
        def _(act):
            def high_part(c, b):
                act.wait_ge(turned, c + 1)
                for k in range(KC):
                    act.activation(hh[b][:, k, :], ps_t[k][:], ACT.Copy, scale=ln1[:, k:k + 1]).then_inc(hh_done, 1)

            def chunk(c, b, pair, last):
                act.wait_ge(moved[b], pair * (16 * MOVES))
                for j in range(3):
                    if j == 2 and not last:
                        act.wait_ge(v_done, c)
                        high_part(c + 1, 1 - b)
                    act.wait_ge(rope_done, c * 3 + (j + 1))
                    act.activation(rh[b][:, j, :], ta[:, j, :], ACT.Copy).then_inc(rh_done, 1)
                act.wait_ge(v_done, c + 1)
                act.activation(va[:, bass.ds(c * TPC, TPC), :, 0:D].rearrange("p t g d -> p (t g) d"),
                               ps_v[:].rearrange("p (t g d) -> p (t g) d", g=KV, d=D), ACT.Copy).then_inc(vh_done, 1)

            act.wait_ge(loaded, 16 * LOADS)
            act.activation(wh[:], raw[:], ACT.Copy).then_inc(wh_done, 1)
            act.wait_ge(var_done, 1)
            act.activation(root[:], var[:], ACT.Sqrt).then_inc(root_done, 1)
            act.wait_ge(ms_done, 1)
            act.activation(root[:], mean_square[:], ACT.Sqrt).then_inc(root2_done, 1)
            high_part(0, 0)
            run(act, chunk)

        @block.tensor
        def _(pe):
            def turn(c):
                pe.wait_ge(hn_done, c * TPC + TPC)
                for k in range(KC):
                    for it in range(TPC):
                        last = pe.transpose(ps_t[k][:, it * P:(it + 1) * P], hn[:, it, k * P:(k + 1) * P], ident[:])
                last.then_inc(turned, 1)

            def chunk(c, b, pair, last_chunk):
                pe.wait_ge(hh_done, c * KC + KC)
                pe.wait_ge(hl_done, c * KC + KC)
                act_k = [(hh[b][:, k, :], hl[b][:, k, :]) for k in range(KC)]
                for j in range(3):
                    if j == 2 and not last_chunk:
                        turn(c + 1)
                    pe.wait_ge(tb_done, c * 3 + max(0, j - 1))
                    pe.wait_ge(ta_done, c * 3 + max(0, j - 1))
                    for s, ps in ((0, ps_a), (1, ps_b)):
                        col = slice((2 * j + s) * P, (2 * j + s + 1) * P)
                        last = products(pe, ps[j % 2][:], [(wh[:, k, col], wl[:, k, col]) for k in range(KC)], act_k)
                    last.then_inc(pair_done, 1)
                pe.wait_ge(vh_done, c)
                pe.wait_ge(vl_done, c)
                for it in range(TPC):
                    tok = slice(it * P, (it + 1) * P)
                    last = products(pe, ps_v[:, tok], [(hh[b][:, k, tok], hl[b][:, k, tok]) for k in range(KC)],
                                    [(wh[:, k, QKW:], wl[:, k, QKW:]) for k in range(KC)])
                last.then_inc(v_done, 1)

            pe.wait_ge(loaded, 16 * LOADS)
            pe.wait_ge(wh_done, 1)
            pe.wait_ge(wl_done, 1)
            turn(0)
            run(pe, chunk)

        @block.vector
        def _(dve):
            chain = Chain(dve, dve_steps)

            def normalise(c):
                for it in range(TPC):
                    t = c * TPC + it
                    dve.tensor_scalar(hn[:, it:it + 1, :], y[:, bass.ds(t, 1), :], rstd[:, bass.ds(t, 1)], None, ALU.mult).then_inc(hn_done, 1)

            def low_part(c, b):
                for k in range(KC):
                    dve.wait_ge(hh_done, c * KC + (k + 1))
                    dve.scalar_tensor_tensor(hl[b][:, k, :], ps_t[k][:], ln1[:, k:k + 1], hh[b][:, k, :].bitcast(F32), ALU.mult,
                                             ALU.subtract).then_inc(hl_done, 1)

            def chunk(c, b, pair, last):
                if not last:
                    dve.wait_ge(turned, c + 1)
                    normalise(c + 1)
                dve.wait_ge(trig_in[b], pair * 16 + 16)
                dve.wait_ge(moved[b], pair * (16 * MOVES))
                for j in range(3):
                    if j == 2 and not last:
                        low_part(c + 1, 1 - b)
                    dve.wait_ge(pair_done, c * 3 + (j + 1))
                    dve.wait_ge(rh_done, c * 3)
                    dve.tensor_tensor(ta[:, j, :], ps_a[j % 2][:], trig[b][:, 0, :], ALU.mult).then_inc(ta_done, 1)
                    dve.tensor_tensor(tb[:, j, :], ps_b[j % 2][:], trig[b][:, 1, :], ALU.mult).then_inc(tb_done, 1)
                    dve.wait_ge(tb_done, c * 3 + (j + 1))
                    dve.wait_ge(ta_done, c * 3 + (j + 1))
                    dve.tensor_tensor(ta[:, j, :], ta[:, j, :], tb[:, j, :], ALU.add).then_inc(rope_done, 1)
                    dve.wait_ge(rope_done, c * 3 + (j + 1))
                    dve.wait_ge(rh_done, c * 3 + (j + 1))
                    dve.tensor_tensor(rl[b][:, j, :], ta[:, j, :], rh[b][:, j, :].bitcast(F32), ALU.subtract).then_inc(rl_done, 1)
                dve.wait_ge(vh_done, c + 1)
                vt = va[:, bass.ds(c * TPC, TPC), :, :].rearrange("p t g d -> p (t g) d")
                dve.tensor_tensor(vt[:, :, DA:DA + D], ps_v[:].rearrange("p (t g d) -> p (t g) d", g=KV, d=D),
                                  vt[:, :, 0:D].bitcast(F32), ALU.subtract).then_inc(vl_done, 1)

            dve.wait_ge(loaded, 16 * LOADS)
            dve.wait_ge(wh_done, 1)
            dve.tensor_tensor(wl[:], raw[:], wh[:].bitcast(F32), ALU.subtract).then_inc(wl_done, 1)
            for t in range(NT):
                if t % 8 == 0:
                    dve.wait_ge(x1_in[t // 8], 16)
                dve.bn_stats(st[:, t, :], y[:, t, :]).then_inc(stats_done, 1)
            dve.wait_ge(stats_done, NT)
            layer_norm_tail(chain, st, mu, var, tmp, var_done, mean_square)
            inverse_root(chain, var[:], root[:], rstd[:], tmp[:], root_done, 1)
            chain.step(dve.tensor_tensor(mean_square[:], mean_square[:], rstd[:], ALU.mult))
            chain.step(dve.tensor_tensor(mean_square[:], mean_square[:], rstd[:], ALU.mult))
            dve.tensor_scalar(mean_square[:], mean_square[:], 1e-6, None, ALU.add).then_inc(ms_done, 1)
            with dve.Fori(0, NT // 4) as i:
                for b in range(4):
                    t = i * 4 + b
                    dve.tensor_scalar(y[:, bass.ds(t, 1), :], y[:, bass.ds(t, 1), :], mu[:, bass.ds(t, 1)], rstd[:, bass.ds(t, 1)],
                                      ALU.subtract, ALU.mult).then_inc(y_done, 1)
            dve.wait_ge(y_done, NT)
            inverse_root(chain, mean_square[:], root[:], rstd[:], tmp[:], root2_done, 1)
            normalise(0)
            low_part(0, 0)
            run(dve, chunk)


def sequence_attention(nc, io, keep):
    with ExitStack() as ctx:
        m = Pool(nc, ctx)
        identb = m.sb("sa_identb", [P, P], BF16)
        ident = m.sb("sa_ident", [P, P])
        late_k = m.sb("sa_late_k", [P, P], BF16)
        late_q = m.sb("sa_late_q", [P, P], BF16)
        onesf = m.sb("sa_onesf", [P, P])
        ones = m.sb("sa_ones", [P, DA], F32R)
        zeros = m.sb("sa_zeros", [P, SLOTS * CH * C // (P * 4)])
        ks = m.sb("sa_ks", [P, N], F32R)
        kb = m.sb("sa_kb", [DA, N], F32R)
        va = m.sb("sa_va", [P, NT, VW], F32R)
        qa = [m.sb(f"sa_qa{b}", [P, CH], F32R) for b in range(3)]
        qb = [m.sb(f"sa_qb{b}", [DA, CH], F32R) for b in range(3)]
        mx = [m.sb(f"sa_mx{b}", [P, TPC, NC]) for b in range(2)]
        m4 = [m.sb(f"sa_m4{b}", [P, TPC]) for b in range(2)]
        dg = m.sb("sa_dg", [P, TPC, P], F32R)
        ph = [m.sb(f"sa_ph{b}", [P, CH], F32R) for b in range(3)]
        pl = [m.sb(f"sa_pl{b}", [P, CH], F32R) for b in range(3)]
        ysb = m.sb("sa_ysb", [DA, CH])
        rec = m.sb("sa_rec", [P, TPC])
        yo = [m.sb(f"sa_yo{b}", [P, TPC, D]) for b in range(2)]
        ps_n = [m.bank(f"sa_ps_n{b}") for b in range(2)]
        ps_s = [m.bank(f"sa_ps_s{b}") for b in range(3)]
        ps_y = m.bank("sa_ps_y")
        ps_m = m.bank("sa_ps_m")
        ps_x = m.bank("sa_ps_x")
        const_in = m.sem("sa_const_in")
        cast_in = m.sem("sa_cast_in")
        ones_set = m.sem("sa_ones_set")
        zeros_set = m.sem("sa_zeros_set")
        blanked = m.sem("sa_blanked")
        kv_first_in = m.sem("sa_kv_first_in")
        kv_rest_in = m.sem("sa_kv_rest_in")
        q_in = [m.sem(f"sa_q_in{b}") for b in range(3)]
        scored = [m.sem(f"sa_scored{b}") for b in range(2)]
        part_max = [m.sem(f"sa_part_max{b}") for b in range(2)]
        max_done = m.sem("sa_max_done")
        diag_done = m.sem("sa_diag_done")
        spread_done = m.sem("sa_spread_done")
        shift_done = m.sem("sa_shift_done")
        full_scored = m.sem("sa_full_scored")
        exp_done = m.sem("sa_exp_done")
        ph_done = m.sem("sa_ph_done")
        pl_done = m.sem("sa_pl_done")
        p_used = m.sem("sa_p_used")
        y_kept = m.sem("sa_y_kept")
        y_turned = m.sem("sa_y_turned")
        rec_done = m.sem("sa_rec_done")
        y_done = m.sem("sa_y_done")
        stored = [m.sem(f"sa_stored{b}") for b in range(2)]
        block = ctx.enter_context(nc.Block())

        ROUNDS = [(c, b) for c in range(NC) for b in range(2)]
        R = len(ROUNDS)
        first = [[(it, kc, CH if kc < c else (it + 1) * P) for it in range(TPC) for kc in range(c + 1)] for c, _ in ROUNDS]
        second = [[(kt, max(0, kt - c * TPC) * P) for kt in range((c + 1) * TPC)] for c, _ in ROUNDS]
        first_before = [sum(map(len, first[:n])) for n in range(R + 1)]
        second_before = [sum(map(len, second[:n])) for n in range(R + 1)]
        FIRST, SECOND = first_before[R], second_before[R]
        assert FIRST % 2 == 0

        EARLY, MARGIN, BOOST = 5, 1, 2

        def ahead(n, i):
            within, all_ = spread_at(n) - MARGIN + 1 if len(second[n]) > 4 else 1, len(first[n + 1])
            def until(i):
                return 0 if i == 0 else min(all_, BOOST + i * (all_ - BOOST) // within)
            return range(until(i), until(i + 1))

        def spread_at(n):
            return len(second[n]) - (EARLY if len(second[n]) > 4 else 3)

        BLANKED_AT = (7, 11)
        BLANK = SLOTS * CH // KV // len(BLANKED_AT)

        @block.sync
        def _(sp):
            sp.dma_start(ident[:], io["ident"]).then_inc(const_in, 16)
            sp.wait_ge(zeros_set, 1)
            with sp.Fori(0, KV) as g:
                for n, (c, b) in enumerate(ROUNDS):
                    sp.wait_ge(y_done, g * R + (n + 1))
                    sp.dma_start(io["ya"][c * CH:(c + 1) * CH, bass.ds(g * (2 * D) + b * D, D)].rearrange("(t p) d -> p t d", p=P),
                                 yo[n % 2][:]).then_inc(stored[n % 2], 16)
                    if n in BLANKED_AT:
                        at = g * (SLOTS * CH // KV) + BLANKED_AT.index(n) * BLANK
                        sp.dma_start(io["sorted_rows"][bass.ds(at, BLANK), :].rearrange("(p r) f -> p (r f)", p=P), zeros[:]).then_inc(blanked, 16)
            for b in range(2):
                sp.wait_ge(stored[b], 8 * KV * R)
            sp.wait_ge(blanked, 16 * KV * len(BLANKED_AT))

        @block.gpsimd
        def _(pool):
            pool.memset(onesf[:], 1.0).then_inc(ones_set, 1)
            for tile, name in ((identb, "ident"), (late_k, "late_k"), (late_q, "late_q")):
                pool.dma_start(tile[:], io[name]).then_inc(cast_in, 16)
            with pool.Fori(0, KV) as g:
                rows = bass.ds(g * D, D)
                pool.wait_ge(p_used, g * SECOND)
                def load_kv(tiles, done):
                    at = slice(tiles.start * P, tiles.stop * P)
                    pool.dma_start(ks[0:D, at], io["k_high"][rows, at]).then_inc(done, 16)
                    pool.dma_start(ks[D:P, at], io["k_low"][rows, at]).then_inc(done, 16)
                    pool.dma_start(kb[0:D, at], io["k_high"][rows, at]).then_inc(done, 16)
                    pool.dma_start(va[:, tiles], io["va"][bass.ds(g, 1), :, tiles, :].rearrange("g p t d -> (g p) t d")).then_inc(done, 16)

                load_kv(slice(0, TPC), kv_first_in)
                for n, (c, b) in enumerate(ROUNDS):
                    if n >= 3:
                        pool.wait_ge(p_used, g * SECOND + second_before[n - 2])
                    head, at = bass.ds(g * (2 * D) + b * D, D), slice(c * CH, (c + 1) * CH)
                    pool.dma_start(qa[n % 3][0:D, :], io["q_high"][head, at]).then_inc(q_in[n % 3], 16)
                    pool.dma_start(qa[n % 3][D:P, :], io["q_high"][head, at]).then_inc(q_in[n % 3], 16)
                    pool.dma_start(qb[n % 3][0:D, :], io["q_low"][head, at]).then_inc(q_in[n % 3], 16)
                    if n == 1:
                        load_kv(slice(TPC, NT), kv_rest_in)

        @block.tensor
        def _(pe):
            pe.wait_ge(const_in, 16)
            pe.wait_ge(cast_in, 48)
            pe.wait_ge(ones_set, 3)
            with pe.Fori(0, KV) as g:
                def first_pass(n, some):
                    c, _ = ROUNDS[n]
                    if some.start == 0:
                        of_slot = len(range(n % 3, R, 3))
                        pe.wait_ge(q_in[n % 3], g * (48 * of_slot) + 48 * (n // 3 + 1))
                    for i in some:
                        it, kc, cols = first[n][i]
                        step = first_before[n] + i
                        pe.wait_ge(part_max[step % 2], g * (FIRST // 2) + step // 2)
                        ps = ps_n[step % 2]
                        last = pe.matmul(ps[:, 0:cols], qa[n % 3][0:D, it * P:(it + 1) * P], ks[0:D, kc * CH:kc * CH + cols],
                                         start=True, stop=kc < c)
                        if kc == c:
                            last = pe.matmul(ps[:, cols - P:cols], identb[:], late_k[:], start=False, stop=True)
                        last.then_inc(scored[step % 2], 1)

                def spread_shift(n):
                    pe.wait_ge(diag_done, g * (R * TPC) + TPC * (n + 1))
                    pe.wait_ge(shift_done, g * R + n)
                    for it in range(TPC):
                        last = pe.matmul(ps_m[0:DA, it * P:(it + 1) * P], ones[:], dg[:, it, :], start=True, stop=True)
                    last.then_inc(spread_done, 1)

                def scores(n, i):
                    c, _ = ROUNDS[n]
                    kt, lo = second[n][i]
                    step = second_before[n] + i
                    pe.wait_ge(pl_done, g * SECOND + max(0, step - 2))
                    ps, keys = ps_s[step % 3], slice(kt * P, (kt + 1) * P)
                    pe.matmul(ps[:, lo:CH], ks[:, keys], qa[n % 3][:, lo:CH], start=True, stop=False)
                    last = pe.matmul(ps[:, lo:CH], kb[:, keys], qb[n % 3][:, lo:CH], start=False, stop=kt < c * TPC)
                    if kt >= c * TPC:
                        last = pe.matmul(ps[:, lo:lo + P], identb[:], late_q[:], start=False, stop=True)
                    last.then_inc(full_scored, 1)

                def weigh(n, i):
                    kt, lo = second[n][i]
                    step = second_before[n] + i
                    pe.wait_ge(ph_done, g * SECOND + (step + 1))
                    pe.wait_ge(pl_done, g * SECOND + (step + 1))
                    high, low = va[:, kt, 0:DA], va[:, kt, DA:2 * DA]
                    out, last_kt = ps_y[0:DA, lo:CH], i == len(second[n]) - 1
                    pe.matmul(out, high, ph[step % 3][:, lo:CH], start=i == 0, stop=False)
                    pe.matmul(out, low, ph[step % 3][:, lo:CH], start=False, stop=False)
                    pe.matmul(out, high, pl[step % 3][:, lo:CH], start=False, stop=last_kt).then_inc(p_used, 1)

                def turn_back(n):
                    pe.wait_ge(y_kept, g * R + (n + 1))
                    pe.wait_ge(y_done, g * R + n)
                    for it in range(TPC):
                        last = pe.transpose(ps_x[:, it * DA:(it + 1) * DA], ysb[:, it * P:(it + 1) * P], ident[0:DA, 0:DA])
                    last.then_inc(y_turned, 1)

                pe.wait_ge(kv_first_in, g * 64 + 64)
                first_pass(0, range(len(first[0])))
                spread_shift(0)
                pe.wait_ge(shift_done, g * R + 1)
                scores(0, 0)
                scores(0, 1)
                for n in range(R):
                    for i in range(len(second[n])):
                        if i == spread_at(n) and n + 1 < R:
                            spread_shift(n + 1)
                        if i + 2 < len(second[n]):
                            scores(n, i + 2)
                        elif n + 1 < R:
                            if i + 2 == len(second[n]):
                                pe.wait_ge(shift_done, g * R + (n + 2))
                            scores(n + 1, i + 2 - len(second[n]))
                        if n + 1 < R:
                            if n == 1 and i == 0:
                                pe.wait_ge(kv_rest_in, g * 64 + 64)
                            first_pass(n + 1, ahead(n, i))
                        if i == 0:
                            pe.wait_ge(y_kept, g * R + n)
                        weigh(n, i)
                        if i == 1 and n > 0:
                            turn_back(n - 1)
                turn_back(R - 1)

        @block.scalar
        def _(act):
            act.wait_ge(ones_set, 1)
            act.activation(ones[:], onesf[:, 0:DA], ACT.Copy).then_inc(ones_set, 1)
            for k in range(N // CH):
                last = act.activation(kb[D:DA, k * CH:(k + 1) * CH].rearrange("o (a b) -> o a b", b=P),
                                      spread(onesf[D:DA, :], 1, TPC), ACT.Copy)
            last.then_inc(ones_set, 1)
            with act.Fori(0, KV) as g:
                def keep_shift(n):
                    act.wait_ge(spread_done, g * R + (n + 1))
                    act.wait_ge(p_used, g * SECOND + (second_before[n - 2] if n >= 3 else 0))
                    act.activation(qb[n % 3][D:DA, :], ps_m[D:DA, :], ACT.Copy).then_inc(shift_done, 1)

                def keep_sums(n):
                    act.wait_ge(p_used, g * SECOND + second_before[n + 1])
                    act.wait_ge(y_turned, g * R + n)
                    act.activation(ysb[:], ps_y[0:DA, :], ACT.Copy).then_inc(y_kept, 1)

                def exps(n, i):
                    lo, step = second[n][i][1], second_before[n] + i
                    act.wait_ge(full_scored, g * SECOND + (step + 1))
                    act.activation(ps_s[step % 3][:, lo:CH], ps_s[step % 3][:, lo:CH], ACT.Exp, scale=D ** -0.5).then_inc(exp_done, 1)

                def high_part(n, i):
                    lo, step = second[n][i][1], second_before[n] + i
                    act.wait_ge(exp_done, g * SECOND + (step + 1))
                    act.wait_ge(p_used, g * SECOND + max(0, step - 2))
                    act.activation(ph[step % 3][:, lo:CH], ps_s[step % 3][:, lo:CH], ACT.Copy).then_inc(ph_done, 1)

                keep_shift(0)
                for n in range(R):
                    for i in range(len(second[n])):
                        exps(n, i)
                        if i == spread_at(n) + 1 and n + 1 < R:
                            keep_shift(n + 1)
                        high_part(n, i)
                        if i == 0 and n > 0:
                            keep_sums(n - 1)
                keep_sums(R - 1)

        @block.vector
        def _(dve):
            dve.memset(zeros[:], 0.0).then_inc(zeros_set, 1)
            dve.wait_ge(const_in, 16)
            with dve.Fori(0, KV) as g:
                def maxima(n, some):
                    for i in some:
                        it, kc, cols = first[n][i]
                        step = first_before[n] + i
                        dve.wait_ge(scored[step % 2], g * (FIRST // 2) + (step // 2 + 1))
                        dve.tensor_reduce(mx[n % 2][:, it, kc:kc + 1], ps_n[step % 2][:, 0:cols], AX.X, ALU.max).then_inc(part_max[step % 2], 1)

                def shift(n):
                    c, _ = ROUNDS[n]
                    for w in range(2):
                        dve.wait_ge(part_max[w], g * (FIRST // 2) + (first_before[n + 1] + 1 - w) // 2)
                    dve.tensor_reduce(m4[n % 2][:], mx[n % 2][:, :, 0:c + 1], AX.X, ALU.max).then_inc(max_done, 1)
                    dve.wait_ge(max_done, g * R + (n + 1))
                    dve.wait_ge(spread_done, g * R + n)
                    for it in range(TPC):
                        dve.tensor_scalar(dg[:, it, :], ident[:], m4[n % 2][:, it:it + 1], -1.0, ALU.mult, ALU.mult).then_inc(diag_done, 1)

                def finish(n):
                    dve.wait_ge(y_turned, g * R + (n + 1))
                    px = ps_x[:, 0:TPC * DA].rearrange("p (t d) -> p t d", d=DA)
                    dve.reciprocal(rec[:].unsqueeze(2), px[:, :, D:DA]).then_inc(rec_done, 1)
                    dve.wait_ge(rec_done, g * R + (n + 1))
                    dve.wait_ge(stored[n % 2], g * (8 * R) + 16 * (n // 2))
                    dve.tensor_tensor(yo[n % 2][:], px[:, :, 0:D], spread(rec[:], 2, D), ALU.mult).then_inc(y_done, 1)

                maxima(0, range(len(first[0])))
                shift(0)
                for n in range(R):
                    for i, (kt, lo) in enumerate(second[n]):
                        step = second_before[n] + i
                        dve.wait_ge(ph_done, g * SECOND + (step + 1))
                        dve.tensor_tensor(pl[step % 3][:, lo:CH], ps_s[step % 3][:, lo:CH], ph[step % 3][:, lo:CH].bitcast(F32),
                                          ALU.subtract).then_inc(pl_done, 1)
                        if n + 1 < R:
                            maxima(n + 1, ahead(n, i))
                            if ahead(n, i) and ahead(n, i).stop == len(first[n + 1]):
                                shift(n + 1)
                        if i == 2 and n > 0:
                            finish(n - 1)
                finish(R - 1)


def join_and_route(nc, io, keep):
    with ExitStack() as ctx:
        m = Pool(nc, ctx)
        y = keep.y
        ident = m.sb("jr_ident", [P, P])
        wo = m.sb("jr_wo", [P, KC, C])
        woh = m.sb("jr_woh", [P, KC, C], F32R)
        wol = m.sb("jr_wol", [P, KC, C], F32R)
        wr = m.sb("jr_wr", [P, KC, E])
        wrh = m.sb("jr_wrh", [P, KC, E], F32R)
        wrl = m.sb("jr_wrl", [P, KC, E], F32R)
        ln2 = m.sb("jr_ln2", [P, KC])
        plan = m.sb("jr_plan", [P, PLAN_COLS])
        before = m.sb("jr_before", [P, P], BF16)
        ones = m.sb("jr_ones", [P, P], BF16)
        ya = [m.sb(f"jr_ya{b}", [P, TPC, C]) for b in range(2)]
        ah = [m.sb(f"jr_ah{b}", [P, KC, CH], F32R) for b in range(2)]
        al = [m.sb(f"jr_al{b}", [P, KC, CH], F32R) for b in range(2)]
        hn = m.sb("jr_hn", [P, NT, C])
        junk = m.sb("jr_junk", [P, TPC, C])
        sq = m.sb("jr_sq", [P, NT])
        var = m.sb("jr_var", [P, NT])
        root = m.sb("jr_root", [P, NT])
        r2 = m.sb("jr_r2", [P, NT])
        tmp = m.sb("jr_tmp", [P, NT])
        lt = m.sb("jr_lt", [E, 2, CH])
        lg = m.sb("jr_lg", [P, NT, E])
        w8 = m.sb("jr_w8", [P, NT, E])
        one = m.sb("jr_one", [P, NT])
        first = m.sb("jr_first", [P, NT, E])
        second = m.sb("jr_second", [P, NT, E])
        pick = m.sb("jr_pick", [P, NT, E])
        chosen = m.sb("jr_chosen", [P, NT, E], BF16)
        top = m.sb("jr_top", [P, NT])
        within = m.sb("jr_within", [P, NT, E])
        of_tile = m.sb("jr_of_tile", [P, NT, E])
        upto = [m.sb(f"jr_upto{b}", [P, NT, E]) for b in range(2)]
        place = m.sb("jr_place", [P, NT])
        over = m.sb("jr_over", [P, E, NC])
        slots = m.sb("jr_slots", [P, E])
        sums = m.sb("jr_sums", [P, E, E])
        end = m.sb("jr_end", [P, E])
        ended = m.sb("jr_ended", [P, SLOTS, E])
        owner = m.sb("jr_owner", [P, SLOTS])
        ps_t = [[m.bank(f"jr_ps_t{b}{k}") for k in range(KC)] for b in range(2)]
        ps_y = [m.bank(f"jr_ps_y{b}") for b in range(2)]
        ps_l = m.bank("jr_ps_l")
        ps_g = m.bank("jr_ps_g")
        loaded = m.sem("jr_loaded")
        cast_in = m.sem("jr_cast_in")
        ones_set = m.sem("jr_ones_set")
        chosen_done = m.sem("jr_chosen_done")
        counted = m.sem("jr_counted")
        owners_done = m.sem("jr_owners_done")
        places_done = m.sem("jr_places_done")
        scattered = m.sem("jr_scattered")
        expert_in = [m.sem(f"jr_expert_in{b}") for b in range(2)]
        expert_high = m.sem("jr_expert_high")
        expert_low = m.sem("jr_expert_low")
        ya_in = [m.sem(f"jr_ya_in{b}") for b in range(2)]
        high_done = m.sem("jr_high_done")
        low_done = m.sem("jr_low_done")
        ya_turned = m.sem("jr_ya_turned")
        ah_done = m.sem("jr_ah_done")
        al_done = m.sem("jr_al_done")
        joined = m.sem("jr_joined")
        y2_done = m.sem("jr_y2_done")
        sq_done = m.sem("jr_sq_done")
        ms_done = m.sem("jr_ms_done")
        root_done = m.sem("jr_root_done")
        steps = m.sem("jr_steps")
        hn_done = m.sem("jr_hn_done")
        hn_turned = m.sem("jr_hn_turned")
        h2h_done = m.sem("jr_h2h_done")
        h2l_done = m.sem("jr_h2l_done")
        scored = m.sem("jr_scored")
        lt_kept = m.sem("jr_lt_kept")
        lt_turned = m.sem("jr_lt_turned")
        lg_kept = m.sem("jr_lg_kept")
        shifted = m.sem("jr_shifted")
        exps_done = m.sem("jr_exps_done")
        x1_in = [m.sem(f"jr_x1_in{b}") for b in range(2)]
        x1_added = m.sem("jr_x1_added")
        block = ctx.enter_context(nc.Block())
        LOADS = 5

        @block.sync
        def _(sp):
            sp.dma_start(wo[:], io["w_o"].rearrange("(k p) o -> p k o", p=P)).then_inc(loaded, 16)
            sp.dma_start(ident[:], io["ident"]).then_inc(loaded, 16)
            sp.dma_start(wr[:], io["w_r"].rearrange("(k p) o -> p k o", p=P)).then_inc(loaded, 16)
            sp.dma_start(ln2[:], io["ln2"]).then_inc(loaded, 16)
            sp.dma_start(plan[:], io["plan"]).then_inc(loaded, 16)
            with sp.Fori(0, NC // 2) as i:
                for b in range(2):
                    sp.wait_ge(ya_turned, i * 2 + b)
                    sp.dma_start(ya[b][:], io["ya"][bass.ds((i * 2 + b) * CH, CH), :].rearrange("(t p) f -> p t f", p=P)).then_inc(ya_in[b], 16)
            for c in range(NC):
                if c < 2:
                    sp.wait_ge(ya_turned, NC - 1 + c)
                else:
                    sp.wait_ge(x1_added, c - 1)
                sp.dma_start(ya[c % 2][:], io["x1"][c * CH:(c + 1) * CH, :].rearrange("(t p) f -> p t f", p=P)).then_inc(x1_in[c % 2], 16)

        @block.gpsimd
        def _(pool):
            pool.dma_start(before[:], io["before"]).then_inc(cast_in, 16)
            pool.memset(ones[:], 1.0).then_inc(ones_set, 1)
            for c in range(NC):
                tiles = slice(c * TPC, (c + 1) * TPC)
                pool.wait_ge(x1_in[c % 2], 16 * (c // 2 + 1))
                pool.wait_ge(hn_turned, c + 1)
                pool.tensor_tensor(y[:, tiles, :], y[:, tiles, :], ya[c % 2][:], ALU.add).then_inc(x1_added, 1)
            pool.wait_ge(owners_done, 1)
            for b in range(2):
                gather_expert(pool, io, keep, b).then_inc(expert_in[b], 16)
            pool.wait_ge(places_done, 2)
            pool.wait_ge(hn_done, NC)
            for t in range(NT):
                for r in range(2):
                    pool.indirect_dma_start(io["sorted_rows"], bass.IndirectOffsetOnAxis(keep.place[:, r, t:t + 1], 0),
                                            hn[:, t, :], None).then_inc(scattered, 16)
            pool.wait_ge(scattered, 16 * 2 * NT)
            for b in range(2):
                pool.wait_ge(expert_in[b], 16)

        @block.tensor
        def _(pe):
            pe.wait_ge(loaded, 16 * LOADS)
            pe.wait_ge(high_done, 2)
            pe.wait_ge(low_done, 2)
            with pe.Fori(0, NC // 2) as i:
                for b in range(2):
                    pe.wait_ge(ya_in[b], i * 16 + 16)
                    pe.wait_ge(al_done, i * 2 + b)
                    for k in range(KC):
                        for it in range(TPC):
                            last = pe.transpose(ps_t[b][k][:, it * P:(it + 1) * P], ya[b][:, it, k * P:(k + 1) * P], ident[:])
                    last.then_inc(ya_turned, 1)
                for b in range(2):
                    pe.wait_ge(ah_done, i * 2 + (b + 1))
                    pe.wait_ge(al_done, i * 2 + (b + 1))
                    for half in range(2):
                        pe.wait_ge(y2_done, i * 4 + max(0, 2 * b + half - 1))
                        for j in range(2):
                            tok = slice((2 * half + j) * P, (2 * half + j + 1) * P)
                            last = products(pe, ps_y[half][:, j * C:(j + 1) * C], [(ah[b][:, k, tok], al[b][:, k, tok]) for k in range(KC)],
                                            [(woh[:, k, :], wol[:, k, :]) for k in range(KC)])
                        last.then_inc(joined, 1)
            def score(c):
                pe.wait_ge(h2h_done, c + 1)
                pe.wait_ge(h2l_done, c + 1)
                if c > 0:
                    pe.wait_ge(lt_kept, c)
                products(pe, ps_l[0:E, :], [(wrh[:, k, :], wrl[:, k, :]) for k in range(KC)],
                         [(ah[c % 2][:, k, :], al[c % 2][:, k, :]) for k in range(KC)]).then_inc(scored, 1)
            def turn_scores(c):
                pe.wait_ge(lt_kept, c + 1)
                if c > 0:
                    pe.wait_ge(lg_kept, c)
                for it in range(TPC):
                    last = pe.transpose(ps_g[:, it * E:(it + 1) * E], lt[:, c % 2, it * P:(it + 1) * P], ident[0:E, 0:E])
                last.then_inc(lt_turned, 1)
            for c in range(NC + 2):
                if c < NC:
                    b = c % 2
                    pe.wait_ge(hn_done, c + 1)
                    if c >= 2:
                        pe.wait_ge(h2h_done, c - 1)
                        pe.wait_ge(h2l_done, c - 1)
                    for k in range(KC):
                        for it in range(TPC):
                            last = pe.transpose(ps_t[b][k][:, it * P:(it + 1) * P],
                                                hn[:, c * TPC + it, k * P:(k + 1) * P], ident[:])
                    last.then_inc(hn_turned, 1)
                if c >= 2:
                    turn_scores(c - 2)
                if 1 <= c <= NC:
                    score(c - 1)
            pe.wait_ge(chosen_done, 1)
            pe.wait_ge(cast_in, 16)
            pe.wait_ge(ones_set, 1)
            pe.wait_ge(lg_kept, NC)
            picks = chosen[:].rearrange("p t e -> p (t e)")
            pe.matmul(ps_l[:, 0:NT * E], before[:], picks, start=True, stop=True)
            pe.matmul(ps_g[:, 0:NT * E], ones[:], picks, start=True, stop=True).then_inc(counted, 1)

        @block.scalar
        def _(act):
            act.wait_ge(loaded, 16 * LOADS)
            act.activation(woh[:], wo[:], ACT.Copy).then_inc(high_done, 1)
            act.activation(wrh[:], wr[:], ACT.Copy).then_inc(high_done, 1)
            with act.Fori(0, NC // 2) as i:
                for b in range(2):
                    act.wait_ge(ya_turned, i * 2 + (b + 1))
                    act.wait_ge(joined, i * 4)
                    for k in range(KC):
                        last = act.activation(ah[b][:, k, :], ps_t[b][k][:], ACT.Copy)
                    last.then_inc(ah_done, 1)
                for q in range(4):
                    act.wait_ge(y2_done, i * 4 + (q + 1))
                    act.wait_ge(sq_done, i * 4 + q)
                    for j in range(2):
                        t = i * 8 + (2 * q + j)
                        last = act.activation(junk[:, j:j + 1, :], y[:, bass.ds(t, 1), :], ACT.Square, accum_out=sq[:, bass.ds(t, 1)])
                    last.then_inc(sq_done, 1)
            act.wait_ge(ms_done, 1)
            act.activation(root[:], var[:], ACT.Sqrt).then_inc(root_done, 1)
            for c in range(NC):
                b = c % 2
                act.wait_ge(hn_turned, c + 1)
                if c >= 2:
                    act.wait_ge(scored, c - 1)
                for k in range(KC):
                    last = act.activation(ah[b][:, k, :], ps_t[b][k][:], ACT.Copy, scale=ln2[:, k:k + 1])
                last.then_inc(h2h_done, 1)
                act.wait_ge(scored, c + 1)
                if c >= 2:
                    act.wait_ge(lt_turned, c - 1)
                act.activation(lt[:, b, :], ps_l[0:E, :], ACT.Copy).then_inc(lt_kept, 1)
            act.wait_ge(shifted, 1)
            act.activation(lg[:], lg[:], ACT.Exp).then_inc(exps_done, 1)
            act.wait_ge(expert_in[0], 16)
            act.activation(keep.wh[0][:], keep.raw[0][:], ACT.Copy).then_inc(expert_high, 1)

        @block.vector
        def _(dve):
            chain = Chain(dve, steps)
            dve.wait_ge(high_done, 2)
            dve.tensor_tensor(wol[:], wo[:], woh[:].bitcast(F32), ALU.subtract).then_inc(low_done, 1)
            dve.tensor_tensor(wrl[:], wr[:], wrh[:].bitcast(F32), ALU.subtract).then_inc(low_done, 1)
            with dve.Fori(0, NC // 2) as i:
                for b in range(2):
                    dve.wait_ge(ah_done, i * 2 + (b + 1))
                    for k in range(KC):
                        last = dve.tensor_tensor(al[b][:, k, :], ps_t[b][k][:], ah[b][:, k, :].bitcast(F32), ALU.subtract)
                    last.then_inc(al_done, 1)
                for q in range(4):
                    dve.wait_ge(joined, i * 4 + (q + 1))
                    yt = y[:, bass.ds(i * 8 + 2 * q, 2), :]
                    dve.tensor_tensor(yt, yt, ps_y[q % 2][:].rearrange("p (t f) -> p t f", t=2), ALU.add).then_inc(y2_done, 1)
            dve.wait_ge(sq_done, NT // 2)
            dve.tensor_scalar(var[:], sq[:], 1.0 / C, 1e-6, ALU.mult, ALU.add).then_inc(ms_done, 1)
            inverse_root(chain, var[:], root[:], r2[:], tmp[:], root_done, 1)
            def normalise(c):
                tiles = slice(c * TPC, (c + 1) * TPC)
                dve.tensor_tensor(hn[:, tiles, :], y[:, tiles, :], spread(r2[:, tiles], 2, C), ALU.mult).then_inc(hn_done, 1)
            def keep_scores(c):
                dve.wait_ge(lt_turned, c + 1)
                dve.tensor_copy(lg[:, c * TPC:(c + 1) * TPC, :], ps_g[:, 0:TPC * E].rearrange("p (t e) -> p t e", e=E)).then_inc(lg_kept, 1)
            normalise(0)
            for c in range(NC):
                if c + 1 < NC:
                    normalise(c + 1)
                dve.wait_ge(h2h_done, c + 1)
                for k in range(KC):
                    last = dve.scalar_tensor_tensor(al[c % 2][:, k, :], ps_t[c % 2][k][:], ln2[:, k:k + 1], ah[c % 2][:, k, :].bitcast(F32),
                                                    ALU.mult, ALU.subtract)
                last.then_inc(h2l_done, 1)
                if c >= 2:
                    keep_scores(c - 2)
            keep_scores(NC - 2)
            keep_scores(NC - 1)
            dve.wait_ge(lg_kept, NC)
            chain.step(dve.tensor_reduce(one[:], lg[:], AX.X, ALU.max))
            dve.tensor_tensor(lg[:], lg[:], spread(one[:], 2, E), ALU.subtract).then_inc(shifted, 1)
            dve.wait_ge(exps_done, 1)
            chain.step(dve.tensor_reduce(one[:], lg[:], AX.X, ALU.add))
            chain.step(dve.reciprocal(one[:], one[:]))
            chain.step(dve.tensor_tensor(lg[:], lg[:], spread(one[:], 2, E), ALU.mult))
            def choose(out):
                chain.step(dve.tensor_reduce(top[:], w8[:], AX.X, ALU.max))
                chain.step(dve.tensor_tensor(pick[:], w8[:], spread(top[:], 2, E), ALU.is_equal))
                chain.step(dve.tensor_tensor(pick[:], pick[:], spread(plan[:, RANK], 1, NT), ALU.mult))
                chain.step(dve.tensor_reduce(one[:], pick[:], AX.X, ALU.max))
                chain.step(dve.tensor_tensor(out[:], spread(one[:], 2, E), spread(plan[:, RANK], 1, NT), ALU.is_equal))
            chain.step(dve.tensor_copy(w8[:], lg[:]))
            choose(first)
            chain.step(dve.scalar_tensor_tensor(w8[:], first[:], -2.0, w8[:], ALU.mult, ALU.add))
            choose(second)
            chain.step(dve.tensor_tensor(pick[:], second[:], first[:], ALU.add))
            dve.tensor_copy(chosen[:], pick[:]).then_inc(chosen_done, 1)
            chain.step(dve.tensor_tensor(w8[:], lg[:], pick[:], ALU.mult))
            dve.wait_ge(counted, 1)
            chain.step(dve.tensor_copy(of_tile[:].rearrange("p t e -> p (t e)"), ps_g[:, 0:NT * E]))
            old = of_tile
            for n in range(NT.bit_length() - 1):
                new, far = upto[n % 2], 1 << n
                chain.step(dve.tensor_copy(new[:, 0:far, :], old[:, 0:far, :]))
                chain.step(dve.tensor_tensor(new[:, far:, :], old[:, far:, :], old[:, 0:NT - far, :], ALU.add))
                old = new
            count = old[:, NT - 1, :]
            chain.step(dve.tensor_tensor(over[:], spread(count, 2, NC), spread(plan[:, EDGES], 1, E), ALU.is_gt))
            chain.step(dve.tensor_reduce(slots[:], over[:], AX.X, ALU.add))
            chain.step(dve.tensor_tensor(sums[:], spread(slots[:], 1, E), plan[:, UPTO].rearrange("p (a b) -> p a b", b=E), ALU.mult))
            chain.step(dve.tensor_reduce(end[:], sums[:], AX.X, ALU.add))
            chain.step(dve.tensor_tensor(ended[:], spread(end[:], 1, SLOTS), spread(plan[:, SLOT], 2, E), ALU.is_le))
            chain.step(dve.tensor_reduce(owner[:], ended[:], AX.X, ALU.add))
            chain.step(dve.tensor_scalar(owner[:], owner[:], E - 1.0, float(P), ALU.min, ALU.mult))
            dve.tensor_tensor(keep.owner_row[:], owner[:], plan[:, ROW].to_broadcast([P, SLOTS]), ALU.add).then_inc(owners_done, 1)
            chain.step(dve.tensor_tensor(end[:], end[:], slots[:], ALU.subtract))
            chain.step(dve.scalar_tensor_tensor(old[:], spread(end[:], 1, NT), float(CH), old[:], ALU.mult, ALU.add))
            chain.step(dve.tensor_tensor(old[:], old[:], of_tile[:], ALU.subtract))
            chain.step(dve.tensor_tensor(old[:].rearrange("p t e -> p (t e)"), old[:].rearrange("p t e -> p (t e)"), ps_l[:, 0:NT * E], ALU.add))
            for r, mine in enumerate((first, second)):
                chain.step(dve.tensor_tensor(pick[:], old[:], mine[:], ALU.mult))
                chain.step(dve.tensor_reduce(place[:], pick[:], AX.X, ALU.add))
                dve.tensor_copy(keep.place[:, r, :], place[:]).then_inc(places_done, 1)
                dve.wait_ge(places_done, r + 1)
            chain.step(dve.tensor_reduce(one[:], w8[:], AX.X, ALU.add))
            chain.step(dve.tensor_scalar(one[:], one[:], 1e-9, None, ALU.add))
            chain.step(dve.reciprocal(one[:], one[:]))
            for r, mine in enumerate((first, second)):
                chain.step(dve.tensor_tensor(pick[:], lg[:], mine[:], ALU.mult))
                chain.step(dve.tensor_reduce(top[:], pick[:], AX.X, ALU.add))
                chain.step(dve.tensor_tensor(keep.share[:, r, :], top[:], one[:], ALU.mult))
            dve.wait_ge(expert_high, 1)
            dve.tensor_tensor(keep.wl[0][:], keep.raw[0][:], keep.wh[0][:].bitcast(F32), ALU.subtract).then_inc(expert_low, 1)


def gather_expert(pool, io, keep, slot):
    return pool.indirect_dma_start(keep.raw[slot % 2][:], None, io["w_experts"],
                                   bass.IndirectOffsetOnAxis(keep.owner_row[:, slot:slot + 1], 0))


def experts(nc, io, keep):
    PIECE = EW // PIECES
    TURN_AT = MT - 3
    with ExitStack() as ctx:
        m = Pool(nc, ctx)
        ident = m.sb("ex_ident", [P, P])
        ln2 = m.sb("ex_ln2", [P, KC])
        rows = [m.sb(f"ex_rows{b}", [P, TPC, C]) for b in range(2)]
        xh = [m.sb(f"ex_xh{b}", [P, KC, CH], F32R) for b in range(2)]
        xl = [m.sb(f"ex_xl{b}", [P, KC, CH], F32R) for b in range(2)]
        silu = [m.sb(f"ex_silu{b}", [P, CH]) for b in range(2)]
        prod = [m.sb(f"ex_prod{b}", [P, CH]) for b in range(2)]
        ph = [m.sb(f"ex_ph{b}", [P, CH], F32R) for b in range(3)]
        pl = [m.sb(f"ex_pl{b}", [P, CH], F32R) for b in range(3)]
        out = [m.sb(f"ex_out{b}", [P, TPC, C]) for b in range(2)]
        ps_g = [m.bank(f"ex_ps_g{b}") for b in range(2)]
        ps_u = [m.bank(f"ex_ps_u{b}") for b in range(2)]
        ps_o = [m.bank(f"ex_ps_o{b}") for b in range(TPC // 2)]
        ps_x = [m.bank(f"ex_ps_x{k}") for k in range(KC)]
        loaded = m.sem("ex_loaded")
        rows_in = [m.sem(f"ex_rows_in{b}") for b in range(2)]
        turned = m.sem("ex_turned")
        xh_done = m.sem("ex_xh_done")
        xl_done = m.sem("ex_xl_done")
        expert_in = [m.sem(f"ex_expert_in{b}") for b in range(2)]
        high_split = m.sem("ex_high_split")
        low_split = m.sem("ex_low_split")
        up_done = m.sem("ex_up_done")
        silu_done = m.sem("ex_silu_done")
        prod_done = m.sem("ex_prod_done")
        ph_done = m.sem("ex_ph_done")
        pl_done = m.sem("ex_pl_done")
        used = m.sem("ex_used")
        out_act = m.sem("ex_out_act")
        out_dve = m.sem("ex_out_dve")
        stored = [m.sem(f"ex_stored{b}") for b in range(2)]
        block = ctx.enter_context(nc.Block())
        assert MT % 2 == 0 and MT % 3 == 0
        assert SLOTS % 2 == 1

        def tall(mt):
            return P if mt < MF else MR

        def run(eng, slot):
            with eng.Fori(0, SLOTS // 2) as pair:
                for b in range(2):
                    slot(pair * 2 + b, b, pair, False)
            slot(SLOTS - 1, 0, SLOTS // 2, True)

        @block.sync
        def _(sp):
            def load(s, b):
                sp.dma_start(rows[b][:], io["sorted_rows"][bass.ds(s * CH, CH), :].rearrange("(t p) f -> p t f", p=P)).then_inc(rows_in[b], 16)

            def slot(s, b, pair, last):
                if not last:
                    sp.wait_ge(turned, s * KC)
                    load(s + 1, 1 - b)
                sp.wait_ge(out_act, s + 1)
                sp.wait_ge(out_dve, s + 1)
                sp.dma_start(io["expert_rows"][bass.ds(s * CH, CH), :].rearrange("(t p) f -> p t f", p=P), out[b][:]).then_inc(stored[b], 16)

            sp.dma_start(ident[:], io["ident"]).then_inc(loaded, 16)
            sp.dma_start(ln2[:], io["ln2"]).then_inc(loaded, 16)
            load(0, 0)
            run(sp, slot)
            sp.wait_ge(stored[0], 16 * (SLOTS // 2 + 1))
            sp.wait_ge(stored[1], 16 * (SLOTS // 2))

        @block.gpsimd
        def _(pool):
            for s in range(2, SLOTS):
                pool.wait_ge(low_split, (s - 2) * PIECES)
                if s >= 4:
                    pool.wait_ge(expert_in[s % 2], 16 * (s // 2 - 1))
                gather_expert(pool, io, keep, s).then_inc(expert_in[s % 2], 16)

        @block.tensor
        def _(pe):
            def turn(s, b, pair, k):
                if k == 0:
                    pe.wait_ge(rows_in[b], pair * 16 + 16)
                for it in range(TPC):
                    last = pe.transpose(ps_x[k][:, it * P:(it + 1) * P], rows[b][:, it, k * P:(k + 1) * P], ident[:])
                last.then_inc(turned, 1)

            def up(b, mt):
                if mt < MF:
                    parts = ((ps_g[mt % 2][:], mt * 2 * P, P), (ps_u[mt % 2][:], (mt * 2 + 1) * P, P))
                else:
                    parts = ((ps_g[mt % 2][0:64 + MR, :], mt * 2 * P, 64 + MR),)
                for ps, at, cols in parts:
                    last = products(pe, ps, [(keep.wh[b][:, k * UPW + at:k * UPW + at + cols],
                                              keep.wl[b][:, k * UPW + at:k * UPW + at + cols]) for k in range(KC)],
                                    [(xh[b][:, k, :], xl[b][:, k, :]) for k in range(KC)])
                last.then_inc(up_done, 1)

            def down(b, mt):
                n, at = tall(mt), KC * UPW + mt * C
                for it in range(TPC):
                    tok = slice(it * P, (it + 1) * P)
                    last = products(pe, ps_o[it // 2][:, (it % 2) * C:(it % 2 + 1) * C], [(ph[mt % 3][0:n, tok], pl[mt % 3][0:n, tok])],
                                    [(keep.wh[b][0:n, at:at + C], keep.wl[b][0:n, at:at + C])],
                                    start=mt == 0 and it % 2 == 0, stop=mt == MT - 1, shared=True)
                last.then_inc(used, 1)

            def slot(s, b, pair, last):
                for mt in range(MT):
                    if mt + 1 < MT:
                        pe.wait_ge(prod_done, s * MT + mt)
                        up(b, mt + 1)
                    elif not last:
                        pe.wait_ge(low_split, s * PIECES + PIECES)
                        pe.wait_ge(xl_done, s * KC + 2 * KC)
                        pe.wait_ge(prod_done, s * MT + mt)
                        up(1 - b, 0)
                    if mt == TURN_AT and not last:
                        for k in range(KC):
                            turn(s + 1, 1 - b, pair + b, k)
                    if mt == 0:
                        pe.wait_ge(out_act, s)
                        pe.wait_ge(out_dve, s)
                    pe.wait_ge(pl_done, s * MT + (mt + 1))
                    down(b, mt)

            pe.wait_ge(loaded, 32)
            for k in range(KC):
                turn(0, 0, 0, k)
            pe.wait_ge(xl_done, KC)
            up(0, 0)
            run(pe, slot)

        @block.scalar
        def _(act):
            def hidden(base, mt):
                act.wait_ge(up_done, base + (mt + 1))
                if mt < MF:
                    act.activation(silu[mt % 2][:], ps_g[mt % 2][:], ACT.Silu).then_inc(silu_done, 1)
                else:
                    act.activation(silu[mt % 2][64:64 + MR, :], ps_g[mt % 2][0:MR, :], ACT.Silu).then_inc(silu_done, 1)
                act.wait_ge(prod_done, base + (mt + 1))
                act.activation(ph[mt % 3][0:tall(mt), :], prod[mt % 2][0:tall(mt), :], ACT.Copy).then_inc(ph_done, 1)

            def split_rows(s, b, k):
                act.wait_ge(turned, s * KC + (k + 1))
                act.activation(xh[b][:, k, :], ps_x[k][:], ACT.Copy, scale=ln2[:, k:k + 1]).then_inc(xh_done, 1)

            def slot(s, b, pair, last):
                for mt in range(MT):
                    if mt > 0:
                        hidden(s * MT, mt)
                    if mt < PIECES and not last:
                        if mt == 0:
                            act.wait_ge(used, s * MT)
                            act.wait_ge(expert_in[1 - b], pair * 16 + 16 * b)
                        at = slice(mt * PIECE, (mt + 1) * PIECE)
                        act.activation(keep.wh[1 - b][:, at], keep.raw[1 - b][:, at], ACT.Copy).then_inc(high_split, 1)
                    if mt == TURN_AT + 1 and not last:
                        for k in range(KC):
                            split_rows(s + 1, 1 - b, k)
                if not last:
                    hidden(s * MT + MT, 0)
                act.wait_ge(used, s * MT + MT)
                act.wait_ge(stored[b], pair * 16)
                act.activation(out[b][:, 0:2, :], ps_o[0][:].rearrange("p (t f) -> p t f", t=2), ACT.Copy).then_inc(out_act, 1)

            act.wait_ge(loaded, 32)
            for k in range(KC):
                split_rows(0, 0, k)
            hidden(0, 0)
            run(act, slot)

        @block.vector
        def _(dve):
            def hidden(base, mt):
                n = tall(mt)
                dve.wait_ge(silu_done, base + (mt + 1))
                if mt < MF:
                    dve.tensor_tensor(prod[mt % 2][:], silu[mt % 2][:], ps_u[mt % 2][:], ALU.mult).then_inc(prod_done, 1)
                else:
                    dve.tensor_tensor(prod[mt % 2][0:MR, :], silu[mt % 2][64:64 + MR, :], ps_g[mt % 2][64:64 + MR, :],
                                      ALU.mult).then_inc(prod_done, 1)
                dve.wait_ge(ph_done, base + (mt + 1))
                dve.tensor_tensor(pl[mt % 3][0:n, :], prod[mt % 2][0:n, :], ph[mt % 3][0:n, :].bitcast(F32),
                                  ALU.subtract).then_inc(pl_done, 1)

            def split_rows(s, b, k):
                dve.wait_ge(xh_done, s * KC + (k + 1))
                dve.scalar_tensor_tensor(xl[b][:, k, :], ps_x[k][:], ln2[:, k:k + 1], xh[b][:, k, :].bitcast(F32),
                                         ALU.mult, ALU.subtract).then_inc(xl_done, 1)

            def slot(s, b, pair, last):
                for mt in range(MT):
                    if mt > 0:
                        hidden(s * MT, mt)
                    if mt < PIECES and not last:
                        at = slice(mt * PIECE, (mt + 1) * PIECE)
                        dve.wait_ge(high_split, s * PIECES + (mt + 1))
                        dve.tensor_tensor(keep.wl[1 - b][:, at], keep.raw[1 - b][:, at], keep.wh[1 - b][:, at].bitcast(F32),
                                          ALU.subtract).then_inc(low_split, 1)
                    if mt == TURN_AT + 1 and not last:
                        for k in range(KC):
                            split_rows(s + 1, 1 - b, k)
                if not last:
                    hidden(s * MT + MT, 0)
                dve.wait_ge(used, s * MT + MT)
                dve.wait_ge(stored[b], pair * 16)
                dve.tensor_copy(out[b][:, 2:TPC, :], ps_o[1][:].rearrange("p (t f) -> p t f", t=2)).then_inc(out_dve, 1)

            for k in range(KC):
                split_rows(0, 0, k)
            hidden(0, 0)
            run(dve, slot)


def combine(nc, io, keep):
    RING = 4
    with ExitStack() as ctx:
        m = Pool(nc, ctx)
        y = keep.y
        got = [[m.sb(f"cb_got{b}{r}", [P, C]) for r in range(2)] for b in range(RING)]
        row_in = [[m.sem(f"cb_row_in{b}{r}") for r in range(2)] for b in range(RING)]
        half = m.sem("cb_half")
        added = m.sem("cb_added")
        stored = m.sem("cb_stored")
        block = ctx.enter_context(nc.Block())

        @block.gpsimd
        def _(pool):
            for t in range(NT):
                if t >= RING:
                    pool.wait_ge(added, t - RING + 1)
                for r in range(2):
                    pool.indirect_dma_start(got[t % RING][r][:], None, io["expert_rows"],
                                            bass.IndirectOffsetOnAxis(keep.place[:, r, t:t + 1], 0)).then_inc(row_in[t % RING][r], 16)

        @block.vector
        def _(dve):
            for t in range(NT):
                for r, done in enumerate((half, added)):
                    dve.wait_ge(row_in[t % RING][r], 16 * (t // RING + 1))
                    if r == 1:
                        dve.wait_ge(half, t + 1)
                    dve.scalar_tensor_tensor(y[:, t, :], got[t % RING][r][:], keep.share[:, r, t:t + 1], y[:, t, :],
                                             ALU.mult, ALU.add).then_inc(done, 1)

        @block.sync
        def _(sp):
            for c in range(NC):
                sp.wait_ge(added, (c + 1) * TPC)
                to = io["out"][c * CH:(c + 1) * CH, :].rearrange("(t p) f -> p t f", p=P)
                sp.dma_start(to, y[:, c * TPC:(c + 1) * TPC, :]).then_inc(stored, 16)
            sp.wait_ge(stored, 16 * NC)


class Keep:
    pass


def scratch(nc, io):
    for name, shape in (("s1_rows", [H, N]), ("x1", [N, C]), ("q_high", [C, N]), ("q_low", [C, N]), ("k_high", [KV * D, N]),
                        ("k_low", [KV * D, N]), ("va", [KV, P, NT, VW]), ("ya", [N, C]),
                        ("sorted_rows", [SLOTS * CH, C]), ("expert_rows", [SLOTS * CH, C])):
        if name not in io:
            io[name] = nc.dram_tensor(name, shape, F32, kind="Internal").ap()


def build(nc, io):
    scratch(nc, io)
    keep = Keep()
    with ExitStack() as ctx:
        g = Pool(nc, ctx)
        keep.s1 = g.sb("s1", [P, NT, H])
        keep.s2 = g.sb("s2", [P, NT, H])
        keep.e1 = g.sb("e1", [P, NT, H])
        keep.f1 = g.sb("f1", [P, NT, H])
        keep.mean = g.sb("mean_wh", [P, C])
        keep.ge = g.sb("ge", [P, NT * H, GW], BF16)
        keep.gf = g.sb("gf", [P, NT * H, GW], BF16)
        graph_prepare(nc, io, keep)
        graph_attention(nc, io, keep)
    keep = Keep()
    with ExitStack() as ctx:
        g = Pool(nc, ctx)
        keep.y = g.sb("y", [P, NT, C])
        project_qkv(nc, io, keep)
        sequence_attention(nc, io, keep)
        keep.place = g.sb("place", [P, 2, NT], U32)
        keep.share = g.sb("share", [P, 2, NT])
        keep.owner_row = g.sb("owner_row", [P, SLOTS], U32)
        keep.raw = [g.sb(f"expert_raw{b}", [P, EW]) for b in range(2)]
        keep.wh = [g.sb("expert_high0", [P, EW], F32R)]
        keep.wl = [g.sb("expert_low0", [P, EW], F32R)]
        join_and_route(nc, io, keep)
        keep.wh.append(g.sb("expert_high1", [P, EW], F32R))
        keep.wl.append(g.sb("expert_low1", [P, EW], F32R))
        experts(nc, io, keep)
        combine(nc, io, keep)


def lay_out(inputs):
    def given(name):
        return np.asarray(inputs[name])

    def turned(w):
        return w.reshape(C, -1, 2, D // 2)[:, :, ::-1, :].reshape(C, -1)

    w, a = given("L0_gnn_W"), given("L0_gnn_a")
    wq, wk, wv = (given("L0_ffn_" + n).T for n in ("wq", "wk", "wv"))
    w1, w2, w3 = (given("L0_ffn_" + n) for n in ("w1", "w2", "w3"))
    pieces = []
    for j in range(2):
        pieces += [wq[:, j * P:(j + 1) * P], turned(wq[:, j * P:(j + 1) * P])]
    pieces += [wk, turned(wk), wv]
    up = np.zeros((E, C, UPW), w1.dtype)
    for t in range(MF):
        rows = slice(t * P, (t + 1) * P)
        up[:, :, 2 * t * P:(2 * t + 1) * P] = w1[:, rows].transpose(0, 2, 1)
        up[:, :, (2 * t + 1) * P:(2 * t + 2) * P] = w3[:, rows].transpose(0, 2, 1)
    up[:, :, 2 * MF * P:2 * MF * P + MR] = w1[:, MF * P:].transpose(0, 2, 1)
    up[:, :, 2 * MF * P + 64:] = w3[:, MF * P:].transpose(0, 2, 1)
    down = np.zeros((E, MT * P, C), w2.dtype)
    down[:, :HID] = w2.transpose(0, 2, 1)
    w_experts = np.zeros((E, P, EW), w1.dtype)
    for k in range(KC):
        w_experts[:, :, k * UPW:(k + 1) * UPW] = up[:, k * P:(k + 1) * P]
    w_experts[:, :, KC * UPW:KC * UPW + MT * C] = down.reshape(E, MT, P, C).transpose(0, 2, 1, 3).reshape(E, P, MT * C)
    inv_freq = 1.0 / 10000.0 ** (np.arange(0, D, 2, dtype=np.float32) / D)
    freqs = np.outer(np.arange(N, dtype=np.float32), inv_freq)
    emb = np.concatenate([freqs, freqs], axis=-1)
    cos, sin = np.cos(emb).T, np.sin(emb).T
    sin = np.concatenate([-sin[:D // 2], sin[D // 2:]])
    trig = np.stack([np.tile(cos, (P // D, 1)), np.tile(sin, (P // D, 1))], axis=1).astype(np.float32)
    row = np.arange(P)
    plan = np.zeros((P, PLAN_COLS), np.float32)
    plan[:, RANK] = E - np.arange(E)
    plan[:, EDGES] = CH * np.arange(NC)
    plan[:, UPTO] = np.tril(np.ones((E, E))).reshape(1, E * E)
    plan[:, SLOT] = np.arange(SLOTS)
    plan[:, ROW] = row[:, None]
    arrays = {
        "x": given("x"),
        "adj": given("adj"),
        "w_cat": w.transpose(1, 0, 2).reshape(C, C),
        "w_t": w.transpose(0, 2, 1),
        "a_t": a.reshape(H, 2, D).transpose(2, 0, 1).reshape(D, 2 * H),
        "w_qkv": np.concatenate(pieces, axis=1),
        "ln1": given("L0_ffn_ln1_w").reshape(KC, P).T,
        "ln2": given("L0_ffn_ln2_w").reshape(KC, P).T,
        "w_o": given("L0_ffn_wo").T,
        "w_r": given("L0_ffn_router_w").T,
        "w_experts": w_experts.reshape(E * P, EW),
        "ident": np.eye(P, dtype=np.float32),
        "mean_of": np.full((P, P), 1.0 / N, np.float32),
        "trig": trig,
        "late_k": np.where(row[None, :] > row[:, None], -1e30, 0.0).astype(np.float32),
        "late_q": np.where(row[None, :] < row[:, None], -1e30, 0.0).astype(np.float32),
        "plan": plan,
        "before": np.triu(np.ones((P, P), np.float32), 1),
    }
    return {name: np.ascontiguousarray(value) for name, value in arrays.items()}


def kernel(**inputs):
    import concourse.bacc as bacc
    from concourse.bass_utils import run_bass_kernel_spmd

    nc = bacc.Bacc("TRN2", target_bir_lowering=False, num_devices=1)
    arrays = lay_out(inputs)
    io = {name: nc.dram_tensor(name, a.shape, mybir.dt.from_np(a.dtype), kind="ExternalInput").ap() for name, a in arrays.items()}
    io["out"] = nc.dram_tensor("out", [N, C], F32, kind="ExternalOutput").ap()
    build(nc, io)
    return run_bass_kernel_spmd(nc, [arrays], core_ids=[0]).results[0]["out"]
```
